# Optimizing a Trainium2 kernel written in Bass

```python
import numpy as np
import jax
import jax.numpy as jnp

def _softmax(x, axis=-1):
    return jax.nn.softmax(x, axis=axis)

def _gelu(x):
    return jax.nn.gelu(x, approximate=True)

def _silu(x):
    return jax.nn.silu(x)

def _sigmoid(x):
    return jax.nn.sigmoid(x)

def _layernorm(x, axis=-1, eps=1e-05):
    m = jnp.mean(x, axis=axis, keepdims=True)
    v = jnp.var(x, axis=axis, keepdims=True)
    return (x - m) / jnp.sqrt(v + eps)

def _scatter_add(tgt, idx, src, axis=0):
    return tgt.at[idx].add(src)

def _segment_sum(src, seg, n):
    return jax.ops.segment_sum(src, seg, n)
kernel_name = 'mk_decoder_preln_d1_seqx_r8_17dff2'

def setup_inputs(seed: int=0):
    np.random.seed(seed)
    _w = jnp.asarray

    def _rec_inputs():
        import jax
        import jax.numpy as jnp
        _rk = jax.random.key(seed)
        x = -0.0003929 + 0.9999 * jax.random.normal(jax.random.fold_in(_rk, 1), (8, 128, 512), jnp.float32)
        _lenS = 128 - jax.random.randint(jax.random.fold_in(_rk, 7), (8,), 0, max(1, 128 // 4) + 1, jnp.int32)
        _lenS2 = 128 - jax.random.randint(jax.random.fold_in(_rk, 8), (8,), 0, max(1, 128 // 4) + 1, jnp.int32)
        _ctx_4096P = jax.random.normal(jax.random.fold_in(_rk, 11), (8, 16, 512), jnp.float32)
        _ctx_4096c = jax.random.dirichlet(jax.random.fold_in(_rk, 511), 0.3 * jnp.ones((16,), jnp.float32), (8, 128))
        _ctx_4096t = jnp.einsum('bsk,bkd->bsd', _ctx_4096c, _ctx_4096P)
        _ctx_4096t = _ctx_4096t * jax.lax.rsqrt(jnp.mean(jnp.square(_ctx_4096t)) + 1e-12) * 0.953939
        ctx_4096 = 2.81802e-05 + 1.00001 * (_ctx_4096t + 0.3 * jax.random.normal(jax.random.fold_in(_rk, 611), (8, 128, 512), jnp.float32))
        return (x, ctx_4096)
    x, ctx_4096 = _rec_inputs()

    def _L0_attn_setup():
        import jax, jax.numpy as jnp
        import numpy as np
        B, N, HID = (1, 256, 512)
        H, KVH, D, W = (32, 8, 128, 64)
        THETA = 10000.0
        GATE_NORM = 16.0

        def rope(x, pos):
            half = jnp.arange(D // 2, dtype=jnp.float32)
            inv = 1.0 / THETA ** (2.0 * half / D)
            fr = pos[:, None].astype(jnp.float32) * inv[None, :]
            emb = jnp.concatenate([fr, fr], axis=-1)
            cos, sin = (jnp.cos(emb)[None, None], jnp.sin(emb)[None, None])
            x1, x2 = jnp.split(x, 2, axis=-1)
            rot = jnp.concatenate([-x2, x1], axis=-1)
            return x * cos + rot * sin

        def gla_scan(q, k, v, g):
            qt, kt, vt, gt = (jnp.moveaxis(t, 2, 0) for t in (q, k, v, g))
            b, h = (q.shape[0], q.shape[1])
            S0 = jnp.zeros((b, h, D, D), jnp.float32)

            def step(S, x):
                q_t, k_t, v_t, g_t = x
                S = S * jnp.exp(g_t)[..., None] + k_t[..., None] * v_t[..., None, :]
                return (S, jnp.einsum('bhk,bhkv->bhv', q_t, S))
            _, o = jax.lax.scan(step, S0, (qt, kt, vt, gt))
            return jnp.moveaxis(o, 0, 2)

        def sliding_window_attn(q, k, v):
            b, h, n, d = q.shape
            nb = n // W
            qb = q.reshape(b, h, nb, W, d)

            def two_blocks(x):
                xb = x.reshape(b, h, nb, W, d)
                prev = jnp.concatenate([jnp.zeros_like(xb[:, :, :1]), xb[:, :, :-1]], axis=2)
                return jnp.concatenate([prev, xb], axis=3)
            kb, vb = (two_blocks(k), two_blocks(v))
            scores = jnp.einsum('bhnqd,bhnkd->bhnqk', qb, kb) / jnp.sqrt(jnp.float32(d))
            a = jnp.arange(W)[:, None]
            c = jnp.arange(2 * W)[None, :]
            rel = a + W - c
            base = (rel >= 0) & (rel <= W)
            blk = jnp.arange(nb)[:, None, None]
            keypos = (blk - 1) * W + c[None]
            mask = base[None] & (keypos >= 0)
            scores = jnp.where(mask[None, None], scores, -jnp.inf)
            p = jax.nn.softmax(scores, axis=-1)
            ob = jnp.einsum('bhnqk,bhnkd->bhnqd', p, vb)
            return ob.reshape(b, h, n, d)
        key = jax.random.key(seed)
        ks = jax.random.split(key, 5)
        s = 0.02
        return {'hidden_states': jax.random.normal(ks[0], (B, N, HID), jnp.float32), 'Wq': jax.random.normal(ks[1], (HID, H * D), jnp.float32) * s, 'Wk': jax.random.normal(ks[2], (HID, KVH * D), jnp.float32) * s, 'Wv': jax.random.normal(ks[3], (HID, KVH * D), jnp.float32) * s, 'Wo': jax.random.normal(ks[4], (H * D, HID), jnp.float32) * s}
    _L0_attn_all = _L0_attn_setup()
    _L0_attn_in = {k: v for k, v in _L0_attn_all.items() if k in ('Wq', 'Wk', 'Wv', 'Wo')}
    del _L0_attn_all

    def _L0_xattn_setup():
        import jax, jax.numpy as jnp
        import numpy as np
        B, D, N, H, K = (4, 128, 512, 16, 32)
        HD = D // H

        def _conv1x1(x, W, b):
            return jnp.einsum('od,bdn->bon', W, x) + b[None, :, None]
        key = jax.random.key(seed)
        ks = jax.random.split(key, 12)
        std_w = 1.0 / np.sqrt(D)
        std_p = 1.0 / np.sqrt(K)
        u = lambda k, shape, s: jax.random.uniform(k, shape, jnp.float32, -s, s)
        return {'query': jax.random.normal(ks[0], (B, D, N), jnp.float32), 'key': jax.random.normal(ks[1], (B, D, N), jnp.float32), 'value': jax.random.normal(ks[2], (B, D, N), jnp.float32), 'Wq': u(ks[3], (D, D), std_w), 'bq': u(ks[4], (D,), std_w), 'Wk': u(ks[5], (D, D), std_w), 'bk': u(ks[6], (D,), std_w), 'Wv': u(ks[7], (D, D), std_w), 'bv': u(ks[8], (D,), std_w), 'proj_k': u(ks[9], (N, K), std_p), 'proj_v': u(ks[10], (N, K), std_p), 'Wm': u(ks[11], (D, D), std_w), 'bm': u(jax.random.fold_in(key, 99), (D,), std_w)}
    _L0_xattn_all = _L0_xattn_setup()
    _L0_xattn_in = {k: v for k, v in _L0_xattn_all.items() if k in ('Wq', 'bq', 'Wk', 'bk', 'Wv', 'bv', 'proj_k', 'proj_v', 'Wm', 'bm')}
    del _L0_xattn_all

    def _L0_ffn_setup():
        import jax, jax.numpy as jnp
        import numpy as np
        IN_F = 512
        OUT_F = 512
        RANK = 8
        NUM_EXPERTS = 64
        TOP_K = 16
        ROUTER_DIM = 16
        ALPHA = 32
        SCALING = ALPHA / TOP_K
        BOTTLENECK = NUM_EXPERTS * RANK
        key = jax.random.key(seed)
        ks = jax.random.split(key, 5)
        x = jax.random.normal(ks[0], (4, 512, IN_F), dtype=jnp.float32)
        bound_a = float(np.sqrt(6.0 / IN_F))
        A_w = jax.random.uniform(ks[1], (BOTTLENECK, IN_F), jnp.float32, -bound_a, bound_a)
        B_w = jax.random.normal(ks[2], (OUT_F, BOTTLENECK), dtype=jnp.float32) * 0.02
        Wq_w = jax.random.normal(ks[3], (ROUTER_DIM, IN_F), dtype=jnp.float32) * 0.02
        keys = jax.random.normal(ks[4], (NUM_EXPERTS, ROUTER_DIM), dtype=jnp.float32) * 0.01
        return {'x': x, 'A_w': A_w, 'B_w': B_w, 'Wq_w': Wq_w, 'keys': keys}
    _L0_ffn_all = _L0_ffn_setup()
    _L0_ffn_in = {k: v for k, v in _L0_ffn_all.items() if k in ('A_w', 'B_w', 'Wq_w', 'keys')}
    del _L0_ffn_all
    return {'x': x, 'ctx_4096': ctx_4096, 'L0_attn_Wq': _L0_attn_in['Wq'], 'L0_attn_Wk': _L0_attn_in['Wk'], 'L0_attn_Wv': _L0_attn_in['Wv'], 'L0_attn_Wo': _L0_attn_in['Wo'], 'L0_xattn_Wq': _L0_xattn_in['Wq'], 'L0_xattn_bq': _L0_xattn_in['bq'], 'L0_xattn_Wk': _L0_xattn_in['Wk'], 'L0_xattn_bk': _L0_xattn_in['bk'], 'L0_xattn_Wv': _L0_xattn_in['Wv'], 'L0_xattn_bv': _L0_xattn_in['bv'], 'L0_xattn_proj_k': _L0_xattn_in['proj_k'], 'L0_xattn_proj_v': _L0_xattn_in['proj_v'], 'L0_xattn_Wm': _L0_xattn_in['Wm'], 'L0_xattn_bm': _L0_xattn_in['bm'], 'L0_ffn_A_w': _L0_ffn_in['A_w'], 'L0_ffn_B_w': _L0_ffn_in['B_w'], 'L0_ffn_Wq_w': _L0_ffn_in['Wq_w'], 'L0_ffn_keys': _L0_ffn_in['keys']}

def reference(x, ctx_4096, L0_attn_Wq, L0_attn_Wk, L0_attn_Wv, L0_attn_Wo, L0_xattn_Wq, L0_xattn_bq, L0_xattn_Wk, L0_xattn_bk, L0_xattn_Wv, L0_xattn_bv, L0_xattn_proj_k, L0_xattn_proj_v, L0_xattn_Wm, L0_xattn_bm, L0_ffn_A_w, L0_ffn_B_w, L0_ffn_Wq_w, L0_ffn_keys):
    import jax
    import jax.numpy as jnp

    def _L0_attn_ref(hidden_states, Wq, Wk, Wv, Wo):
        import jax, jax.numpy as jnp
        import numpy as np
        B, N, HID = (1, 256, 512)
        H, KVH, D, W = (32, 8, 128, 64)
        THETA = 10000.0
        GATE_NORM = 16.0

        def rope(x, pos):
            half = jnp.arange(D // 2, dtype=jnp.float32)
            inv = 1.0 / THETA ** (2.0 * half / D)
            fr = pos[:, None].astype(jnp.float32) * inv[None, :]
            emb = jnp.concatenate([fr, fr], axis=-1)
            cos, sin = (jnp.cos(emb)[None, None], jnp.sin(emb)[None, None])
            x1, x2 = jnp.split(x, 2, axis=-1)
            rot = jnp.concatenate([-x2, x1], axis=-1)
            return x * cos + rot * sin

        def gla_scan(q, k, v, g):
            qt, kt, vt, gt = (jnp.moveaxis(t, 2, 0) for t in (q, k, v, g))
            b, h = (q.shape[0], q.shape[1])
            S0 = jnp.zeros((b, h, D, D), jnp.float32)

            def step(S, x):
                q_t, k_t, v_t, g_t = x
                S = S * jnp.exp(g_t)[..., None] + k_t[..., None] * v_t[..., None, :]
                return (S, jnp.einsum('bhk,bhkv->bhv', q_t, S))
            _, o = jax.lax.scan(step, S0, (qt, kt, vt, gt))
            return jnp.moveaxis(o, 0, 2)

        def sliding_window_attn(q, k, v):
            b, h, n, d = q.shape
            nb = n // W
            qb = q.reshape(b, h, nb, W, d)

            def two_blocks(x):
                xb = x.reshape(b, h, nb, W, d)
                prev = jnp.concatenate([jnp.zeros_like(xb[:, :, :1]), xb[:, :, :-1]], axis=2)
                return jnp.concatenate([prev, xb], axis=3)
            kb, vb = (two_blocks(k), two_blocks(v))
            scores = jnp.einsum('bhnqd,bhnkd->bhnqk', qb, kb) / jnp.sqrt(jnp.float32(d))
            a = jnp.arange(W)[:, None]
            c = jnp.arange(2 * W)[None, :]
            rel = a + W - c
            base = (rel >= 0) & (rel <= W)
            blk = jnp.arange(nb)[:, None, None]
            keypos = (blk - 1) * W + c[None]
            mask = base[None] & (keypos >= 0)
            scores = jnp.where(mask[None, None], scores, -jnp.inf)
            p = jax.nn.softmax(scores, axis=-1)
            ob = jnp.einsum('bhnqk,bhnkd->bhnqd', p, vb)
            return ob.reshape(b, h, n, d)
        b, n, _ = hidden_states.shape
        grp = H // KVH
        q = hidden_states @ Wq
        k = hidden_states @ Wk
        v = hidden_states @ Wv
        g = k
        q = q.reshape(b, n, H, D).transpose(0, 2, 1, 3)
        k = k.reshape(b, n, KVH, D).transpose(0, 2, 1, 3)
        v = v.reshape(b, n, KVH, D).transpose(0, 2, 1, 3)
        g = g.reshape(b, n, KVH, D).transpose(0, 2, 1, 3)
        k = jnp.repeat(k, grp, axis=1)
        v = jnp.repeat(v, grp, axis=1)
        g = jnp.repeat(g, grp, axis=1)
        sq, sk, sv = (q, k, v)
        qs = jax.nn.softmax(q.astype(jnp.float32), axis=-1)
        ks_ = jax.nn.softmax(k.astype(jnp.float32), axis=-1)
        gs = jax.nn.log_sigmoid(g.astype(jnp.float32)) / GATE_NORM
        o_lin = gla_scan(qs, ks_, v.astype(jnp.float32), gs)
        pos = jnp.arange(n)
        sq = rope(sq, pos)
        sk = rope(sk, pos)
        y = sliding_window_attn(sq, sk, sv)
        o_ = 0.5 * y + 0.5 * o_lin
        o_ = o_.astype(jnp.bfloat16).astype(jnp.float32)
        o = o_.transpose(0, 2, 1, 3).reshape(b, n, H * D) @ Wo
        return o

    def _L0_xattn_ref(query, key, value, Wq, bq, Wk, bk, Wv, bv, proj_k, proj_v, Wm, bm):
        import jax, jax.numpy as jnp
        import numpy as np
        B, D, N, H, K = (4, 128, 512, 16, 32)
        HD = D // H

        def _conv1x1(x, W, b):
            return jnp.einsum('od,bdn->bon', W, x) + b[None, :, None]
        b = query.shape[0]
        q = _conv1x1(query, Wq, bq)
        k = _conv1x1(key, Wk, bk)
        v = _conv1x1(value, Wv, bv)
        k = jnp.einsum('bdn,nk->bdk', k, proj_k)
        v = jnp.einsum('bdn,nk->bdk', v, proj_v)
        q = q.reshape(b, HD, H, -1)
        k = k.reshape(b, HD, H, -1)
        v = v.reshape(b, HD, H, -1)
        scores = jnp.einsum('bdhn,bdhk->bhnk', q, k) / HD ** 0.5
        prob = jax.nn.softmax(scores, axis=-1)
        x = jnp.einsum('bhnk,bdhk->bdhn', prob, v)
        return _conv1x1(x.reshape(b, HD * H, -1), Wm, bm)

    def _L0_ffn_ref(x, A_w, B_w, Wq_w, keys):
        import jax, jax.numpy as jnp
        import numpy as np
        IN_F = 512
        OUT_F = 512
        RANK = 8
        NUM_EXPERTS = 64
        TOP_K = 16
        ROUTER_DIM = 16
        ALPHA = 32
        SCALING = ALPHA / TOP_K
        BOTTLENECK = NUM_EXPERTS * RANK
        q = jnp.einsum('bsd,rd->bsr', x, Wq_w)
        scores = jnp.einsum('bsr,er->bse', q, keys)
        top_vals, top_idx = jax.lax.top_k(scores, TOP_K)
        top_w = jax.nn.softmax(top_vals, axis=-1)
        gate = jnp.sum(jax.nn.one_hot(top_idx, NUM_EXPERTS, dtype=top_w.dtype) * top_w[..., None], axis=-2)
        z = jnp.einsum('bsd,nd->bsn', x, A_w)
        z = z.reshape(*z.shape[:-1], NUM_EXPERTS, RANK)
        z_gated = (z * gate[..., None]).reshape(*z.shape[:-2], BOTTLENECK)
        out = jnp.einsum('bsn,on->bso', z_gated, B_w) * SCALING
        return out
    x = x + _L0_attn_ref(_layernorm(x, axis=-1), L0_attn_Wq, L0_attn_Wk, L0_attn_Wv, L0_attn_Wo)
    x = x + _L0_xattn_ref(_layernorm(x, axis=-1), ctx_4096, ctx_4096, L0_xattn_Wq, L0_xattn_bq, L0_xattn_Wk, L0_xattn_bk, L0_xattn_Wv, L0_xattn_bv, L0_xattn_proj_k, L0_xattn_proj_v, L0_xattn_Wm, L0_xattn_bm)
    x = x + _L0_ffn_ref(_layernorm(x, axis=-1), L0_ffn_A_w, L0_ffn_B_w, L0_ffn_Wq_w, L0_ffn_keys)
    return x

_drawn_inputs = setup_inputs


def setup_inputs(seed=0):
    import zlib

    import numpy as np

    out = dict(_drawn_inputs(seed))
    spreads = {}
    factors = {'L0_attn_Wq': 4.764,
     'L0_attn_Wk': 4.889,
     'L0_xattn_bq': 4.941,
     'L0_xattn_bk': 4.588,
     'L0_xattn_bv': 5.349}
    for name, (base, spread) in spreads.items():
        noise = np.random.default_rng([zlib.crc32(name.encode()), seed]).standard_normal(out[name].shape)
        drawn = base * np.exp(spread * noise) if base else spread * noise
        out[name] = jnp.asarray(drawn.astype(out[name].dtype))
    for name, factor in factors.items():
        out[name] = (out[name] * factor).astype(out[name].dtype)
    return out
```

```python
import concourse.bass as bass
import numpy as np
from concourse import mybir
from contextlib import ExitStack

F32 = mybir.dt.float32
F32R = mybir.dt.float32r
BF16 = mybir.dt.bfloat16
ALU = mybir.AluOpType
ACT = mybir.ActivationFunctionType
AX = mybir.AxisListType

P = 128
B = 8
HID = 512
C = HID // P
KVH = 8
GRP = 4
H = KVH * GRP
D = 128
WIN = 64
BLK = 32
NB = P // BLK
SPAN = WIN + BLK
LW = [BLK * (i + 1) for i in range(NB)]
LO = [sum(LW[:i]) for i in range(NB)]
LT = sum(LW)
HALF = B // 2
THETA = 10000.0
GATE_NORM = 16.0
EPS = 1e-5
BIG = 1e30

K_ID, K_COS, K_SIN, K_AB, K_MS, K_ML = 0, P, 2 * P, 3 * P, 4 * P + LT, 4 * P + LT + NB * SPAN
K_ALL = K_ML + LT


def constants():
    c = np.zeros((P, K_ALL), np.float32)
    t = np.arange(P)
    c[:, K_ID:K_ID + P] = np.eye(P)
    half = np.arange(D // 2, dtype=np.float32)
    inv = (np.float32(1.0) / np.float32(THETA) ** (np.float32(2.0) * half / np.float32(D))).astype(np.float32)
    angle = t[:, None].astype(np.float32) * inv[None, :]
    cos, sin = np.cos(angle.astype(np.float64)), np.sin(angle.astype(np.float64))
    c[:, K_COS:K_COS + D] = np.concatenate([cos, cos], 1)
    c[:, K_SIN:K_SIN + D] = np.concatenate([-sin, sin], 1)
    upto = (t[:, None] <= t[None, :]).astype(np.float32)
    mid = BLK * (t // BLK) + BLK // 2 - 1
    ab = c[:, K_AB:K_AB + P + LT]
    ab[:, 0:P] = (upto - upto[:, mid]) / GATE_NORM
    for i in range(NB):
        m = BLK * i + BLK // 2 - 1
        ab[:, P + LO[i]:P + LO[i] + LW[i]] = (upto[:, m:m + 1] - upto[:, 0:LW[i]]) / GATE_NORM
    row = t % BLK
    ms = c[:, K_MS:K_MS + NB * SPAN].reshape(P, NB, SPAN)
    for i in range(NB):
        s = BLK * i - WIN + np.arange(SPAN)[None, :]
        back = BLK * i + row[:, None] - s
        ms[:, i] = np.where((s >= 0) & (back >= 0) & (back <= WIN), 0.0, -BIG)
        c[:, K_ML + LO[i]:K_ML + LO[i] + LW[i]] = 0.5 * (np.arange(LW[i])[None, :] <= BLK * i + row[:, None])
    return c


def some(count):
    return not isinstance(count, int) or count > 0


def attention(nc, x, consts, Wq, Wk, Wv, oT, xall, semctx, ctx):
    sb = lambda n, s, d=F32: ctx.enter_context(nc.sbuf_tensor(n, s, d))
    ps = lambda n, s, d=F32: ctx.enter_context(nc.psum_tensor(n, s, d))
    sem = lambda n: semctx.enter_context(nc.semaphore(n))

    cst = sb("cst", [P, K_ALL])
    ident = cst[:, K_ID:K_ID + P]
    mask_w = cst[:, K_MS:K_MS + NB * SPAN].rearrange("p (i s) -> p i s", i=NB)
    mask_l = cst[:, K_ML:K_ML + LT]
    ab = sb("ab", [P, P + LT], F32R)
    stats = sb("stats", [P, B, 6])
    veps = sb("veps", [P, B])
    mv = sb("mv", [P, B, 2])
    std = sb("std", [P, B])
    rstd = sb("rstd", [P, B])
    newt = sb("newt", [P, B])
    hT_hi = sb("hT_hi", [P, C, B * P], F32R)
    hT_lo = sb("hT_lo", [P, C, B * P], F32R)
    wq_raw = sb("wq_raw", [P, C, GRP * D])
    wq_hi = sb("wq_hi", [P, C, GRP * D], F32R)
    wq_lo = sb("wq_lo", [P, C, GRP * D], F32R)
    wkv_raw = sb("wkv_raw", [P, C, 2 * D])
    wkv_hi = sb("wkv_hi", [P, C, 2 * D], F32R)
    wkv_lo = sb("wkv_lo", [P, C, 2 * D], F32R)
    kall = sb("kall", [P, HALF, D])
    ek = sb("ek", [P, HALF, D])
    gate = sb("gate", [P, HALF, D])
    g_hi = sb("g_hi", [P, HALF, D], F32R)
    g_lo = sb("g_lo", [P, HALF, D], F32R)
    kr = sb("kr", [P, HALF, D])
    kr2 = sb("kr2", [P, HALF, D])
    kmx = sb("kmx", [P, HALF])
    ksm = sb("ksm", [P, HALF])
    krz = sb("krz", [P, HALF])
    ksT = sb("ksT", [P, HALF, P])
    krT = sb("krT", [P, B, WIN + P])
    dec = sb("dec", [P, B, P + LT])
    vS = sb("vS", [P, B, D])
    qs = sb("qs", [P, 2, GRP, D])
    eq = sb("eq", [P, 2, GRP, D])
    qr = sb("qr", [P, 2, GRP, D])
    qr2 = sb("qr2", [P, GRP, D])
    qmx = sb("qmx", [P, 2, GRP])
    qsm = sb("qsm", [P, 2, GRP])
    qrz = sb("qrz", [P, 2, GRP])
    qrT = sb("qrT", [P, NB, GRP, BLK])
    qdT = sb("qdT", [P, NB, GRP, BLK])
    ss = sb("ss", [P, NB, SPAN])
    smx = sb("smx", [P, NB])
    ssm = sb("ssm", [P, NB])
    srz = sb("srz", [P, NB])
    srh = sb("srh", [P, NB])
    pm = sb("pm", [P, 2, LT])
    pT = sb("pT", [P, NB * P])

    Qp = ps("Qp", [P, GRP, D])
    TQ = ps("TQ", [P, GRP, NB, BLK])
    TE = ps("TE", [P, GRP, NB, BLK])
    Sp = ps("Sp", [P, 512])
    Lp = ps("Lp", [P, 512])
    PTp = ps("PTp", [P, NB * P])
    OTp = ps("OTp", [P, NB, GRP, BLK])
    Kp = ps("Kp", [P, 512])

    x_in = [sem(f"x_in{b}") for b in range(B)]
    consts_in = sem("consts_in")
    var_ok = sem("var_ok")
    kall_ok = sem("kall_ok")
    wq_in = sem("wq_in")
    wkv_in = sem("wkv_in")
    stats_ok = sem("stats_ok")
    mv_ok = sem("mv_ok")
    std_ok = sem("std_ok")
    rstd_ok = sem("rstd_ok")
    newton_ok = sem("newton_ok")
    h_ok = sem("h_ok")
    hT_ps = sem("hT_ps")
    hT_ok = sem("hT_ok")
    hT_lo_ok = sem("hT_lo_ok")
    ab_ok = sem("ab_ok")
    pads_ok = sem("pads_ok")
    wq_hi_ok = sem("wq_hi_ok")
    wq_ok = sem("wq_ok")
    wkv_hi_ok = sem("wkv_hi_ok")
    wkv_ok = sem("wkv_ok")
    kv_ps = sem("kv_ps")
    kv_ok = sem("kv_ok")
    kmax_ok = sem("kmax_ok")
    ksub_ok = sem("ksub_ok")
    kexp_ok = sem("kexp_ok")
    ksum_ok = sem("ksum_ok")
    krz_ok = sem("krz_ok")
    knorm_ok = sem("knorm_ok")
    gabs_ok = sem("gabs_ok")
    gexp_ok = sem("gexp_ok")
    gln_ok = sem("gln_ok")
    gate_ok = sem("gate_ok")
    ghi_ok = sem("ghi_ok")
    glo_ok = sem("glo_ok")
    krope_a = sem("krope_a")
    krope_b = sem("krope_b")
    krope_ok = sem("krope_ok")
    krT_ps = sem("krT_ps")
    krT_ok = sem("krT_ok")
    ksT_ps = sem("ksT_ps")
    ksT_ok = sem("ksT_ok")
    dec_ps = sem("dec_ps")
    dec_ok = sem("dec_ok")
    kd_ok = sem("kd_ok")
    q_ps = sem("q_ps")
    q_ok = sem("q_ok")
    qmax_ok = sem("qmax_ok")
    qsub_ok = sem("qsub_ok")
    qexp_ok = sem("qexp_ok")
    qsum_ok = sem("qsum_ok")
    qrz_ok = sem("qrz_ok")
    qnorm_ok = sem("qnorm_ok")
    qrope_a = sem("qrope_a")
    qrope_b = sem("qrope_b")
    qrope_ok = sem("qrope_ok")
    qrT_ps = sem("qrT_ps")
    qrT_ok = sem("qrT_ok")
    qeT_ps = sem("qeT_ps")
    qdT_ok = sem("qdT_ok")
    s_ps = sem("s_ps")
    l_ps = sem("l_ps")
    smask_ok = sem("smask_ok")
    smax_ok = sem("smax_ok")
    ssub_ok = sem("ssub_ok")
    sexp_ok = sem("sexp_ok")
    ssum_ok = sem("ssum_ok")
    srz_ok = sem("srz_ok")
    srh_ok = sem("srh_ok")
    lin_ok = sem("lin_ok")
    p_ok = sem("p_ok")
    pT_ps = sem("pT_ps")
    pT_ok = sem("pT_ok")
    o_ps = sem("o_ps")
    o_ok = sem("o_ok")

    def spread(ap, n):
        return ap.unsqueeze(2).broadcast_to([ap.shape[0], ap.shape[1], n])

    def table(lo, n):
        return cst[:, lo:lo + D].unsqueeze(1).broadcast_to([P, n, D])

    wq_v = Wq.rearrange("(c p) (k n) -> k p c n", p=P, k=KVH)
    wk_v = Wk.rearrange("(c p) (k n) -> k p c n", p=P, k=KVH)
    wv_v = Wv.rearrange("(c p) (k n) -> k p c n", p=P, k=KVH)
    x_v = x.rearrange("b t d -> t b d")
    x8 = xall

    block = ctx.enter_context(nc.Block())

    @block.sync
    def _(sp):
        sp.dma_start(cst[:, :], consts).then_inc(consts_in, 16)
        for b in range(B):
            sp.dma_start(x8[:, b, :], x_v[:, b, :]).then_inc(x_in[b], 16)
            if b == 1:
                sp.dma_start(wkv_raw[:, :, 0:D], wk_v[0]).then_inc(wkv_in, 16)
                sp.dma_start(wkv_raw[:, :, D:2 * D], wv_v[0]).then_inc(wkv_in, 16)
            if b == 3:
                sp.dma_start(wq_raw[:, :, :], wq_v[0]).then_inc(wq_in, 16)

        def weights(k):
            sp.wait_ge(wkv_ok, k)
            sp.dma_start(wkv_raw[:, :, 0:D], wk_v[k]).then_inc(wkv_in, 16)
            sp.dma_start(wkv_raw[:, :, D:2 * D], wv_v[k]).then_inc(wkv_in, 16)
            sp.wait_ge(wq_ok, k)
            sp.dma_start(wq_raw[:, :, :], wq_v[k]).then_inc(wq_in, 16)

        for k in range(1, KVH):
            weights(k)

    @block.tensor
    def _(pe):
        def product(out, hi, lo, whi, wlo):
            for c in range(C):
                pe.matmul(out, hi[c], whi[c], start=(c == 0), stop=False)
                pe.matmul(out, hi[c], wlo[c], start=False, stop=False)
                mm = pe.matmul(out, lo[c], whi[c], start=False, stop=(c == C - 1))
            return mm

        def h_of(b):
            return [[t[:, c, b * P:(b + 1) * P] for c in range(C)] for t in (hT_hi, hT_lo)]

        def project_q(k, b):
            if b == 0:
                pe.wait_ge(wq_ok, k + 1)
            if some(8 * k + b):
                pe.wait_ge(q_ok, 8 * k + b)
            product(Qp[:, :, :].rearrange("p h d -> p (h d)"), *h_of(b), [wq_hi[:, c, :] for c in range(C)],
                    [wq_lo[:, c, :] for c in range(C)]).then_inc(q_ps, 1)

        def transpose_q(k, b):
            n = 8 * k + b
            pe.wait_ge(qrope_ok, n + 1)
            if some(n):
                pe.wait_ge(qrT_ok, n)
            for h in range(GRP):
                mm = pe.transpose(TQ[:, h, :, :].rearrange("p i t -> p (i t)"), qr[:, b % 2, h, :], ident)
            mm.then_inc(qrT_ps, 1)
            pe.wait_ge(qnorm_ok, n + 1)
            if some(n):
                pe.wait_ge(qdT_ok, n)
            for h in range(GRP):
                mm = pe.transpose(TE[:, h, :, :].rearrange("p i t -> p (i t)"), eq[:, b % 2, h, :], ident)
            mm.then_inc(qeT_ps, 1)

        def scores(k, b):
            n = 8 * k + b
            m = 2 * k + b // HALF
            if b % HALF == 0:
                pe.wait_ge(krT_ok, m + 1)
                pe.wait_ge(kd_ok, m + 1)
            pe.wait_ge(qrT_ok, n + 1)
            if some(n):
                pe.wait_ge(smask_ok, n)
            for i in range(NB):
                mm = pe.matmul(Sp[:, i * SPAN:(i + 1) * SPAN], qrT[:, i, :, :].rearrange("p h t -> p (h t)"),
                               krT[:, b, BLK * i:BLK * i + SPAN], start=True, stop=True)
            mm.then_inc(s_ps, 1)
            pe.wait_ge(qdT_ok, n + 1)
            if some(n):
                pe.wait_ge(lin_ok, n)
            for i in range(NB):
                mm = pe.matmul(Lp[:, LO[i]:LO[i] + LW[i]], qdT[:, i, :, :].rearrange("p h t -> p (h t)"),
                               dec[:, b, P + LO[i]:P + LO[i] + LW[i]], start=True, stop=True)
            mm.then_inc(l_ps, 1)

        def transpose_p(k, b):
            n = 8 * k + b
            pe.wait_ge(p_ok, n + 1)
            if some(n):
                pe.wait_ge(pT_ok, n)
            if isinstance(n, int) and n == 0:
                pe.wait_ge(pads_ok, 2)
            for i in range(NB):
                mm = pe.transpose(PTp[0:LW[i], i * P:(i + 1) * P], pm[:, b % 2, LO[i]:LO[i] + LW[i]], ident)
            mm.then_inc(pT_ps, 1)

        def mix(k, b):
            n = 8 * k + b
            pe.wait_ge(pT_ok, n + 1)
            if some(n):
                pe.wait_ge(o_ok, n)
            pe.matmul(OTp[:, :, :, :].rearrange("p i h t -> p (i h t)"), vS[:, b, :], pT[:, :],
                      start=True, stop=True).then_inc(o_ps, 1)

        def project_kv(k, hf, pair):
            m = 2 * k + hf
            if pair == 0:
                pe.wait_ge(wkv_ok, k + 1)
                if some(4 * m):
                    pe.wait_ge(dec_ok, 4 * m)
            else:
                pe.wait_ge(kv_ok, 2 * m + 1)
            for y in range(2):
                b = HALF * hf + 2 * pair + y
                mm = product(Kp[:, y * 2 * D:(y + 1) * 2 * D], *h_of(b), [wkv_hi[:, c, :] for c in range(C)],
                             [wkv_lo[:, c, :] for c in range(C)])
            mm.then_inc(kv_ps, 1)

        def transpose_kr(m):
            pe.wait_ge(krope_ok, m + 1)
            pe.wait_ge(kv_ok, 2 * m + 2)
            for y in range(HALF):
                mm = pe.transpose(Kp[:, y * P:(y + 1) * P], kr[:, y, :], ident)
            mm.then_inc(krT_ps, 1)

        def transpose_ks(m):
            pe.wait_ge(knorm_ok, m + 1)
            pe.wait_ge(krT_ok, m + 1)
            for y in range(HALF):
                mm = pe.transpose(Kp[:, y * P:(y + 1) * P], ek[:, y, :], ident)
            mm.then_inc(ksT_ps, 1)

        def decays(m, y):
            if y == 0:
                pe.wait_ge(glo_ok, m + 1)
                pe.wait_ge(ksT_ok, m + 1)
            else:
                if some(4 * m + y):
                    pe.wait_ge(dec_ok, 4 * m + y)
            pe.matmul(Kp[:, 0:P + LT], g_hi[:, y, :], ab[:, :], start=True, stop=False)
            pe.matmul(Kp[:, 0:P + LT], g_lo[:, y, :], ab[:, :], start=False, stop=True).then_inc(dec_ps, 1)

        pe.wait_ge(consts_in, 16)
        for b in range(B):
            bank = (Kp, Sp)[b % 2]
            pe.wait_ge(h_ok, b + 1)
            if some(b - 1):
                pe.wait_ge(hT_lo_ok, b - 1)
            for c in range(C):
                mm = pe.transpose(bank[:, c * P:(c + 1) * P], x8[:, b, c * P:(c + 1) * P], ident)
            mm.then_inc(hT_ps, 1)
        pe.wait_ge(ab_ok, 1)
        pe.wait_ge(hT_lo_ok, B)
        project_kv(0, 0, 0)
        project_kv(0, 0, 1)
        transpose_kr(0)
        transpose_ks(0)
        decays(0, 0)

        def head(k, first=False, last=False):
            for j in range(B):
                w = j % HALF
                kk, hf = (k, 1) if j < HALF else (k + 1, 0)
                m = 2 * kk + hf
                work = not (last and j >= HALF)
                k1, b1 = (k, j - 1) if j >= 1 else (k - 1, B - 1)
                k2, b2 = (k, j - 2) if j >= 2 else (k - 1, B + j - 2)
                live1, live2 = not (first and j < 1), not (first and j < 2)
                project_q(k, j)
                if w == 0:
                    decays(m - 1, 1)
                if w == 2 and work:
                    project_kv(kk, hf, 1)
                if w == 3 and work:
                    transpose_kr(m)
                if live1:
                    transpose_q(k1, b1)
                if live2:
                    transpose_p(k2, b2)
                if w == 0:
                    decays(m - 1, 2)
                if w == 3 and work:
                    transpose_ks(m)
                if live1:
                    scores(k1, b1)
                if live2:
                    mix(k2, b2)
                if w == 0:
                    decays(m - 1, 3)
                if w == 1 and work:
                    project_kv(kk, hf, 0)
                if w == 3 and work:
                    decays(m, 0)

        head(0, first=True)
        with pe.Fori(1, KVH - 1) as k:
            head(k)
        head(KVH - 1, last=True)
        transpose_q(KVH - 1, B - 1)
        transpose_p(KVH - 1, B - 2)
        scores(KVH - 1, B - 1)
        mix(KVH - 1, B - 2)
        transpose_p(KVH - 1, B - 1)
        mix(KVH - 1, B - 1)

    @block.scalar
    def _(act):
        def split_wkv(k):
            act.wait_ge(wkv_in, 32 * k + 32)
            if some(4 * k):
                act.wait_ge(kv_ps, 4 * k)
            act.activation(wkv_hi[:, :, :], wkv_raw[:, :, :], ACT.Copy).then_inc(wkv_hi_ok, 1)

        def split_wq(k):
            act.wait_ge(wq_in, 16 * k + 16)
            if some(8 * k):
                act.wait_ge(q_ps, 8 * k)
            act.activation(wq_hi[:, :, :], wq_raw[:, :, :], ACT.Copy).then_inc(wq_hi_ok, 1)

        def copy_q(k, b):
            n = 8 * k + b
            act.wait_ge(q_ps, n + 1)
            if some(n - 1):
                act.wait_ge(qsub_ok, n - 1)
            if some(n - 1):
                act.wait_ge(qrope_b, n - 1)
            act.activation(qs[:, b % 2, :, :], Qp[:, :, :], ACT.Copy).then_inc(q_ok, 1)

        def exp_q(k, b):
            act.wait_ge(qsub_ok, 8 * k + b + 1)
            act.activation(eq[:, b % 2, :, :], eq[:, b % 2, :, :], ACT.Exp).then_inc(qexp_ok, 1)

        def copy_qrT(k, b):
            n = 8 * k + b
            act.wait_ge(qrT_ps, n + 1)
            if some(n):
                act.wait_ge(s_ps, n)
            act.activation(qrT[:, :, :, :], TQ[:, :, :, :].rearrange("p h i t -> p i h t"),
                           ACT.Copy).then_inc(qrT_ok, 1)

        def exp_s(k, b):
            act.wait_ge(ssub_ok, 8 * k + b + 1)
            act.activation(ss[:, :, :], ss[:, :, :], ACT.Exp).then_inc(sexp_ok, 1)

        def copy_pT(k, b):
            n = 8 * k + b
            act.wait_ge(pT_ps, n + 1)
            if some(n):
                act.wait_ge(o_ps, n)
            act.activation(pT[:, :], PTp[:, :], ACT.Copy).then_inc(pT_ok, 1)

        def copy_o(k, b):
            act.wait_ge(o_ps, 8 * k + b + 1)
            act.wait_ge(ab_ok, 1)
            act.activation(oT[:, bass.ds(GRP * k, GRP), b * P:(b + 1) * P].rearrange("p h (i t) -> p i h t", i=NB),
                           OTp[:, :, :, :], ACT.Copy).then_inc(o_ok, 1)

        def copy_kv(k, hf, pair):
            m = 2 * k + hf
            kv = Kp[:, :].rearrange("p (y a d) -> p y a d", y=2, a=2)
            act.wait_ge(kv_ps, 2 * m + pair + 1)
            if pair == 0:
                if some(m):
                    act.wait_ge(ksub_ok, m)
                if some(m):
                    act.wait_ge(gate_ok, m)
                if some(m):
                    act.wait_ge(gabs_ok, m)
                if some(m):
                    act.wait_ge(krope_b, m)
            act.activation(kall[:, 2 * pair:2 * pair + 2, :], kv[:, :, 0, :], ACT.Copy).then_inc(kall_ok, 1)
            if some(8 * k + HALF * hf - HALF):
                act.wait_ge(o_ps, 8 * k + HALF * hf - HALF)
            b = HALF * hf + 2 * pair
            act.activation(vS[:, b:b + 2, :], kv[:, :, 1, :], ACT.Copy).then_inc(kv_ok, 1)

        def gates(m):
            act.wait_ge(kall_ok, 2 * m + 2)
            if some(m):
                act.wait_ge(glo_ok, m)
            act.activation(gate[:, :, :], kall[:, :, :], ACT.Abs).then_inc(gabs_ok, 1)
            act.wait_ge(gabs_ok, m + 1)
            act.activation(gate[:, :, :], gate[:, :, :], ACT.Exp, scale=-1.0).then_inc(gexp_ok, 1)
            act.wait_ge(gexp_ok, m + 1)
            act.activation(gate[:, :, :], gate[:, :, :], ACT.Ln, bias=1.0).then_inc(gln_ok, 1)

        def exp_k(m):
            act.wait_ge(ksub_ok, m + 1)
            act.activation(ek[:, :, :], ek[:, :, :], ACT.Exp).then_inc(kexp_ok, 1)

        def gate_hi(m):
            act.wait_ge(gate_ok, m + 1)
            if some(4 * m):
                act.wait_ge(dec_ps, 4 * m)
            act.activation(g_hi[:, :, :], gate[:, :, :], ACT.Copy).then_inc(ghi_ok, 1)

        def copy_krT(k, hf):
            m = 2 * k + hf
            act.wait_ge(krT_ps, m + 1)
            if some(8 * k + HALF * hf - HALF):
                act.wait_ge(s_ps, 8 * k + HALF * hf - HALF)
            act.activation(krT[:, HALF * hf:HALF * hf + HALF, WIN:WIN + P],
                           Kp[:, :].rearrange("p (y s) -> p y s", y=HALF), ACT.Copy).then_inc(krT_ok, 1)

        def copy_ksT(m):
            act.wait_ge(ksT_ps, m + 1)
            if some(m):
                act.wait_ge(kd_ok, m)
            act.activation(ksT[:, :, :], Kp[:, :].rearrange("p (y s) -> p y s", y=HALF), ACT.Copy).then_inc(ksT_ok, 1)

        def exp_dec(k, hf, y):
            m = 2 * k + hf
            act.wait_ge(dec_ps, 4 * m + y + 1)
            if some(8 * k + HALF * hf - HALF):
                act.wait_ge(l_ps, 8 * k + HALF * hf - HALF)
            act.activation(dec[:, HALF * hf + y, :], Kp[:, 0:P + LT], ACT.Exp).then_inc(dec_ok, 1)

        act.wait_ge(consts_in, 16)
        act.activation(ab[:, :], cst[:, K_AB:K_AB + P + LT], ACT.Copy).then_inc(ab_ok, 1)
        act.wait_ge(var_ok, 1)
        act.activation(std[:, :], veps[:, :], ACT.Sqrt).then_inc(std_ok, 1)
        split_wkv(0)
        split_wq(0)
        for b in range(B):
            bank = (Kp, Sp)[b % 2]
            act.wait_ge(hT_ps, b + 1)
            act.activation(hT_hi[:, :, b * P:(b + 1) * P], bank[:, :].rearrange("p (c t) -> p c t", c=C),
                           ACT.Copy).then_inc(hT_ok, 1)
        copy_kv(0, 0, 0)
        copy_kv(0, 0, 1)
        gates(0)
        exp_k(0)
        gate_hi(0)
        copy_krT(0, 0)
        copy_ksT(0)
        exp_dec(0, 0, 0)

        def head(k, first=False, last=False):
            for j in range(B):
                w = j % HALF
                kk, hf = (k, 1) if j < HALF else (k + 1, 0)
                kp, hp = (k, 0) if j < HALF else (k, 1)
                m = 2 * kk + hf
                work = not (last and j >= HALF)
                k1, b1 = (k, j - 1) if j >= 1 else (k - 1, B - 1)
                k2, b2 = (k, j - 2) if j >= 2 else (k - 1, B + j - 2)
                live1, live2 = not (first and j < 1), not (first and j < 2)
                copy_q(k, j)
                if w == 0:
                    exp_dec(kp, hp, 1)
                if w == 2 and work:
                    copy_kv(kk, hf, 1)
                if w == 3 and work:
                    copy_krT(kk, hf)
                if live1:
                    copy_qrT(k1, b1)
                if live2:
                    copy_pT(k2, b2)
                if w == 0:
                    exp_dec(kp, hp, 2)
                if w == 3 and work:
                    copy_ksT(m)
                exp_q(k, j)
                if w == 2 and work:
                    gates(m)
                if live1:
                    exp_s(k1, b1)
                if live2:
                    copy_o(k2, b2)
                if w == 0:
                    exp_dec(kp, hp, 3)
                if w == 1 and work:
                    copy_kv(kk, hf, 0)
                if w == 2 and work:
                    exp_k(m)
                    gate_hi(m)
                if w == 3 and work:
                    exp_dec(kk, hf, 0)
                if j == 3 and not last:
                    split_wkv(k + 1)
                if j == B - 1 and not last:
                    split_wq(k + 1)

        head(0, first=True)
        with act.Fori(1, KVH - 1) as k:
            head(k)
        head(KVH - 1, last=True)
        copy_qrT(KVH - 1, B - 1)
        copy_pT(KVH - 1, B - 2)
        exp_s(KVH - 1, B - 1)
        copy_o(KVH - 1, B - 2)
        copy_pT(KVH - 1, B - 1)
        copy_o(KVH - 1, B - 1)

    @block.vector
    def _(dve):
        def split_wkv(k):
            dve.wait_ge(wkv_hi_ok, k + 1)
            dve.tensor_tensor(wkv_lo[:, :, :], wkv_raw[:, :, :], wkv_hi[:, :, :].bitcast(F32),
                              ALU.subtract).then_inc(wkv_ok, 1)

        def split_wq(k):
            dve.wait_ge(wq_hi_ok, k + 1)
            dve.tensor_tensor(wq_lo[:, :, :], wq_raw[:, :, :], wq_hi[:, :, :].bitcast(F32),
                              ALU.subtract).then_inc(wq_ok, 1)

        def max_q(k, b):
            n = 8 * k + b
            dve.wait_ge(q_ok, n + 1)
            dve.tensor_reduce(qmx[:, b % 2, :], qs[:, b % 2, :, :], AX.X, ALU.max).then_inc(qmax_ok, 1)
            dve.wait_ge(qmax_ok, n + 1)
            if some(n - 1):
                dve.wait_ge(qeT_ps, n - 1)
            dve.tensor_tensor(eq[:, b % 2, :, :], qs[:, b % 2, :, :], spread(qmx[:, b % 2, :], D),
                              ALU.subtract).then_inc(qsub_ok, 1)

        def sum_q(k, b):
            n = 8 * k + b
            dve.wait_ge(qexp_ok, n + 1)
            dve.tensor_reduce(qsm[:, b % 2, :], eq[:, b % 2, :, :], AX.X, ALU.add).then_inc(qsum_ok, 1)
            dve.wait_ge(qsum_ok, n + 1)
            if some(n - 1):
                dve.wait_ge(qnorm_ok, n - 1)
            dve.reciprocal(qrz[:, b % 2, :], qsm[:, b % 2, :]).then_inc(qrz_ok, 1)

        def decay_q(k, b):
            n = 8 * k + b
            dve.wait_ge(qeT_ps, n + 1)
            if some(n):
                dve.wait_ge(l_ps, n)
            if isinstance(n, int) and n == 0:
                dve.wait_ge(dec_ok, HALF)
            dve.tensor_tensor(qdT[:, :, :, :], TE[:, :, :, :].rearrange("p h i t -> p i h t"),
                              dec[:, b, 0:P].rearrange("p (i t) -> p i t", i=NB).unsqueeze(2)
                              .broadcast_to([P, NB, GRP, BLK]), ALU.mult).then_inc(qdT_ok, 1)

        def mask_s(k, b):
            n = 8 * k + b
            dve.wait_ge(s_ps, n + 1)
            dve.scalar_tensor_tensor(out=ss[:, :, :], in0=Sp[:, 0:NB * SPAN].rearrange("p (i s) -> p i s", i=NB),
                                     scalar=float(D) ** -0.5, in1=mask_w, op0=ALU.mult,
                                     op1=ALU.add).then_inc(smask_ok, 1)
            dve.wait_ge(smask_ok, n + 1)
            dve.tensor_reduce(smx[:, :], ss[:, :, :], AX.X, ALU.max).then_inc(smax_ok, 1)
            dve.wait_ge(smax_ok, n + 1)
            dve.tensor_tensor(ss[:, :, :], ss[:, :, :], spread(smx[:, :], SPAN), ALU.subtract).then_inc(ssub_ok, 1)

        def linear(k, b):
            n = 8 * k + b
            dve.wait_ge(l_ps, n + 1)
            if some(n - 1):
                dve.wait_ge(pT_ps, n - 1)
            dve.scalar_tensor_tensor(out=pm[:, b % 2, :], in0=Lp[:, 0:LT], scalar=BIG, in1=mask_l, op0=ALU.min,
                                     op1=ALU.mult).then_inc(lin_ok, 1)

        def combine(k, b):
            n = 8 * k + b
            dve.wait_ge(sexp_ok, n + 1)
            dve.tensor_reduce(ssm[:, :], ss[:, :, :], AX.X, ALU.add).then_inc(ssum_ok, 1)
            dve.wait_ge(ssum_ok, n + 1)
            dve.reciprocal(srz[:, :], ssm[:, :]).then_inc(srz_ok, 1)
            dve.wait_ge(srz_ok, n + 1)
            dve.tensor_scalar(srh[:, :], srz[:, :], 0.5, None, ALU.mult).then_inc(srh_ok, 1)
            dve.wait_ge(srh_ok, n + 1)
            dve.wait_ge(lin_ok, n + 1)
            for i in range(NB):
                w = min(LW[i], SPAN)
                seen = pm[:, b % 2, LO[i] + LW[i] - w:LO[i] + LW[i]]
                op = dve.scalar_tensor_tensor(out=seen, in0=ss[:, i, SPAN - w:SPAN], scalar=srh[:, i:i + 1], in1=seen,
                                              op0=ALU.mult, op1=ALU.add)
            op.then_inc(p_ok, 1)

        def softmax_k(m):
            dve.wait_ge(kv_ok, 2 * m + 2)
            dve.tensor_reduce(kmx[:, :], kall[:, :, :], AX.X, ALU.max).then_inc(kmax_ok, 1)
            dve.wait_ge(kmax_ok, m + 1)
            if some(m):
                dve.wait_ge(ksT_ps, m)
            dve.tensor_tensor(ek[:, :, :], kall[:, :, :], spread(kmx[:, :], D), ALU.subtract).then_inc(ksub_ok, 1)

        def sum_k(m):
            dve.wait_ge(gln_ok, m + 1)
            dve.scalar_tensor_tensor(out=gate[:, :, :], in0=kall[:, :, :], scalar=0.0, in1=gate[:, :, :], op0=ALU.min,
                                     op1=ALU.subtract).then_inc(gate_ok, 1)
            dve.wait_ge(kexp_ok, m + 1)
            dve.tensor_reduce(ksm[:, :], ek[:, :, :], AX.X, ALU.add).then_inc(ksum_ok, 1)
            dve.wait_ge(ksum_ok, m + 1)
            if some(m):
                dve.wait_ge(knorm_ok, m)
            dve.reciprocal(krz[:, :], ksm[:, :]).then_inc(krz_ok, 1)
            dve.wait_ge(ghi_ok, m + 1)
            if some(4 * m):
                dve.wait_ge(dec_ps, 4 * m)
            dve.tensor_tensor(g_lo[:, :, :], gate[:, :, :], g_hi[:, :, :].bitcast(F32), ALU.subtract).then_inc(glo_ok, 1)

        def decay_k(m, hf):
            dve.wait_ge(dec_ok, 4 * m + HALF)
            dve.wait_ge(ksT_ok, m + 1)
            for i in range(NB):
                to = dec[:, HALF * hf:HALF * hf + HALF, P + LO[i]:P + LO[i] + LW[i]]
                op = dve.tensor_tensor(to, ksT[:, :, 0:LW[i]], to, ALU.mult)
            op.then_inc(kd_ok, 1)

        dve.memset(krT[:, :, 0:WIN], 0.0).then_inc(pads_ok, 1)
        dve.memset(PTp[:, :], 0.0).then_inc(pads_ok, 1)

        for b in range(B):
            dve.wait_ge(x_in[b], 16)
            dve.bn_stats(stats[:, b, :], x8[:, b, :]).then_inc(stats_ok, 1)
            dve.wait_ge(stats_ok, b + 1)
            dve.bn_aggr(mv[:, b, :], stats[:, b, :]).then_inc(mv_ok, 1)
        dve.wait_ge(mv_ok, B)
        dve.tensor_scalar(veps[:, :], mv[:, :, 1], EPS, None, ALU.add).then_inc(var_ok, 1)
        dve.wait_ge(std_ok, 1)
        dve.reciprocal(rstd[:, :], std[:, :]).then_inc(rstd_ok, 1)
        dve.wait_ge(rstd_ok, 1)
        dve.tensor_tensor(newt[:, :], rstd[:, :], rstd[:, :], ALU.mult).then_inc(newton_ok, 1)
        dve.wait_ge(newton_ok, 1)
        dve.tensor_tensor(newt[:, :], newt[:, :], veps[:, :], ALU.mult).then_inc(newton_ok, 1)
        dve.wait_ge(newton_ok, 2)
        dve.tensor_scalar(newt[:, :], newt[:, :], -0.5, 1.5, ALU.mult, ALU.add).then_inc(newton_ok, 1)
        dve.wait_ge(newton_ok, 3)
        dve.tensor_tensor(rstd[:, :], rstd[:, :], newt[:, :], ALU.mult).then_inc(newton_ok, 1)
        dve.wait_ge(newton_ok, 4)
        for b in range(B):
            dve.tensor_scalar(x8[:, b, :], x8[:, b, :], mv[:, b, 0:1], rstd[:, b:b + 1], ALU.subtract,
                              ALU.mult).then_inc(h_ok, 1)
        split_wkv(0)
        split_wq(0)
        for b in range(B):
            bank = (Kp, Sp)[b % 2]
            cols = slice(b * P, (b + 1) * P)
            dve.wait_ge(hT_ok, b + 1)
            dve.tensor_tensor(hT_lo[:, :, cols], bank[:, :].rearrange("p (c t) -> p c t", c=C),
                              hT_hi[:, :, cols].bitcast(F32), ALU.subtract).then_inc(hT_lo_ok, 1)
        softmax_k(0)
        sum_k(0)

        def head(k, first=False, last=False):
            for j in range(B):
                w = j % HALF
                kk, hf = (k, 1) if j < HALF else (k + 1, 0)
                m = 2 * kk + hf
                work = not (last and j >= HALF)
                k1, b1 = (k, j - 1) if j >= 1 else (k - 1, B - 1)
                live1 = not (first and j < 1)
                if live1:
                    decay_q(k1, b1)
                max_q(k, j)
                if live1:
                    mask_s(k1, b1)
                if w == 2 and work:
                    softmax_k(m)
                sum_q(k, j)
                if live1:
                    linear(k1, b1)
                    combine(k1, b1)
                if w == 2 and work:
                    sum_k(m)
                if w == 0:
                    decay_k(m - 1, 1 - hf)
                if j == 3 and not last:
                    split_wkv(k + 1)
                if j == B - 1 and not last:
                    split_wq(k + 1)

        head(0, first=True)
        with dve.Fori(1, KVH - 1) as k:
            head(k)
        head(KVH - 1, last=True)
        decay_q(KVH - 1, B - 1)
        mask_s(KVH - 1, B - 1)
        linear(KVH - 1, B - 1)
        combine(KVH - 1, B - 1)

    @block.gpsimd
    def _(pool):
        def swapped_sin(src, to, n):
            for a in range(2):
                half, other = slice(a * (D // 2), (a + 1) * (D // 2)), slice((1 - a) * (D // 2), (2 - a) * (D // 2))
                sin = cst[:, K_SIN + a * (D // 2):K_SIN + (a + 1) * (D // 2)].unsqueeze(1).broadcast_to([P, n, D // 2])
                op = pool.tensor_tensor(to[:, :, half], src[:, :, other], sin, ALU.mult)
            return op

        def rotate_q(k, b):
            n = 8 * k + b
            pool.wait_ge(q_ok, n + 1)
            if some(n - 1):
                pool.wait_ge(qrT_ps, n - 1)
            pool.tensor_tensor(qr[:, b % 2, :, :], qs[:, b % 2, :, :], table(K_COS, GRP), ALU.mult).then_inc(qrope_a, 1)
            if some(n):
                pool.wait_ge(qrope_ok, n)
            swapped_sin(qs[:, b % 2, :, :], qr2, GRP).then_inc(qrope_b, 1)
            pool.wait_ge(qrope_a, n + 1)
            pool.wait_ge(qrope_b, n + 1)
            pool.tensor_tensor(qr[:, b % 2, :, :], qr[:, b % 2, :, :], qr2[:, :, :], ALU.add).then_inc(qrope_ok, 1)

        def normalise_q(k, b):
            pool.wait_ge(qrz_ok, 8 * k + b + 1)
            pool.tensor_tensor(eq[:, b % 2, :, :], eq[:, b % 2, :, :], spread(qrz[:, b % 2, :], D),
                               ALU.mult).then_inc(qnorm_ok, 1)

        def keys(m):
            pool.wait_ge(kall_ok, 2 * m + 2)
            if some(m):
                pool.wait_ge(krT_ps, m)
            pool.tensor_tensor(kr[:, :, :], kall[:, :, :], table(K_COS, HALF), ALU.mult).then_inc(krope_a, 1)
            if some(m):
                pool.wait_ge(krope_ok, m)
            swapped_sin(kall, kr2, HALF).then_inc(krope_b, 1)
            pool.wait_ge(krope_a, m + 1)
            pool.wait_ge(krope_b, m + 1)
            pool.tensor_tensor(kr[:, :, :], kr[:, :, :], kr2[:, :, :], ALU.add).then_inc(krope_ok, 1)
            pool.wait_ge(krz_ok, m + 1)
            pool.tensor_tensor(ek[:, :, :], ek[:, :, :], spread(krz[:, :], D), ALU.mult).then_inc(knorm_ok, 1)

        pool.wait_ge(consts_in, 16)
        keys(0)

        def head(k, last=False):
            for j in range(B):
                rotate_q(k, j)
                normalise_q(k, j)
                if j % HALF == 2 and not (last and j >= HALF):
                    keys(2 * k + (1 if j < HALF else 2))

        head(0)
        with pool.Fori(1, KVH - 1) as k:
            head(k)
        head(KVH - 1, last=True)

HC = 4
NCH = H // HC
XH, XK = 16, 32
XD = P // XH
XJ = XH * XK // P
NT = HID // P
E_NUM, RANK, TOP_K, RDIM = 64, 8, 16, 16
SCALING = 2.0

R_ID, R_HM, R_WQ, R_WK, R_WV, R_WM, R_B = 0, P, P + XH, 2 * P + XH, 3 * P + XH, 4 * P + XH, 5 * P + XH
R_ALL = R_B + 4


def head_mask():
    return (np.arange(P)[:, None] % XH == np.arange(XH)[None, :]).astype(np.float32)


def rest(nc, x, consts, small, ctxT, proj, keysT, wrT, Wo, AT, BT, out, oT, semctx, ctx):
    sb = lambda n, s, d=F32: ctx.enter_context(nc.sbuf_tensor(n, s, d))
    ps = lambda n, s, d=F32: ctx.enter_context(nc.psum_tensor(n, s, d))
    sem = lambda n: semctx.enter_context(nc.semaphore(n))

    cs = sb("cs", [P, R_ALL])
    ident = cs[:, R_ID:R_ID + P]
    wqT, wkT, wvT, wmT = (cs[:, o:o + P] for o in (R_WQ, R_WK, R_WV, R_WM))
    bq, bk, bv, bm = (cs[:, R_B + i:R_B + i + 1] for i in range(4))
    hmask = cs[:, R_HM:R_HM + XH]
    xs = sb("xs", [P, B, HID])
    wo_raw = sb("wo_raw", [P, 2, HC, HID])
    wo_hi = sb("wo_hi", [P, 2, HC, HID], F32R)
    wo_lo = sb("wo_lo", [P, 2, HC, HID], F32R)
    oF = sb("oF", [P, 2, HC, P], F32R)
    ctx_sb = sb("ctx_sb", [P, NT, B, P])
    proj_sb = sb("proj_sb", [P, NT, 2 * XK])
    ones = sb("ones", [P, P])
    cp = sb("cp", [P, 2, B, XK])
    kvb = sb("kvb", [P, 2, XK])
    kvx = sb("kvx", [P, 2, B, XK])
    hms = sb("hms", [P, XH])
    kbd = sb("kbd", [P, B, XH, XK])
    vbd = sb("vbd", [P, XH, XK])
    vbT = sb("vbT", [P, B, XJ, P])
    aT = sb("aT", [P, C, HID])
    bT = sb("bT", [P, C, HID])
    wr = sb("wr", [P, C, RDIM])
    keys = sb("keys", [RDIM, E_NUM])
    st6 = sb("st6", [P, 2, 6])
    mv2 = sb("mv2", [P, 2, 2])
    vep2 = sb("vep2", [P, 2])
    lnv = sb("lnv", [P, 2])
    y0 = sb("y0", [P, 2])
    y1 = sb("y1", [P, 2])
    y2 = sb("y2", [P, 2])
    rs2 = sb("rs2", [P, 2])
    xmx = sb("xmx", [P, 2, XH])
    xsm = sb("xsm", [P, 2, XH])
    xrz = sb("xrz", [P, 2, XH])
    top = sb("top", [P, 2, 8])
    top2 = sb("top2", [P, 8])
    ntop = sb("ntop", [P, 2])
    gsum = sb("gsum", [P, 2])
    grz = sb("grz", [P, 2])

    late = oT[:, 0:H - HC, :].rearrange("p h t -> p (h t)").bitcast(F32)
    taken = [0]

    def view(shape):
        n = int(np.prod(shape))
        at = taken[0]
        taken[0] += n
        assert taken[0] <= (H - HC) * B * P // 2
        letters = "abcd"[:len(shape)]
        return late[:, at:at + n].rearrange(f"p ({' '.join(letters)}) -> p {' '.join(letters)}",
                                            **{l: m for l, m in zip(letters[1:], shape[1:])})

    h2 = view([2, HID])
    qx = view([2, HID])
    ex = view([3, XH, XK])
    pxT = view([2, XJ, HID])
    xo = view([2, HID])
    h3T = view([2, C, P])
    zg = view([2, HID])
    zgT = view([2, C, P])
    fin = view([2, HID])
    q16 = view([2, P])[0:RDIM]
    gt = view([2, E_NUM])
    esc = view([2, E_NUM])
    sc2 = view([E_NUM])
    sc1 = view([E_NUM])
    sc = view([2, E_NUM])

    bank = [ps(f"bank{i}", [P, HID]) for i in range(8)]
    small_in = sem("small_in")
    ctx_in = sem("ctx_in")
    x2_in = sem("x2_in")
    ffn_in = sem("ffn_in")
    ones_ok = sem("ones_ok")
    cp_ps = sem("cp_ps")
    cp_ok = sem("cp_ok")
    sum_ps = sem("sum_ps")
    kvb_ok = sem("kvb_ok")
    kvx_ps = sem("kvx_ps")
    kvx_ok = sem("kvx_ok")
    hms_ok = sem("hms_ok")
    kbd_ok = sem("kbd_ok")
    vbd_ok = sem("vbd_ok")
    vbT_ps = sem("vbT_ps")
    vbT_ok = sem("vbT_ok")
    wo_hi_ok = sem("wo_hi_ok")
    wo_ok = sem("wo_ok")
    of_ok = sem("of_ok")
    w_ps = sem("w_ps")
    x1_ok = sem("x1_ok")
    st_ok = sem("st_ok")
    mv_ok2 = sem("mv_ok2")
    ve_ok = sem("ve_ok")
    lnv_ok = sem("lnv_ok")
    y0_ok = sem("y0_ok")
    nw1_ok = sem("nw1_ok")
    nw2_ok = sem("nw2_ok")
    rs_ok = sem("rs_ok")
    h2_ok = sem("h2_ok")
    qx_ps = sem("qx_ps")
    qx_ok = sem("qx_ok")
    xs_ps = sem("xs_ps")
    xmax_ok = sem("xmax_ok")
    xsub_ok = sem("xsub_ok")
    xexp_ok = sem("xexp_ok")
    xsum_ok = sem("xsum_ok")
    xrz_ok = sem("xrz_ok")
    xn_ok = sem("xn_ok")
    xt_ps = sem("xt_ps")
    xt_ok = sem("xt_ok")
    xv_ps = sem("xv_ps")
    xo_ok = sem("xo_ok")
    wm_ps = sem("wm_ps")
    x2_ok = sem("x2_ok")
    h3T_ps = sem("h3T_ps")
    h3T_ok = sem("h3T_ok")
    rq_ps = sem("rq_ps")
    rq_ok = sem("rq_ok")
    rs_ps = sem("rs_ps")
    sc_ok = sem("sc_ok")
    t1_ok = sem("t1_ok")
    r1_ok = sem("r1_ok")
    t2_ok = sem("t2_ok")
    r2_ok = sem("r2_ok")
    mk_ok = sem("mk_ok")
    nt_ok = sem("nt_ok")
    es_ok = sem("es_ok")
    gm_ok = sem("gm_ok")
    gs_ok = sem("gs_ok")
    gr_ok = sem("gr_ok")
    gt_ok = sem("gt_ok")
    z_ps = sem("z_ps")
    zg_ok = sem("zg_ok")
    zT_ps = sem("zT_ps")
    zT_ok = sem("zT_ok")
    f_ps = sem("f_ps")
    fin_ok = sem("fin_ok")

    stored = [sem("stored0"), sem("stored1")]
    wo_in = [sem("wo_in0"), sem("wo_in1")]

    wo_v = Wo.rearrange("(c h p) n -> c p h n", p=P, h=HC)

    def spread(ap, n):
        return ap.unsqueeze(2).broadcast_to([ap.shape[0], ap.shape[1], n])

    block = ctx.enter_context(nc.Block())

    @block.sync
    def _(sp):
        def weights(p):
            for u in range(2):
                if some(2 * p + u - 1):
                    sp.wait_ge(wo_ok, 2 * p + u - 1)
                sp.dma_start(wo_raw[:, u, :, :], wo_v[2 * p + u]).then_inc(wo_in[u], 16)

        weights(0)
        sp.dma_start(cs[:, :], small).then_inc(small_in, 16)
        sp.dma_start(proj_sb[:, :, :], proj.rearrange("(c p) k -> p c k", p=P)).then_inc(ctx_in, 16)
        for c in range(NT):
            sp.dma_start(ctx_sb[:, c, :, :], ctxT[:, c * P:(c + 1) * P, :].rearrange("b p d -> p b d")).then_inc(ctx_in, 16)
        sp.dma_start(xs[:, :, :], x.rearrange("b t d -> t b d")).then_inc(x2_in, 16)
        sp.dma_start(aT[:, :, :], AT.rearrange("(c p) n -> p c n", p=P)).then_inc(ffn_in, 16)
        sp.dma_start(bT[:, :, :], BT.rearrange("(c p) n -> p c n", p=P)).then_inc(ffn_in, 16)
        sp.dma_start(wr[:, :, :], wrT.rearrange("(c p) n -> p c n", p=P)).then_inc(ffn_in, 16)
        sp.dma_start(keys[:, :], keysT).then_inc(ffn_in, 16)
        with sp.Fori(1, NCH // 2) as p:
            weights(p)
        for b in range(B):
            sp.wait_ge(fin_ok, b + 1)
            sp.dma_start(out[b], fin[:, b % 2, :]).then_inc(stored[b % 2], 16)
        for done in stored:
            sp.wait_ge(done, 16 * B // 2)

    @block.tensor
    def _(pe):
        pe.wait_ge(ctx_in, 16 * (NT + 1))
        for b in range(B):
            for c in range(NT):
                mm = pe.matmul(bank[0][:, b * 2 * XK:(b + 1) * 2 * XK], ctx_sb[:, c, b, :], proj_sb[:, c, :],
                               start=(c == 0), stop=(c == NT - 1))
        mm.then_inc(cp_ps, 1)
        pe.wait_ge(ones_ok, 1)
        for c in range(NT):
            mm = pe.matmul(bank[1][:, 0:2 * XK], ones[:, :], proj_sb[:, c, :], start=(c == 0), stop=(c == NT - 1))
        mm.then_inc(sum_ps, 1)
        pe.wait_ge(small_in, 16)
        pe.wait_ge(cp_ok, 1)
        pe.matmul(bank[2][:, 0:B * XK], wkT, cp[:, 0, :, :].rearrange("p b k -> p (b k)"), start=True, stop=True)
        pe.matmul(bank[2][:, B * XK:2 * B * XK], wvT, cp[:, 1, :, :].rearrange("p b k -> p (b k)"),
                  start=True, stop=True).then_inc(kvx_ps, 1)
        for b in range(B):
            pe.wait_ge(vbd_ok, b + 1)
            if some(b - 1):
                pe.wait_ge(vbT_ok, b - 1)
            for j in range(XJ):
                mm = pe.transpose(bank[3 + b % 2][:, j * P:(j + 1) * P],
                                  vbd[:, :, :].rearrange("p h k -> p (h k)")[:, j * P:(j + 1) * P], ident)
            mm.then_inc(vbT_ps, 1)
        pe.wait_ge(vbT_ok, B)
        pe.wait_ge(kvx_ok, 2)

        def chunks(p, first=False):
            for u in range(2):
                pe.wait_ge(wo_ok, 2 * p + u + 1)
                for b in range(B):
                    pe.wait_ge(of_ok, 8 * (2 * p + u) + b + 1)
                    for h in range(HC):
                        new = first and u == 0 and h == 0
                        pe.matmul(bank[b][:, :], oF[:, b % 2, h, :], wo_hi[:, u, h, :], start=new, stop=False,
                                  skip_group_check=True)
                        mm = pe.matmul(bank[b][:, :], oF[:, b % 2, h, :], wo_lo[:, u, h, :], start=False,
                                       stop=(h == HC - 1), skip_group_check=True)
                    mm.then_inc(w_ps, 1)

        chunks(0, first=True)
        with pe.Fori(1, NCH // 2) as p:
            chunks(p)

        def query(b):
            pe.wait_ge(h2_ok, b + 1)
            pe.wait_ge(x1_ok, B)
            if some(b):
                pe.wait_ge(qx_ok, b)
            pe.matmul(bank[0][:, :], wqT, h2[:, b % 2, :], start=True, stop=True).then_inc(qx_ps, 1)

        def xscores(b, i):
            t = NT * b + i
            pe.wait_ge(qx_ok, b + 1)
            if some(t - 1):
                pe.wait_ge(xsub_ok, t - 1)
            pe.matmul(bank[1 + t % 2][:, :], qx[:, b % 2, i * P:(i + 1) * P],
                      kbd[:, b, :, :].rearrange("p h k -> p (h k)"), start=True, stop=True).then_inc(xs_ps, 1)

        def xtranspose(t):
            pe.wait_ge(xn_ok, t + 1)
            if some(t - 1):
                pe.wait_ge(xt_ok, t - 1)
            for j in range(XJ):
                mm = pe.transpose(bank[3 + t % 2][:, j * P:(j + 1) * P],
                                  ex[:, t % 3, :, :].rearrange("p h k -> p (h k)")[:, j * P:(j + 1) * P], ident)
            mm.then_inc(xt_ps, 1)

        def xmix(b):
            pe.wait_ge(xt_ok, NT * b + NT)
            if some(b):
                pe.wait_ge(xo_ok, b)
            for j in range(XJ):
                mm = pe.matmul(bank[5][:, :], vbT[:, b, j, :], pxT[:, b % 2, j, :], start=(j == 0), stop=(j == XJ - 1))
            mm.then_inc(xv_ps, 1)

        def xout(b):
            pe.wait_ge(xo_ok, b + 1)
            if some(b):
                pe.wait_ge(x2_ok, b)
            pe.matmul(bank[6][:, :], wmT, xo[:, b % 2, :], start=True, stop=True).then_inc(wm_ps, 1)

        query(0)
        for b in range(B + 1):
            for i in range(NT):
                t = NT * b + i
                if b < B:
                    xscores(b, i)
                if i == 0 and b + 1 < B:
                    query(b + 1)
                if 2 <= t < NT * B + 2:
                    xtranspose(t - 2)
                if i == 2 and b >= 1:
                    xmix(b - 1)
                if i == 3 and b >= 1:
                    xout(b - 1)

        def tokens(b):
            pe.wait_ge(h2_ok, B + b + 1)
            if some(b):
                pe.wait_ge(h3T_ok, b)
            for c in range(C):
                mm = pe.transpose(bank[0][:, c * P:(c + 1) * P], h2[:, b % 2, c * P:(c + 1) * P], ident)
            mm.then_inc(h3T_ps, 1)

        def router(b):
            pe.wait_ge(ffn_in, 64)
            pe.wait_ge(h3T_ok, b + 1)
            if some(b):
                pe.wait_ge(sc_ok, b)
            for c in range(C):
                mm = pe.matmul(bank[1][0:RDIM, 0:P], wr[:, c, :], h3T[:, b % 2, c, :], start=(c == 0), stop=(c == C - 1))
            mm.then_inc(rq_ps, 1)
            pe.wait_ge(rq_ok, b + 1)
            pe.matmul(bank[2][:, 0:E_NUM], q16[:, b % 2, :], keys[:, :], start=True, stop=True).then_inc(rs_ps, 1)

        def down(b):
            if some(b):
                pe.wait_ge(zg_ok, b)
            for c in range(C):
                mm = pe.matmul(bank[3][:, :], h3T[:, b % 2, c, :], aT[:, c, :], start=(c == 0), stop=(c == C - 1))
            mm.then_inc(z_ps, 1)

        def turn(b):
            pe.wait_ge(zg_ok, b + 1)
            if some(b):
                pe.wait_ge(zT_ok, b)
            for c in range(C):
                mm = pe.transpose(bank[4][:, c * P:(c + 1) * P], zg[:, b % 2, c * P:(c + 1) * P], ident)
            mm.then_inc(zT_ps, 1)

        def up(b):
            pe.wait_ge(zT_ok, b + 1)
            if some(b):
                pe.wait_ge(fin_ok, b)
            for c in range(C):
                mm = pe.matmul(bank[7][:, :], zgT[:, b % 2, c, :], bT[:, c, :], start=(c == 0), stop=(c == C - 1))
            mm.then_inc(f_ps, 1)

        tokens(0)
        router(0)
        for b in range(B + 1):
            if b + 1 < B:
                tokens(b + 1)
            if b < B:
                down(b)
            if b + 1 < B:
                router(b + 1)
            if b >= 1:
                turn(b - 1)
                up(b - 1)

    @block.scalar
    def _(act):
        def split(p, u):
            act.wait_ge(wo_in[u], 16 * p + 16)
            if some(8 * (2 * p + u - 1)):
                act.wait_ge(w_ps, 8 * (2 * p + u - 1))
            act.activation(wo_hi[:, u, :, :], wo_raw[:, u, :, :], ACT.Copy).then_inc(wo_hi_ok, 1)

        split(0, 0)
        act.wait_ge(cp_ps, 1)
        act.activation(cp[:, :, :, :], bank[0][:, :].rearrange("p (b a k) -> p a b k", b=B, a=2), ACT.Copy).then_inc(cp_ok, 1)
        split(0, 1)
        for b in range(B):
            act.wait_ge(vbT_ps, b + 1)
            act.activation(vbT[:, b, :, :], bank[3 + b % 2][:, :].rearrange("p (j c) -> p j c", j=XJ),
                           ACT.Copy).then_inc(vbT_ok, 1)
        with act.Fori(1, NCH // 2) as p:
            split(p, 0)
            split(p, 1)

        def rsqrt(n):
            act.wait_ge(ve_ok, n + 1)
            act.activation(lnv[:, n % 2:n % 2 + 1], vep2[:, n % 2:n % 2 + 1], ACT.Ln).then_inc(lnv_ok, 1)
            act.wait_ge(lnv_ok, n + 1)
            if some(n - 1):
                act.wait_ge(rs_ok, n - 1)
            act.activation(y0[:, n % 2:n % 2 + 1], lnv[:, n % 2:n % 2 + 1], ACT.Exp, scale=-0.5).then_inc(y0_ok, 1)

        def copy_query(b):
            act.wait_ge(qx_ps, b + 1)
            if some(NT * (b - 1)):
                act.wait_ge(xs_ps, NT * (b - 1))
            act.activation(qx[:, b % 2, :], bank[0][:, :], ACT.Identity, bias=bq).then_inc(qx_ok, 1)

        def xexp(t):
            act.wait_ge(xsub_ok, t + 1)
            act.activation(ex[:, t % 3, :, :], ex[:, t % 3, :, :], ACT.Exp).then_inc(xexp_ok, 1)

        def copy_xt(b, i):
            t = NT * b + i
            act.wait_ge(xt_ps, t + 1)
            if some(b - 1):
                act.wait_ge(xv_ps, b - 1)
            act.activation(pxT[:, b % 2, :, i * P:(i + 1) * P], bank[3 + t % 2][:, :].rearrange("p (j n) -> p j n", j=XJ),
                           ACT.Copy).then_inc(xt_ok, 1)

        def copy_mix(b):
            act.wait_ge(xv_ps, b + 1)
            if some(b - 1):
                act.wait_ge(wm_ps, b - 1)
            act.activation(xo[:, b % 2, :], bank[5][:, :], ACT.Copy).then_inc(xo_ok, 1)

        rsqrt(0)
        rsqrt(1)
        copy_query(0)
        for b in range(B + 1):
            for i in range(NT):
                t = NT * b + i
                if i == 0 and b + 1 < B:
                    copy_query(b + 1)
                if b < B:
                    xexp(t)
                if 2 <= t < NT * B + 2:
                    copy_xt((t - 2) // NT, (t - 2) % NT)
                if i == 1 and b + 2 < B:
                    rsqrt(b + 2)
                if i == 2 and b >= 1:
                    copy_mix(b - 1)

        def copy_h3T(b):
            act.wait_ge(h3T_ps, b + 1)
            if some(b - 1):
                act.wait_ge(z_ps, b - 1)
            if some(b - 1):
                act.wait_ge(rq_ps, b - 1)
            act.activation(h3T[:, b % 2, :, :], bank[0][:, :].rearrange("p (c t) -> p c t", c=C),
                           ACT.Copy).then_inc(h3T_ok, 1)

        def copy_router(b):
            act.wait_ge(rq_ps, b + 1)
            if some(b - 1):
                act.wait_ge(rs_ps, b - 1)
            act.activation(q16[:, b % 2, :], bank[1][0:RDIM, 0:P], ACT.Copy).then_inc(rq_ok, 1)
            act.wait_ge(rs_ps, b + 1)
            if some(b - 1):
                act.wait_ge(r2_ok, b - 1)
            if some(b - 1):
                act.wait_ge(es_ok, b - 1)
            act.activation(sc[:, b % 2, :], bank[2][:, 0:E_NUM], ACT.Copy).then_inc(sc_ok, 1)

        def exp_router(b):
            act.wait_ge(nt_ok, b + 1)
            act.wait_ge(sc_ok, b + 1)
            if some(b - 1):
                act.wait_ge(gm_ok, b - 1)
            act.activation(esc[:, b % 2, :], sc[:, b % 2, :], ACT.Exp, bias=ntop[:, b % 2:b % 2 + 1]).then_inc(es_ok, 1)

        def copy_zT(b):
            act.wait_ge(zT_ps, b + 1)
            if some(b - 1):
                act.wait_ge(f_ps, b - 1)
            act.activation(zgT[:, b % 2, :, :], bank[4][:, :].rearrange("p (c t) -> p c t", c=C),
                           ACT.Copy).then_inc(zT_ok, 1)

        rsqrt(B)
        rsqrt(B + 1)
        copy_h3T(0)
        copy_router(0)
        exp_router(0)
        for b in range(B + 1):
            if b + 1 < B:
                copy_h3T(b + 1)
            if b + 2 < B:
                rsqrt(B + b + 2)
            if b + 1 < B:
                copy_router(b + 1)
                exp_router(b + 1)
            if b >= 1:
                copy_zT(b - 1)

    @block.vector
    def _(dve):
        dve.memset(ones[:, :], 1.0).then_inc(ones_ok, 1)

        def split(p, u):
            dve.wait_ge(wo_hi_ok, 2 * p + u + 1)
            dve.tensor_tensor(wo_lo[:, u, :, :], wo_raw[:, u, :, :], wo_hi[:, u, :, :].bitcast(F32),
                              ALU.subtract).then_inc(wo_ok, 1)

        def widen(p, u, b):
            n = 8 * (2 * p + u) + b
            if some(n - 1):
                dve.wait_ge(w_ps, n - 1)
            dve.tensor_scalar(oF[:, b % 2, :, :], oT[:, bass.ds(HC * (2 * p + u), HC), b * P:(b + 1) * P], 1.0, None,
                              ALU.mult).then_inc(of_ok, 1)

        split(0, 0)
        dve.wait_ge(sum_ps, 1)
        dve.wait_ge(small_in, 16)
        dve.tensor_scalar(kvb[:, 0, :], bank[1][:, 0:XK], bk, None, ALU.mult).then_inc(kvb_ok, 1)
        dve.tensor_scalar(kvb[:, 1, :], bank[1][:, XK:2 * XK], bv, None, ALU.mult).then_inc(kvb_ok, 1)
        dve.tensor_scalar(hms[:, :], hmask, float(XD) ** -0.5, None, ALU.mult).then_inc(hms_ok, 1)
        dve.wait_ge(kvb_ok, 2)
        dve.wait_ge(kvx_ps, 1)
        for a in range(2):
            dve.tensor_tensor(kvx[:, a, :, :], bank[2][:, a * B * XK:(a + 1) * B * XK].rearrange("p (b k) -> p b k", b=B),
                              kvb[:, a, :].unsqueeze(1).broadcast_to([P, B, XK]), ALU.add).then_inc(kvx_ok, 1)
        split(0, 1)

        for u in range(2):
            for b in range(B):
                widen(0, u, b)
        with dve.Fori(1, NCH // 2) as p:
            for u in range(2):
                split(p, u)
                for b in range(B):
                    widen(p, u, b)

        def stats(n):
            i = n % 2
            dve.wait_ge(x1_ok if n < B else x2_ok, n % B + 1)
            dve.bn_stats(st6[:, i, :], xs[:, n % B, :]).then_inc(st_ok, 1)
            dve.wait_ge(st_ok, n + 1)
            dve.bn_aggr(mv2[:, i, :], st6[:, i, :]).then_inc(mv_ok2, 1)
            dve.wait_ge(mv_ok2, n + 1)
            if some(n - 1):
                dve.wait_ge(lnv_ok, n - 1)
            dve.tensor_scalar(vep2[:, i:i + 1], mv2[:, i, 1:2], EPS, None, ALU.add).then_inc(ve_ok, 1)

        def normalise(n):
            i = slice(n % 2, n % 2 + 1)
            dve.wait_ge(y0_ok, n + 1)
            dve.scalar_tensor_tensor(out=y1[:, i], in0=y0[:, i], scalar=vep2[:, i], in1=y0[:, i], op0=ALU.mult,
                                     op1=ALU.mult).then_inc(nw1_ok, 1)
            dve.wait_ge(nw1_ok, n + 1)
            dve.tensor_scalar(y2[:, i], y1[:, i], -0.5, 1.5, ALU.mult, ALU.add).then_inc(nw2_ok, 1)
            dve.wait_ge(nw2_ok, n + 1)
            dve.tensor_tensor(rs2[:, i], y0[:, i], y2[:, i], ALU.mult).then_inc(rs_ok, 1)
            dve.wait_ge(rs_ok, n + 1)
            if n < B:
                if some(n - 1):
                    dve.wait_ge(qx_ps, n - 1)
            else:
                dve.wait_ge(qx_ps, B)
                if some(n - B - 1):
                    dve.wait_ge(h3T_ps, n - B - 1)
            dve.tensor_scalar(h2[:, n % 2, :], xs[:, n % B, :], mv2[:, n % 2, 0:1], rs2[:, i], ALU.subtract,
                              ALU.mult).then_inc(h2_ok, 1)

        dve.wait_ge(x2_in, 16)
        for b in range(B):
            if some(8 * (NCH - 1) + b + 1):
                dve.wait_ge(w_ps, 8 * (NCH - 1) + b + 1)
            dve.tensor_tensor(xs[:, b, :], bank[b][:, :], xs[:, b, :], ALU.add).then_inc(x1_ok, 1)
            if b < 2:
                stats(b)
        normalise(0)
        normalise(1)

        def xmax(t):
            dve.wait_ge(xs_ps, t + 1)
            dve.tensor_reduce(xmx[:, t % 2, :], bank[1 + t % 2][:, :].rearrange("p (h k) -> p h k", h=XH), AX.X,
                              ALU.max).then_inc(xmax_ok, 1)
            dve.wait_ge(xmax_ok, t + 1)
            if some(t - 2):
                dve.wait_ge(xt_ps, t - 2)
            dve.tensor_tensor(ex[:, t % 3, :, :], bank[1 + t % 2][:, :].rearrange("p (h k) -> p h k", h=XH),
                              spread(xmx[:, t % 2, :], XK), ALU.subtract).then_inc(xsub_ok, 1)

        def xsum(t):
            dve.wait_ge(xexp_ok, t + 1)
            dve.tensor_reduce(xsm[:, t % 2, :], ex[:, t % 3, :, :], AX.X, ALU.add).then_inc(xsum_ok, 1)
            dve.wait_ge(xsum_ok, t + 1)
            if some(t - 1):
                dve.wait_ge(xn_ok, t - 1)
            dve.reciprocal(xrz[:, t % 2, :], xsm[:, t % 2, :]).then_inc(xrz_ok, 1)

        def residual(b):
            dve.wait_ge(wm_ps, b + 1)
            dve.scalar_tensor_tensor(out=xs[:, b, :], in0=bank[6][:, :], scalar=bm, in1=xs[:, b, :], op0=ALU.add,
                                     op1=ALU.add).then_inc(x2_ok, 1)

        for b in range(B + 1):
            for i in range(NT):
                t = NT * b + i
                if b < B:
                    xmax(t)
                if i == 0 and b >= 1 and b + 1 < B:
                    normalise(b + 1)
                if 1 <= t < NT * B + 1:
                    xsum(t - 1)
                if i == 0 and b + 2 < B:
                    stats(b + 2)
                if i == 3 and b >= 1:
                    residual(b - 1)

        def choose(b):
            i = b % 2
            dve.wait_ge(sc_ok, b + 1)
            dve.max(top[:, i, :], sc[:, i, :]).then_inc(t1_ok, 1)
            dve.wait_ge(t1_ok, b + 1)
            dve.match_replace(out=sc1[:, :], in_to_replace=top[:, i, :], in_values=sc[:, i, :],
                              imm_value=-3e38).then_inc(r1_ok, 1)
            if some(b - 1):
                dve.wait_ge(es_ok, b - 1)
            dve.tensor_scalar(ntop[:, i:i + 1], top[:, i, 0:1], -1.0, None, ALU.mult).then_inc(nt_ok, 1)
            dve.wait_ge(r1_ok, b + 1)
            dve.max(top2[:, :], sc1[:, :]).then_inc(t2_ok, 1)
            dve.wait_ge(t2_ok, b + 1)
            dve.match_replace(out=sc2[:, :], in_to_replace=top2[:, :], in_values=sc1[:, :],
                              imm_value=-3e38).then_inc(r2_ok, 1)
            dve.wait_ge(r2_ok, b + 1)
            dve.tensor_scalar(sc2[:, :], sc2[:, :], -2e38, None, ALU.is_lt).then_inc(mk_ok, 1)
            dve.wait_ge(mk_ok, b + 1)
            dve.wait_ge(es_ok, b + 1)
            dve.tensor_tensor(gt[:, i, :], esc[:, i, :], sc2[:, :], ALU.mult).then_inc(gm_ok, 1)
            dve.wait_ge(gm_ok, b + 1)
            dve.tensor_reduce(gsum[:, i:i + 1], gt[:, i, :], AX.X, ALU.add).then_inc(gs_ok, 1)
            dve.wait_ge(gs_ok, b + 1)
            dve.reciprocal(grz[:, i:i + 1], gsum[:, i:i + 1]).then_inc(gr_ok, 1)
            dve.wait_ge(gr_ok, b + 1)
            dve.tensor_scalar(gt[:, i, :], gt[:, i, :], grz[:, i:i + 1], SCALING, ALU.mult, ALU.mult).then_inc(gt_ok, 1)

        def gated(b):
            dve.wait_ge(z_ps, b + 1)
            dve.wait_ge(gt_ok, b + 1)
            if some(b - 1):
                dve.wait_ge(zT_ps, b - 1)
            dve.tensor_tensor(zg[:, b % 2, :].rearrange("p (e r) -> p e r", r=RANK),
                              bank[3][:, :].rearrange("p (e r) -> p e r", r=RANK),
                              spread(gt[:, b % 2, :], RANK), ALU.mult).then_inc(zg_ok, 1)

        def finish(b):
            dve.wait_ge(f_ps, b + 1)
            if some(16 * (b // 2)):
                dve.wait_ge(stored[b % 2], 16 * (b // 2))
            dve.tensor_tensor(fin[:, b % 2, :], bank[7][:, :], xs[:, b, :], ALU.add).then_inc(fin_ok, 1)

        stats(B)
        stats(B + 1)
        normalise(B)
        normalise(B + 1)
        choose(0)
        for b in range(B + 1):
            if b < B:
                if b + 2 < B:
                    stats(B + b + 2)
                gated(b)
            if b + 1 < B:
                choose(b + 1)
            if b + 2 < B:
                normalise(B + b + 2)
            if b >= 1:
                finish(b - 1)

    @block.gpsimd
    def _(pool):
        pool.wait_ge(kvx_ok, 2)
        pool.wait_ge(hms_ok, 1)
        for b in range(B):
            pool.tensor_tensor(kbd[:, b, :, :], kvx[:, 0, b, :].unsqueeze(1).broadcast_to([P, XH, XK]),
                               spread(hms[:, :], XK), ALU.mult).then_inc(kbd_ok, 1)
            if some(b):
                pool.wait_ge(vbT_ps, b)
            pool.tensor_tensor(vbd[:, :, :], kvx[:, 1, b, :].unsqueeze(1).broadcast_to([P, XH, XK]),
                               spread(hmask, XK), ALU.mult).then_inc(vbd_ok, 1)

        for t in range(NT * B):
            pool.wait_ge(xrz_ok, t + 1)
            pool.tensor_tensor(ex[:, t % 3, :, :], ex[:, t % 3, :, :], spread(xrz[:, t % 2, :], XK),
                               ALU.mult).then_inc(xn_ok, 1)


def build(nc, x, consts, small, ctxT, proj, keysT, wrT, Wq, Wk, Wv, Wo, AT, BT, out):
    with ExitStack() as outer:
        oT = outer.enter_context(nc.sbuf_tensor("oT", [P, H, B * P], BF16))
        xall = oT[:, 0:B, :].rearrange("p h t -> p (h t)").bitcast(F32).rearrange("p (b n) -> p b n", b=B)
        with ExitStack() as ctx:
            attention(nc, x, consts, Wq, Wk, Wv, oT, xall, outer, ctx)
        with ExitStack() as ctx:
            rest(nc, x, consts, small, ctxT, proj, keysT, wrT, Wo, AT, BT, out, oT, outer, ctx)


def kernel(**inputs):
    import numpy as _np
    import concourse.bacc as _bacc
    from concourse import mybir as _mybir
    from concourse.bass_utils import run_bass_kernel_spmd as _run

    nc = _bacc.Bacc("TRN2", target_bir_lowering=False, num_devices=1)
    g = {n: _np.asarray(a) for n, a in inputs.items()}
    X = "L0_xattn_"
    column = lambda n: g[X + n].reshape(P, 1)
    ins = {
        "x": g["x"],
        "consts": constants(),
        "small": _np.concatenate([_np.eye(P, dtype=_np.float32), head_mask(), g[X + "Wq"].T, g[X + "Wk"].T, g[X + "Wv"].T,
                                  g[X + "Wm"].T, column("bq"), column("bk"), column("bv"), column("bm")], axis=1),
        "ctxT": g["ctx_4096"].transpose(0, 2, 1),
        "proj": _np.concatenate([g[X + "proj_k"], g[X + "proj_v"]], axis=1),
        "keysT": g["L0_ffn_keys"].T,
        "wrT": g["L0_ffn_Wq_w"].T,
        "Wq": g["L0_attn_Wq"], "Wk": g["L0_attn_Wk"], "Wv": g["L0_attn_Wv"], "Wo": g["L0_attn_Wo"],
        "AT": g["L0_ffn_A_w"].T, "BT": g["L0_ffn_B_w"].T,
    }
    arrays, args = {}, []
    for name, a in ins.items():
        a = _np.ascontiguousarray(a)
        arrays[f"in_{name}"] = a
        args.append(nc.dram_tensor(f"in_{name}", a.shape, _mybir.dt.from_np(a.dtype), kind="ExternalInput").ap())
    args.append(nc.dram_tensor("out_x", (B, P, HID), _mybir.dt.float32, kind="ExternalOutput").ap())
    build(nc, *args)
    r = _run(nc, [arrays], core_ids=[0])
    return r.results[0]["out_x"]
```

```python
import concourse.bass as bass
import numpy as np
from concourse import mybir
from contextlib import ExitStack

F32 = mybir.dt.float32
F32R = mybir.dt.float32r
BF16 = mybir.dt.bfloat16
ALU = mybir.AluOpType
ACT = mybir.ActivationFunctionType
AX = mybir.AxisListType

P = 128
B = 8
HID = 512
C = HID // P
KVH = 8
GRP = 4
H = KVH * GRP
D = 128
WIN = 64
BLK = 32
NB = P // BLK
SPAN = WIN + BLK
LW = [BLK * (i + 1) for i in range(NB)]
LO = [sum(LW[:i]) for i in range(NB)]
LT = sum(LW)
HALF = B // 2
HC = 4
NCH = H // HC
THETA = 10000.0
GATE_NORM = 16.0
EPS = 1e-5
BIG = 1e30

K_ID, K_COS, K_SIN, K_AB, K_MS, K_ML = 0, P, 2 * P, 3 * P, 4 * P + LT, 4 * P + LT + NB * SPAN
K_ALL = K_ML + LT


def constants():
    c = np.zeros((P, K_ALL), np.float32)
    t = np.arange(P)
    c[:, K_ID:K_ID + P] = np.eye(P)
    half = np.arange(D // 2, dtype=np.float32)
    inv = (np.float32(1.0) / np.float32(THETA) ** (np.float32(2.0) * half / np.float32(D))).astype(np.float32)
    angle = t[:, None].astype(np.float32) * inv[None, :]
    cos, sin = np.cos(angle.astype(np.float64)), np.sin(angle.astype(np.float64))
    c[:, K_COS:K_COS + D] = np.concatenate([cos, cos], 1)
    c[:, K_SIN:K_SIN + D] = np.concatenate([-sin, sin], 1)
    upto = (t[:, None] <= t[None, :]).astype(np.float32)
    mid = BLK * (t // BLK) + BLK // 2 - 1
    ab = c[:, K_AB:K_AB + P + LT]
    ab[:, 0:P] = (upto - upto[:, mid]) / GATE_NORM
    for i in range(NB):
        m = BLK * i + BLK // 2 - 1
        ab[:, P + LO[i]:P + LO[i] + LW[i]] = (upto[:, m:m + 1] - upto[:, 0:LW[i]]) / GATE_NORM
    row = t % BLK
    ms = c[:, K_MS:K_MS + NB * SPAN].reshape(P, NB, SPAN)
    for i in range(NB):
        s = BLK * i - WIN + np.arange(SPAN)[None, :]
        back = BLK * i + row[:, None] - s
        ms[:, i] = np.where((s >= 0) & (back >= 0) & (back <= WIN), 0.0, -BIG)
        c[:, K_ML + LO[i]:K_ML + LO[i] + LW[i]] = 0.5 * (np.arange(LW[i])[None, :] <= BLK * i + row[:, None])
    return c


def some(count):
    return not isinstance(count, int) or count > 0


def attention(nc, x, consts, Wq, Wk, Wv, Wo, oT, xall, wq_raw, wq_hi, wq_lo, semctx, ctx):
    sb = lambda n, s, d=F32: ctx.enter_context(nc.sbuf_tensor(n, s, d))
    ps = lambda n, s, d=F32: ctx.enter_context(nc.psum_tensor(n, s, d))
    sem = lambda n: semctx.enter_context(nc.semaphore(n))

    cst = sb("cst", [P, K_ALL])
    ident = cst[:, K_ID:K_ID + P]
    mask_w = cst[:, K_MS:K_MS + NB * SPAN].rearrange("p (i s) -> p i s", i=NB)
    mask_l = cst[:, K_ML:K_ML + LT]
    ab = sb("ab", [P, P + LT], F32R)
    stats = sb("stats", [P, B, 6])
    veps = sb("veps", [P, B])
    mv = sb("mv", [P, B, 2])
    std = sb("std", [P, B])
    rstd = sb("rstd", [P, B])
    newt = sb("newt", [P, B])
    hT_hi = sb("hT_hi", [P, C, B * P], F32R)
    hT_lo = sb("hT_lo", [P, C, B * P], F32R)
    wkv_raw = sb("wkv_raw", [P, C, 2 * D])
    wkv_hi = sb("wkv_hi", [P, C, 2 * D], F32R)
    wkv_lo = sb("wkv_lo", [P, C, 2 * D], F32R)
    kall = sb("kall", [P, HALF, D])
    ek = sb("ek", [P, HALF, D])
    gate = sb("gate", [P, HALF, D])
    g_hi = sb("g_hi", [P, HALF, D], F32R)
    g_lo = sb("g_lo", [P, HALF, D], F32R)
    kr = sb("kr", [P, HALF, D])
    kr2 = sb("kr2", [P, HALF, D])
    kmx = sb("kmx", [P, HALF])
    ksm = sb("ksm", [P, HALF])
    krz = sb("krz", [P, HALF])
    ksT = sb("ksT", [P, HALF, P])
    krT = sb("krT", [P, B, WIN + P])
    dec = sb("dec", [P, B, P + LT])
    vS = sb("vS", [P, B, D])
    qs = sb("qs", [P, 2, GRP, D])
    eq = sb("eq", [P, 2, GRP, D])
    qr = sb("qr", [P, 2, GRP, D])
    qr2 = sb("qr2", [P, GRP, D])
    qmx = sb("qmx", [P, 2, GRP])
    qsm = sb("qsm", [P, 2, GRP])
    qrz = sb("qrz", [P, 2, GRP])
    qrT = sb("qrT", [P, NB, GRP, BLK])
    qdT = sb("qdT", [P, NB, GRP, BLK])
    ss = sb("ss", [P, NB, SPAN])
    smx = sb("smx", [P, NB])
    ssm = sb("ssm", [P, NB])
    srz = sb("srz", [P, NB])
    srh = sb("srh", [P, NB])
    pm = sb("pm", [P, 2, LT])
    pT = sb("pT", [P, NB * P])

    Qp = ps("Qp", [P, GRP, D])
    TQ = ps("TQ", [P, GRP, NB, BLK])
    TE = ps("TE", [P, GRP, NB, BLK])
    Sp = ps("Sp", [P, 512])
    Lp = ps("Lp", [P, 512])
    PTp = ps("PTp", [P, NB * P])
    OTp = ps("OTp", [P, NB, GRP, BLK])
    Kp = ps("Kp", [P, 512])

    x_in = [sem(f"x_in{b}") for b in range(B)]
    consts_in = sem("consts_in")
    var_ok = sem("var_ok")
    kall_ok = sem("kall_ok")
    wq_in = sem("wq_in")
    wo_first = sem("wo_first")
    wo_first_hi = sem("wo_first_hi")
    wkv_in = sem("wkv_in")
    stats_ok = sem("stats_ok")
    mv_ok = sem("mv_ok")
    lnv_ok = sem("lnv_ok1")
    std_ok = sem("std_ok")
    newton_ok = sem("newton_ok")
    h_ok = sem("h_ok")
    hT_ps = sem("hT_ps")
    hT_ok = sem("hT_ok")
    hT_lo_ok = sem("hT_lo_ok")
    ab_ok = sem("ab_ok")
    pads_ok = sem("pads_ok")
    wq_hi_ok = sem("wq_hi_ok")
    wq_ok = sem("wq_ok")
    wkv_hi_ok = sem("wkv_hi_ok")
    wkv_ok = sem("wkv_ok")
    kv_ps = sem("kv_ps")
    kv_ok = sem("kv_ok")
    kmax_ok = sem("kmax_ok")
    ksub_ok = sem("ksub_ok")
    kexp_ok = sem("kexp_ok")
    ksum_ok = sem("ksum_ok")
    krz_ok = sem("krz_ok")
    knorm_ok = sem("knorm_ok")
    gabs_ok = sem("gabs_ok")
    gexp_ok = sem("gexp_ok")
    gln_ok = sem("gln_ok")
    gate_ok = sem("gate_ok")
    ghi_ok = sem("ghi_ok")
    glo_ok = sem("glo_ok")
    krope_a = sem("krope_a")
    krope_b = sem("krope_b")
    krope_ok = sem("krope_ok")
    krT_ps = sem("krT_ps")
    krT_ok = sem("krT_ok")
    ksT_ps = sem("ksT_ps")
    ksT_ok = sem("ksT_ok")
    dec_ps = sem("dec_ps")
    dec_ok = sem("dec_ok")
    kd_ok = sem("kd_ok")
    q_ps = sem("q_ps")
    q_ok = sem("q_ok")
    qmax_ok = sem("qmax_ok")
    qexp_ok = sem("qexp_ok")
    qrz_ok = sem("qrz_ok")
    qnorm_ok = sem("qnorm_ok")
    qrope_a = sem("qrope_a")
    qrope_b = sem("qrope_b")
    qrope_ok = sem("qrope_ok")
    qrT_ps = sem("qrT_ps")
    qrT_ok = sem("qrT_ok")
    qeT_ps = sem("qeT_ps")
    qdT_ok = sem("qdT_ok")
    s_ps = sem("s_ps")
    l_ps = sem("l_ps")
    smask_ok = sem("smask_ok")
    smax_ok = sem("smax_ok")
    ssub_ok = sem("ssub_ok")
    sexp_ok = sem("sexp_ok")
    ssum_ok = sem("ssum_ok")
    srz_ok = sem("srz_ok")
    srh_ok = sem("srh_ok")
    lin_ok = sem("lin_ok")
    p_ok = sem("p_ok")
    pT_ps = sem("pT_ps")
    pT_ok = sem("pT_ok")
    o_ps = sem("o_ps")
    o_ok = sem("o_ok")

    def spread(ap, n):
        return ap.unsqueeze(2).broadcast_to([ap.shape[0], ap.shape[1], n])

    def table(lo, n):
        return cst[:, lo:lo + D].unsqueeze(1).broadcast_to([P, n, D])

    wq_v = Wq.rearrange("(c p) (k n) -> k p c n", p=P, k=KVH)
    wk_v = Wk.rearrange("(c p) (k n) -> k p c n", p=P, k=KVH)
    wv_v = Wv.rearrange("(c p) (k n) -> k p c n", p=P, k=KVH)
    x_v = x.rearrange("b t d -> t b d")
    x8 = xall

    block = ctx.enter_context(nc.Block())

    @block.sync
    def _(sp):
        sp.dma_start(cst[:, :], consts).then_inc(consts_in, 16)
        for b in range(B):
            sp.dma_start(x8[:, b, :], x_v[:, b, :]).then_inc(x_in[b], 16)
            if b == 1:
                sp.dma_start(wkv_raw[:, :, 0:D], wk_v[0]).then_inc(wkv_in, 16)
                sp.dma_start(wkv_raw[:, :, D:2 * D], wv_v[0]).then_inc(wkv_in, 16)
            if b == 3:
                sp.dma_start(wq_raw[:, :, :], wq_v[0]).then_inc(wq_in, 16)

        def weights(k):
            sp.wait_ge(wkv_ok, k)
            sp.dma_start(wkv_raw[:, :, 0:D], wk_v[k]).then_inc(wkv_in, 16)
            sp.dma_start(wkv_raw[:, :, D:2 * D], wv_v[k]).then_inc(wkv_in, 16)
            sp.wait_ge(wq_ok, C * k)
            sp.dma_start(wq_raw[:, :, :], wq_v[k]).then_inc(wq_in, 16)

        for k in range(1, KVH):
            weights(k)
        sp.wait_ge(wq_ok, C * KVH)
        sp.dma_start(wq_raw[:, :, :], Wo[0:HC * P, :].rearrange("(h p) n -> p h n", p=P)).then_inc(wo_first, 16)

    @block.tensor
    def _(pe):
        def product(out, hi, lo, whi, wlo, split_of=None):
            for c in range(C):
                if split_of is not None:
                    pe.wait_ge(wq_ok, C * split_of + c + 1)
                pe.matmul(out, hi[c], whi[c], start=(c == 0), stop=False)
                pe.matmul(out, hi[c], wlo[c], start=False, stop=False)
                mm = pe.matmul(out, lo[c], whi[c], start=False, stop=(c == C - 1))
            return mm

        def h_of(b):
            return [[t[:, c, b * P:(b + 1) * P] for c in range(C)] for t in (hT_hi, hT_lo)]

        def project_q(k, b):
            if some(8 * k + b):
                pe.wait_ge(q_ok, 8 * k + b)
            product(Qp[:, :, :].rearrange("p h d -> p (h d)"), *h_of(b), [wq_hi[:, c, :] for c in range(C)],
                    [wq_lo[:, c, :] for c in range(C)], split_of=k if b == 0 else None).then_inc(q_ps, 1)

        def transpose_q(k, b):
            n = 8 * k + b
            pe.wait_ge(qrope_ok, n + 1)
            if some(n):
                pe.wait_ge(qrT_ok, n)
            for h in range(GRP):
                mm = pe.transpose(TQ[:, h, :, :].rearrange("p i t -> p (i t)"), qr[:, b % 2, h, :], ident)
            mm.then_inc(qrT_ps, 1)
            pe.wait_ge(qnorm_ok, n + 1)
            if some(n):
                pe.wait_ge(qdT_ok, n)
            for h in range(GRP):
                mm = pe.transpose(TE[:, h, :, :].rearrange("p i t -> p (i t)"), eq[:, b % 2, h, :], ident)
            mm.then_inc(qeT_ps, 1)

        def scores(k, b):
            n = 8 * k + b
            m = 2 * k + b // HALF
            if b % HALF == 0:
                pe.wait_ge(krT_ok, m + 1)
            pe.wait_ge(qrT_ok, n + 1)
            if some(n):
                pe.wait_ge(smask_ok, n)
            for i in range(NB):
                mm = pe.matmul(Sp[:, i * SPAN:(i + 1) * SPAN], qrT[:, i, :, :].rearrange("p h t -> p (h t)"),
                               krT[:, b, BLK * i:BLK * i + SPAN], start=True, stop=True)
            mm.then_inc(s_ps, 1)

        def linear_scores(k, b):
            n = 8 * k + b
            if b % HALF == 0:
                pe.wait_ge(kd_ok, 2 * k + b // HALF + 1)
            pe.wait_ge(qdT_ok, n + 1)
            if some(n):
                pe.wait_ge(lin_ok, n)
            for i in range(NB):
                mm = pe.matmul(Lp[:, LO[i]:LO[i] + LW[i]], qdT[:, i, :, :].rearrange("p h t -> p (h t)"),
                               dec[:, b, P + LO[i]:P + LO[i] + LW[i]], start=True, stop=True)
            mm.then_inc(l_ps, 1)

        def transpose_p(k, b):
            n = 8 * k + b
            pe.wait_ge(p_ok, n + 1)
            if some(n):
                pe.wait_ge(pT_ok, n)
            if isinstance(n, int) and n == 0:
                pe.wait_ge(pads_ok, 2)
            for i in range(NB):
                mm = pe.transpose(PTp[0:LW[i], i * P:(i + 1) * P], pm[:, b % 2, LO[i]:LO[i] + LW[i]], ident)
            mm.then_inc(pT_ps, 1)

        def mix(k, b):
            n = 8 * k + b
            pe.wait_ge(pT_ok, n + 1)
            if some(n):
                pe.wait_ge(o_ok, n)
            pe.matmul(OTp[:, :, :, :].rearrange("p i h t -> p (i h t)"), vS[:, b, :], pT[:, :],
                      start=True, stop=True).then_inc(o_ps, 1)

        def project_kv(k, hf, pair):
            m = 2 * k + hf
            if pair == 0:
                pe.wait_ge(wkv_ok, k + 1)
                if some(4 * m):
                    pe.wait_ge(dec_ok, 4 * m)
            else:
                pe.wait_ge(kv_ok, 2 * m + 1)
            for y in range(2):
                b = HALF * hf + 2 * pair + y
                mm = product(Kp[:, y * 2 * D:(y + 1) * 2 * D], *h_of(b), [wkv_hi[:, c, :] for c in range(C)],
                             [wkv_lo[:, c, :] for c in range(C)])
            mm.then_inc(kv_ps, 1)

        def transpose_kr(m):
            pe.wait_ge(krope_ok, m + 1)
            pe.wait_ge(kv_ok, 2 * m + 2)
            for y in range(HALF):
                mm = pe.transpose(Kp[:, y * P:(y + 1) * P], kr[:, y, :], ident)
            mm.then_inc(krT_ps, 1)

        def transpose_ks(m):
            pe.wait_ge(knorm_ok, m + 1)
            pe.wait_ge(krT_ok, m + 1)
            for y in range(HALF):
                mm = pe.transpose(Kp[:, y * P:(y + 1) * P], ek[:, y, :], ident)
            mm.then_inc(ksT_ps, 1)

        def decays(m, y):
            if y == 0:
                pe.wait_ge(glo_ok, m + 1)
                pe.wait_ge(ksT_ok, m + 1)
            else:
                if some(4 * m + y):
                    pe.wait_ge(dec_ok, 4 * m + y)
            pe.matmul(Kp[:, 0:P + LT], g_hi[:, y, :], ab[:, :], start=True, stop=False)
            pe.matmul(Kp[:, 0:P + LT], g_lo[:, y, :], ab[:, :], start=False, stop=True).then_inc(dec_ps, 1)

        pe.wait_ge(consts_in, 16)
        for b in range(B):
            bank = (Kp, Sp)[b % 2]
            pe.wait_ge(h_ok, b + 1)
            if some(b - 1):
                pe.wait_ge(hT_lo_ok, b - 1)
            for c in range(C):
                mm = pe.transpose(bank[:, c * P:(c + 1) * P], x8[:, b, c * P:(c + 1) * P], ident)
            mm.then_inc(hT_ps, 1)
        pe.wait_ge(ab_ok, 1)
        pe.wait_ge(hT_lo_ok, B)
        project_kv(0, 0, 0)
        project_kv(0, 0, 1)
        transpose_kr(0)
        transpose_ks(0)
        decays(0, 0)

        def head(k, first=False, last=False):
            for j in range(B):
                w = j % HALF
                kk, hf = (k, 1) if j < HALF else (k + 1, 0)
                m = 2 * kk + hf
                work = not (last and j >= HALF)
                k1, b1 = (k, j - 1) if j >= 1 else (k - 1, B - 1)
                k2, b2 = (k, j - 2) if j >= 2 else (k - 1, B + j - 2)
                live1, live2 = not (first and j < 1), not (first and j < 2)
                if w == 0:
                    decays(m - 1, 1)
                project_q(k, j)
                if w == 0:
                    decays(m - 1, 2)
                if w == 2 and work:
                    project_kv(kk, hf, 1)
                if w == 3 and work:
                    transpose_kr(m)
                if live1:
                    transpose_q(k1, b1)
                if w == 0:
                    decays(m - 1, 3)
                if live1:
                    scores(k1, b1)
                if live2:
                    transpose_p(k2, b2)
                if live1:
                    linear_scores(k1, b1)
                if w == 3 and work:
                    transpose_ks(m)
                if live2:
                    mix(k2, b2)
                if w == 1 and work:
                    project_kv(kk, hf, 0)
                if w == 3 and work:
                    decays(m, 0)

        head(0, first=True)
        with pe.Fori(1, KVH - 1) as k:
            head(k)
        head(KVH - 1, last=True)
        transpose_q(KVH - 1, B - 1)
        transpose_p(KVH - 1, B - 2)
        scores(KVH - 1, B - 1)
        linear_scores(KVH - 1, B - 1)
        mix(KVH - 1, B - 2)
        transpose_p(KVH - 1, B - 1)
        mix(KVH - 1, B - 1)

    @block.scalar
    def _(act):
        def split_wkv(k):
            act.wait_ge(wkv_in, 32 * k + 32)
            if some(4 * k):
                act.wait_ge(kv_ps, 4 * k)
            act.activation(wkv_hi[:, :, :], wkv_raw[:, :, :], ACT.Copy).then_inc(wkv_hi_ok, 1)

        def split_wq(k, c):
            act.wait_ge(wq_in, 16 * k + 16)
            if some(8 * k):
                act.wait_ge(q_ps, 8 * k)
            act.activation(wq_hi[:, c, :], wq_raw[:, c, :], ACT.Copy).then_inc(wq_hi_ok, 1)

        def copy_q(k, b):
            n = 8 * k + b
            act.wait_ge(q_ps, n + 1)
            if some(n - 1):
                act.wait_ge(qrope_b, n - 1)
            act.activation(qs[:, b % 2, :, :], Qp[:, :, :], ACT.Copy).then_inc(q_ok, 1)

        def exp_q(k, b):
            n = 8 * k + b
            act.wait_ge(qmax_ok, n + 1)
            if some(n - 1):
                act.wait_ge(qeT_ps, n - 1)
                act.wait_ge(qrz_ok, n - 1)
            for h in range(GRP):
                op = act.activation(eq[:, b % 2, h, :], qs[:, b % 2, h, :], ACT.Exp, bias=qmx[:, b % 2, h:h + 1],
                                    accum_out=qsm[:, b % 2, h:h + 1])
            op.then_inc(qexp_ok, 1)

        def copy_qrT(k, b):
            n = 8 * k + b
            act.wait_ge(qrT_ps, n + 1)
            if some(n):
                act.wait_ge(s_ps, n)
            act.activation(qrT[:, :, :, :], TQ[:, :, :, :].rearrange("p h i t -> p i h t"),
                           ACT.Copy).then_inc(qrT_ok, 1)

        def exp_s(k, b):
            act.wait_ge(ssub_ok, 8 * k + b + 1)
            act.activation(ss[:, :, :], ss[:, :, :], ACT.Exp).then_inc(sexp_ok, 1)

        def copy_pT(k, b):
            n = 8 * k + b
            act.wait_ge(pT_ps, n + 1)
            if some(n):
                act.wait_ge(o_ps, n)
            act.activation(pT[:, :], PTp[:, :], ACT.Copy).then_inc(pT_ok, 1)

        def copy_o(k, b):
            act.wait_ge(o_ps, 8 * k + b + 1)
            act.wait_ge(ab_ok, 1)
            act.activation(oT[:, bass.ds(GRP * k, GRP), b * P:(b + 1) * P].rearrange("p h (i t) -> p i h t", i=NB),
                           OTp[:, :, :, :], ACT.Copy).then_inc(o_ok, 1)

        def copy_kv(k, hf, pair):
            m = 2 * k + hf
            kv = Kp[:, :].rearrange("p (y a d) -> p y a d", y=2, a=2)
            act.wait_ge(kv_ps, 2 * m + pair + 1)
            if pair == 0:
                if some(m):
                    act.wait_ge(ksub_ok, m)
                if some(m):
                    act.wait_ge(gate_ok, m)
                if some(m):
                    act.wait_ge(gabs_ok, m)
                if some(m):
                    act.wait_ge(krope_b, m)
            act.activation(kall[:, 2 * pair:2 * pair + 2, :], kv[:, :, 0, :], ACT.Copy).then_inc(kall_ok, 1)
            if some(8 * k + HALF * hf - HALF):
                act.wait_ge(o_ps, 8 * k + HALF * hf - HALF)
            b = HALF * hf + 2 * pair
            act.activation(vS[:, b:b + 2, :], kv[:, :, 1, :], ACT.Copy).then_inc(kv_ok, 1)

        def gates(m):
            act.wait_ge(kall_ok, 2 * m + 2)
            if some(m):
                act.wait_ge(glo_ok, m)
            act.activation(gate[:, :, :], kall[:, :, :], ACT.Abs).then_inc(gabs_ok, 1)
            act.wait_ge(gabs_ok, m + 1)
            act.activation(gate[:, :, :], gate[:, :, :], ACT.Exp, scale=-1.0).then_inc(gexp_ok, 1)
            act.wait_ge(gexp_ok, m + 1)
            act.activation(gate[:, :, :], gate[:, :, :], ACT.Ln, bias=1.0).then_inc(gln_ok, 1)

        def exp_k(m):
            act.wait_ge(ksub_ok, m + 1)
            act.activation(ek[:, :, :], ek[:, :, :], ACT.Exp).then_inc(kexp_ok, 1)

        def gate_hi(m):
            act.wait_ge(gate_ok, m + 1)
            if some(4 * m):
                act.wait_ge(dec_ps, 4 * m)
            act.activation(g_hi[:, :, :], gate[:, :, :], ACT.Copy).then_inc(ghi_ok, 1)

        def copy_krT(k, hf):
            m = 2 * k + hf
            act.wait_ge(krT_ps, m + 1)
            if some(8 * k + HALF * hf - HALF):
                act.wait_ge(s_ps, 8 * k + HALF * hf - HALF)
            act.activation(krT[:, HALF * hf:HALF * hf + HALF, WIN:WIN + P],
                           Kp[:, :].rearrange("p (y s) -> p y s", y=HALF), ACT.Copy).then_inc(krT_ok, 1)

        def copy_ksT(m):
            act.wait_ge(ksT_ps, m + 1)
            if some(m):
                act.wait_ge(kd_ok, m)
            act.activation(ksT[:, :, :], Kp[:, :].rearrange("p (y s) -> p y s", y=HALF), ACT.Copy).then_inc(ksT_ok, 1)

        def exp_dec(k, hf, y):
            m = 2 * k + hf
            act.wait_ge(dec_ps, 4 * m + y + 1)
            if some(8 * k + HALF * hf - HALF):
                act.wait_ge(l_ps, 8 * k + HALF * hf - HALF)
            act.activation(dec[:, HALF * hf + y, :], Kp[:, 0:P + LT], ACT.Exp).then_inc(dec_ok, 1)

        act.preload_act_table_set("natural_log_exp_and_others")
        act.wait_ge(consts_in, 16)
        act.activation(ab[:, :], cst[:, K_AB:K_AB + P + LT], ACT.Copy).then_inc(ab_ok, 1)
        act.wait_ge(var_ok, 1)
        act.activation(std[:, :], veps[:, :], ACT.Ln).then_inc(lnv_ok, 1)
        act.wait_ge(lnv_ok, 1)
        act.activation(rstd[:, :], std[:, :], ACT.Exp, scale=-0.5).then_inc(std_ok, 1)
        split_wkv(0)
        for c in range(C):
            split_wq(0, c)
        for b in range(B):
            bank = (Kp, Sp)[b % 2]
            act.wait_ge(hT_ps, b + 1)
            act.activation(hT_hi[:, :, b * P:(b + 1) * P], bank[:, :].rearrange("p (c t) -> p c t", c=C),
                           ACT.Copy).then_inc(hT_ok, 1)
        copy_kv(0, 0, 0)
        copy_kv(0, 0, 1)
        gates(0)
        exp_k(0)
        gate_hi(0)
        copy_krT(0, 0)
        copy_ksT(0)
        exp_dec(0, 0, 0)

        def head(k, first=False, last=False):
            for j in range(B):
                w = j % HALF
                kk, hf = (k, 1) if j < HALF else (k + 1, 0)
                kp, hp = (k, 0) if j < HALF else (k, 1)
                m = 2 * kk + hf
                work = not (last and j >= HALF)
                k1, b1 = (k, j - 1) if j >= 1 else (k - 1, B - 1)
                k2, b2 = (k, j - 2) if j >= 2 else (k - 1, B + j - 2)
                live1, live2 = not (first and j < 1), not (first and j < 2)
                if w == 0:
                    exp_dec(kp, hp, 1)
                copy_q(k, j)
                if w == 0:
                    exp_dec(kp, hp, 2)
                if w == 2 and work:
                    copy_kv(kk, hf, 1)
                if w == 3 and work:
                    copy_krT(kk, hf)
                splits = j == B - 1 and not last
                if splits:
                    split_wq(k + 1, 0)
                if live1:
                    copy_qrT(k1, b1)
                if w == 0:
                    exp_dec(kp, hp, 3)
                if w == 3 and work:
                    gate_hi(m)
                exp_q(k, j)
                if live2:
                    copy_pT(k2, b2)
                if splits:
                    split_wq(k + 1, 1)
                if live1:
                    exp_s(k1, b1)
                if splits:
                    split_wq(k + 1, 2)
                    split_wq(k + 1, 3)
                if w == 2 and work:
                    exp_k(m)
                if w == 3 and work:
                    copy_ksT(m)
                if live2:
                    copy_o(k2, b2)
                if w == 1 and work:
                    copy_kv(kk, hf, 0)
                if w == 2 and work:
                    gates(m)
                if w == 3 and work:
                    exp_dec(kk, hf, 0)
                if j == 3 and not last:
                    split_wkv(k + 1)

        head(0, first=True)
        with act.Fori(1, KVH - 1) as k:
            head(k)
        head(KVH - 1, last=True)
        act.wait_ge(wo_first, 16)
        act.wait_ge(q_ps, B * KVH)
        act.activation(wq_hi[:, :, :], wq_raw[:, :, :], ACT.Copy).then_inc(wo_first_hi, 1)
        copy_qrT(KVH - 1, B - 1)
        copy_pT(KVH - 1, B - 2)
        exp_s(KVH - 1, B - 1)
        copy_o(KVH - 1, B - 2)
        copy_pT(KVH - 1, B - 1)
        copy_o(KVH - 1, B - 1)

    @block.vector
    def _(dve):
        def split_wkv(k):
            dve.wait_ge(wkv_hi_ok, k + 1)
            dve.tensor_tensor(wkv_lo[:, :, :], wkv_raw[:, :, :], wkv_hi[:, :, :].bitcast(F32),
                              ALU.subtract).then_inc(wkv_ok, 1)

        def split_wq(k, c):
            dve.wait_ge(wq_hi_ok, C * k + c + 1)
            dve.tensor_tensor(wq_lo[:, c, :], wq_raw[:, c, :], wq_hi[:, c, :].bitcast(F32),
                              ALU.subtract).then_inc(wq_ok, 1)

        def max_q(k, b):
            n = 8 * k + b
            dve.wait_ge(q_ok, n + 1)
            if some(n - 1):
                dve.wait_ge(qexp_ok, n - 1)
            dve.tensor_reduce(qmx[:, b % 2, :], qs[:, b % 2, :, :], AX.X, ALU.max, negate=True).then_inc(qmax_ok, 1)

        def recip_q(k, b):
            n = 8 * k + b
            dve.wait_ge(qexp_ok, n + 1)
            if some(n - 1):
                dve.wait_ge(qnorm_ok, n - 1)
            dve.reciprocal(qrz[:, b % 2, :], qsm[:, b % 2, :]).then_inc(qrz_ok, 1)

        def decay_q(k, b):
            n = 8 * k + b
            dve.wait_ge(qeT_ps, n + 1)
            if some(n):
                dve.wait_ge(l_ps, n)
            if isinstance(n, int) and n == 0:
                dve.wait_ge(dec_ok, HALF)
            dve.tensor_tensor(qdT[:, :, :, :], TE[:, :, :, :].rearrange("p h i t -> p i h t"),
                              dec[:, b, 0:P].rearrange("p (i t) -> p i t", i=NB).unsqueeze(2)
                              .broadcast_to([P, NB, GRP, BLK]), ALU.mult).then_inc(qdT_ok, 1)

        def mask_s(k, b):
            n = 8 * k + b
            dve.wait_ge(s_ps, n + 1)
            if some(n):
                dve.wait_ge(p_ok, n)
            dve.scalar_tensor_tensor(out=ss[:, :, :], in0=Sp[:, 0:NB * SPAN].rearrange("p (i s) -> p i s", i=NB),
                                     scalar=float(D) ** -0.5, in1=mask_w, op0=ALU.mult,
                                     op1=ALU.add).then_inc(smask_ok, 1)
            dve.wait_ge(smask_ok, n + 1)
            dve.tensor_reduce(smx[:, :], ss[:, :, :], AX.X, ALU.max).then_inc(smax_ok, 1)
            dve.wait_ge(smax_ok, n + 1)
            dve.tensor_tensor(ss[:, :, :], ss[:, :, :], spread(smx[:, :], SPAN), ALU.subtract).then_inc(ssub_ok, 1)

        def linear(k, b):
            n = 8 * k + b
            dve.wait_ge(l_ps, n + 1)
            if some(n - 1):
                dve.wait_ge(pT_ps, n - 1)
            dve.scalar_tensor_tensor(out=pm[:, b % 2, :], in0=Lp[:, 0:LT], scalar=BIG, in1=mask_l, op0=ALU.min,
                                     op1=ALU.mult).then_inc(lin_ok, 1)

        def combine(k, b):
            n = 8 * k + b
            dve.wait_ge(sexp_ok, n + 1)
            dve.tensor_reduce(ssm[:, :], ss[:, :, :], AX.X, ALU.add).then_inc(ssum_ok, 1)
            dve.wait_ge(ssum_ok, n + 1)
            dve.reciprocal(srz[:, :], ssm[:, :]).then_inc(srz_ok, 1)
            dve.wait_ge(srz_ok, n + 1)
            dve.tensor_scalar(srh[:, :], srz[:, :], 0.5, None, ALU.mult).then_inc(srh_ok, 1)
            dve.wait_ge(srh_ok, n + 1)
            dve.wait_ge(lin_ok, n + 1)
            for i in range(NB):
                w = min(LW[i], SPAN)
                seen = pm[:, b % 2, LO[i] + LW[i] - w:LO[i] + LW[i]]
                op = dve.scalar_tensor_tensor(out=seen, in0=ss[:, i, SPAN - w:SPAN], scalar=srh[:, i:i + 1], in1=seen,
                                              op0=ALU.mult, op1=ALU.add)
            op.then_inc(p_ok, 1)

        def softmax_k(m):
            dve.wait_ge(kv_ok, 2 * m + 2)
            dve.tensor_reduce(kmx[:, :], kall[:, :, :], AX.X, ALU.max).then_inc(kmax_ok, 1)
            dve.wait_ge(kmax_ok, m + 1)
            if some(m):
                dve.wait_ge(ksT_ps, m)
            dve.tensor_tensor(ek[:, :, :], kall[:, :, :], spread(kmx[:, :], D), ALU.subtract).then_inc(ksub_ok, 1)

        def sum_k(m):
            dve.wait_ge(kexp_ok, m + 1)
            dve.tensor_reduce(ksm[:, :], ek[:, :, :], AX.X, ALU.add).then_inc(ksum_ok, 1)
            dve.wait_ge(ksum_ok, m + 1)
            if some(m):
                dve.wait_ge(knorm_ok, m)
            dve.reciprocal(krz[:, :], ksm[:, :]).then_inc(krz_ok, 1)

        def gate_k(m):
            dve.wait_ge(gln_ok, m + 1)
            dve.scalar_tensor_tensor(out=gate[:, :, :], in0=kall[:, :, :], scalar=0.0, in1=gate[:, :, :], op0=ALU.min,
                                     op1=ALU.subtract).then_inc(gate_ok, 1)

        def gate_lo(m):
            dve.wait_ge(ghi_ok, m + 1)
            if some(4 * m):
                dve.wait_ge(dec_ps, 4 * m)
            dve.tensor_tensor(g_lo[:, :, :], gate[:, :, :], g_hi[:, :, :].bitcast(F32), ALU.subtract).then_inc(glo_ok, 1)

        def decay_k(m, hf):
            dve.wait_ge(dec_ok, 4 * m + HALF)
            dve.wait_ge(ksT_ok, m + 1)
            for i in range(NB):
                to = dec[:, HALF * hf:HALF * hf + HALF, P + LO[i]:P + LO[i] + LW[i]]
                op = dve.tensor_tensor(to, ksT[:, :, 0:LW[i]], to, ALU.mult)
            op.then_inc(kd_ok, 1)

        dve.memset(krT[:, :, 0:WIN], 0.0).then_inc(pads_ok, 1)
        dve.memset(PTp[:, :], 0.0).then_inc(pads_ok, 1)

        for b in range(B):
            dve.wait_ge(x_in[b], 16)
            dve.bn_stats(stats[:, b, :], x8[:, b, :]).then_inc(stats_ok, 1)
            dve.wait_ge(stats_ok, b + 1)
            dve.bn_aggr(mv[:, b, :], stats[:, b, :]).then_inc(mv_ok, 1)
        dve.wait_ge(mv_ok, B)
        dve.tensor_scalar(veps[:, :], mv[:, :, 1], EPS, None, ALU.add).then_inc(var_ok, 1)
        dve.wait_ge(std_ok, 1)
        dve.tensor_tensor(newt[:, :], rstd[:, :], rstd[:, :], ALU.mult).then_inc(newton_ok, 1)
        dve.wait_ge(newton_ok, 1)
        dve.tensor_tensor(newt[:, :], newt[:, :], veps[:, :], ALU.mult).then_inc(newton_ok, 1)
        dve.wait_ge(newton_ok, 2)
        dve.tensor_scalar(newt[:, :], newt[:, :], -0.5, 1.5, ALU.mult, ALU.add).then_inc(newton_ok, 1)
        dve.wait_ge(newton_ok, 3)
        dve.tensor_tensor(rstd[:, :], rstd[:, :], newt[:, :], ALU.mult).then_inc(newton_ok, 1)
        dve.wait_ge(newton_ok, 4)
        for b in range(B):
            dve.tensor_scalar(x8[:, b, :], x8[:, b, :], mv[:, b, 0:1], rstd[:, b:b + 1], ALU.subtract,
                              ALU.mult).then_inc(h_ok, 1)
        split_wkv(0)
        for c in range(C):
            split_wq(0, c)
        for b in range(B):
            bank = (Kp, Sp)[b % 2]
            cols = slice(b * P, (b + 1) * P)
            dve.wait_ge(hT_ok, b + 1)
            dve.tensor_tensor(hT_lo[:, :, cols], bank[:, :].rearrange("p (c t) -> p c t", c=C),
                              hT_hi[:, :, cols].bitcast(F32), ALU.subtract).then_inc(hT_lo_ok, 1)
        softmax_k(0)
        sum_k(0)
        gate_k(0)
        gate_lo(0)

        def head(k, first=False, last=False):
            for j in range(B):
                w = j % HALF
                kk, hf = (k, 1) if j < HALF else (k + 1, 0)
                m = 2 * kk + hf
                work = not (last and j >= HALF)
                k1, b1 = (k, j - 1) if j >= 1 else (k - 1, B - 1)
                live1 = not (first and j < 1)
                if live1:
                    decay_q(k1, b1)
                max_q(k, j)
                splits = j == B - 1 and not last
                if w == 3 and work:
                    gate_lo(m)
                if splits:
                    split_wq(k + 1, 0)
                if live1:
                    mask_s(k1, b1)
                if splits:
                    split_wq(k + 1, 1)
                if w == 2 and work:
                    softmax_k(m)
                if w == 0:
                    decay_k(m - 1, 1 - hf)
                recip_q(k, j)
                if w == 2 and work:
                    sum_k(m)
                if live1:
                    linear(k1, b1)
                if splits:
                    split_wq(k + 1, 2)
                if live1:
                    combine(k1, b1)
                if splits:
                    split_wq(k + 1, 3)
                if w == 2 and work:
                    gate_k(m)
                if j == 3 and not last:
                    split_wkv(k + 1)

        head(0, first=True)
        with dve.Fori(1, KVH - 1) as k:
            head(k)
        head(KVH - 1, last=True)
        decay_q(KVH - 1, B - 1)
        mask_s(KVH - 1, B - 1)
        linear(KVH - 1, B - 1)
        combine(KVH - 1, B - 1)
        dve.wait_ge(wo_first_hi, 1)
        dve.tensor_tensor(wq_lo[:, :, :], wq_raw[:, :, :], wq_hi[:, :, :].bitcast(F32), ALU.subtract)

    @block.gpsimd
    def _(pool):
        def swapped_sin(src, to, n):
            for a in range(2):
                half, other = slice(a * (D // 2), (a + 1) * (D // 2)), slice((1 - a) * (D // 2), (2 - a) * (D // 2))
                sin = cst[:, K_SIN + a * (D // 2):K_SIN + (a + 1) * (D // 2)].unsqueeze(1).broadcast_to([P, n, D // 2])
                op = pool.tensor_tensor(to[:, :, half], src[:, :, other], sin, ALU.mult)
            return op

        def rotate_q(k, b):
            n = 8 * k + b
            pool.wait_ge(q_ok, n + 1)
            if some(n - 1):
                pool.wait_ge(qrT_ps, n - 1)
            pool.tensor_tensor(qr[:, b % 2, :, :], qs[:, b % 2, :, :], table(K_COS, GRP), ALU.mult).then_inc(qrope_a, 1)
            if some(n):
                pool.wait_ge(qrope_ok, n)
            swapped_sin(qs[:, b % 2, :, :], qr2, GRP).then_inc(qrope_b, 1)
            pool.wait_ge(qrope_a, n + 1)
            pool.wait_ge(qrope_b, n + 1)
            pool.tensor_tensor(qr[:, b % 2, :, :], qr[:, b % 2, :, :], qr2[:, :, :], ALU.add).then_inc(qrope_ok, 1)

        def normalise_q(k, b):
            pool.wait_ge(qrz_ok, 8 * k + b + 1)
            pool.tensor_tensor(eq[:, b % 2, :, :], eq[:, b % 2, :, :], spread(qrz[:, b % 2, :], D),
                               ALU.mult).then_inc(qnorm_ok, 1)

        def rotate_k(m):
            pool.wait_ge(kall_ok, 2 * m + 2)
            if some(m):
                pool.wait_ge(krT_ps, m)
            pool.tensor_tensor(kr[:, :, :], kall[:, :, :], table(K_COS, HALF), ALU.mult).then_inc(krope_a, 1)
            if some(m):
                pool.wait_ge(krope_ok, m)
            swapped_sin(kall, kr2, HALF).then_inc(krope_b, 1)
            pool.wait_ge(krope_a, m + 1)
            pool.wait_ge(krope_b, m + 1)
            pool.tensor_tensor(kr[:, :, :], kr[:, :, :], kr2[:, :, :], ALU.add).then_inc(krope_ok, 1)

        def normalise_k(m):
            pool.wait_ge(krz_ok, m + 1)
            pool.tensor_tensor(ek[:, :, :], ek[:, :, :], spread(krz[:, :], D), ALU.mult).then_inc(knorm_ok, 1)

        pool.wait_ge(consts_in, 16)
        rotate_k(0)
        normalise_k(0)

        def head(k, last=False):
            for j in range(B):
                m = 2 * k + (1 if j < HALF else 2)
                work = j % HALF == 2 and not (last and j >= HALF)
                rotate_q(k, j)
                if work:
                    rotate_k(m)
                normalise_q(k, j)
                if work:
                    normalise_k(m)

        head(0)
        with pool.Fori(1, KVH - 1) as k:
            head(k)
        head(KVH - 1, last=True)

XH, XK = 16, 32
XD = P // XH
XJ = XH * XK // P
NT = HID // P
E_NUM, RANK, TOP_K, RDIM = 64, 8, 16, 16
SCALING = 2.0

R_ID, R_HM, R_WQ, R_WK, R_WV, R_WM, R_B = 0, P, P + XH, 2 * P + XH, 3 * P + XH, 4 * P + XH, 5 * P + XH
R_ALL = R_B + 4


def head_mask():
    return (np.arange(P)[:, None] % XH == np.arange(XH)[None, :]).astype(np.float32)


def rest(nc, x, small, ctxT, proj, keysT, wrT, Wo, AT, BT, out, oT, w_raw, w_hi, w_lo, semctx, ctx):
    sb = lambda n, s, d=F32: ctx.enter_context(nc.sbuf_tensor(n, s, d))
    ps = lambda n, s, d=F32: ctx.enter_context(nc.psum_tensor(n, s, d))
    sem = lambda n: semctx.enter_context(nc.semaphore(n))

    cs = sb("cs", [P, R_ALL])
    ident = cs[:, R_ID:R_ID + P]
    wqT, wkT, wvT, wmT = (cs[:, o:o + P] for o in (R_WQ, R_WK, R_WV, R_WM))
    bq, bk, bv, bm = (cs[:, R_B + i:R_B + i + 1] for i in range(4))
    hmask = cs[:, R_HM:R_HM + XH]
    xs = sb("xs", [P, B, HID])
    wo_raw = [w_raw, sb("wo_raw1", [P, HC, HID])]
    wo_hi = [w_hi, sb("wo_hi1", [P, HC, HID], F32R)]
    wo_lo = [w_lo, sb("wo_lo1", [P, HC, HID], F32R)]
    oF = sb("oF", [P, 2, HC, P], F32R)
    ctx_sb = sb("ctx_sb", [P, NT, B, P])
    proj_sb = sb("proj_sb", [P, NT, 2 * XK])
    ones = sb("ones", [P, P])
    cp = sb("cp", [P, 2, B, XK])
    kvb = sb("kvb", [P, 2, XK])
    kvx = sb("kvx", [P, 2, B, XK])
    hms = sb("hms", [P, XH])
    kbd = sb("kbd", [P, 2, XH, XK])
    vbd = sb("vbd", [P, XH, XK])
    vbT = sb("vbT", [P, 2, XJ, P])
    aT = sb("aT", [P, C, HID])
    bT = sb("bT", [P, C, HID])
    wr = sb("wr", [P, C, RDIM])
    keys = sb("keys", [RDIM, E_NUM])
    st2 = sb("st2", [P, B, 6])
    mv2 = sb("mv2", [P, B, 2])
    ve2 = sb("ve2", [P, B])
    ln2 = sb("ln2", [P, B])
    y2 = sb("y2", [P, B])
    nt2 = sb("nt2", [P, B])
    rs2 = sb("rs2", [P, B])
    st3 = sb("st3", [P, 6])
    mv3 = sb("mv3", [P, 2])
    ve3 = sb("ve3", [P, 1])
    ln3 = sb("ln3", [P, 1])
    y3 = sb("y3", [P, 1])
    nta3 = sb("nta3", [P, 1])
    ntb3 = sb("ntb3", [P, 1])
    rs3 = sb("rs3", [P, 1])
    xmx = sb("xmx", [P, 2, XH])
    xsm = sb("xsm", [P, 2, XH])
    xrz = sb("xrz", [P, 2, XH])
    top = sb("top", [P, 8])
    top2 = sb("top2", [P, 8])
    ntop = sb("ntop", [P, 1])
    gsum = sb("gsum", [P, 1])
    grz = sb("grz", [P, 1])
    sc = sb("sc", [P, E_NUM])
    sc1 = sb("sc1", [P, E_NUM])
    sc2 = sb("sc2", [P, E_NUM])
    esc = sb("esc", [P, E_NUM])
    gt = sb("gt", [P, E_NUM])
    q16 = sb("q16", [RDIM, P])

    late = oT[:, 0:H - HC, :].rearrange("p h t -> p (h t)").bitcast(F32)
    taken = [0]

    def view(shape):
        n = int(np.prod(shape))
        at = taken[0]
        taken[0] += n
        assert taken[0] <= (H - HC) * B * P // 2
        letters = "abcd"[:len(shape)]
        return late[:, at:at + n].rearrange(f"p ({' '.join(letters)}) -> p {' '.join(letters)}",
                                            **{l: m for l, m in zip(letters[1:], shape[1:])})

    h2 = view([2, HID])
    qx = view([2, HID])
    ex = view([3, XH, XK])
    pxT = view([2, XJ, HID])
    xo = view([HID])
    h3 = view([HID])
    h3T = view([C, P])
    zg = view([HID])
    zgT = view([C, P])
    fin = view([2, HID])

    bank = [ps(f"bank{i}", [P, HID]) for i in range(8)]
    b_query, b_mix, b_route, b_z = bank[0], bank[5], bank[6], bank[7]
    b_scores, b_turned = (bank[1], bank[2]), (bank[3], bank[4])

    small_in = sem("small_in")
    ctx_in = sem("ctx_in")
    x2_in = sem("x2_in")
    ffn_in = sem("ffn_in")
    ones_ok = sem("ones_ok")
    cp_ps = sem("cp_ps")
    cp_ok = sem("cp_ok")
    sum_ps = sem("sum_ps")
    kvb_ok = sem("kvb_ok")
    kvx_ps = sem("kvx_ps")
    kvx_ok = sem("kvx_ok")
    hms_ok = sem("hms_ok")
    kbd_ok = sem("kbd_ok")
    vbd_ok = sem("vbd_ok")
    vbT_ps = sem("vbT_ps")
    vbT_ok = sem("vbT_ok")
    wo_hi_ok = sem("wo_hi_ok")
    wo_ok = sem("wo_ok")
    of_ok = sem("of_ok")
    w_ps = sem("w_ps")
    x1_ok = sem("x1_ok")
    st2_ok = sem("st2_ok")
    mv2_ok = sem("mv2_ok")
    ve2_ok = sem("ve2_ok")
    ln2_ok = sem("ln2_ok")
    y2_ok = sem("y2_ok")
    newton2 = sem("newton2")
    rs2_ok = sem("rs2_ok")
    h2_ok = sem("h2_ok")
    qx_ps = sem("qx_ps")
    qx_ok = sem("qx_ok")
    xs_ps = sem("xs_ps")
    xmax_ok = sem("xmax_ok")
    xsub_ok = sem("xsub_ok")
    xexp_ok = sem("xexp_ok")
    xsum_ok = sem("xsum_ok")
    xrz_ok = sem("xrz_ok")
    xn_ok = sem("xn_ok")
    xt_ps = sem("xt_ps")
    xt_ok = sem("xt_ok")
    xv_ps = sem("xv_ps")
    xo_ok = sem("xo_ok")
    wm_ps = sem("wm_ps")
    x2_ok = sem("x2_ok")
    moments3 = sem("moments3")
    ve3_ok = sem("ve3_ok")
    ln3_ok = sem("ln3_ok")
    y3_ok = sem("y3_ok")
    newton3 = sem("newton3")
    h3_ok = sem("h3_ok")
    h3T_ps = sem("h3T_ps")
    h3T_ok = sem("h3T_ok")
    rq_ps = sem("rq_ps")
    rq_ok = sem("rq_ok")
    rs_ps = sem("rs_ps")
    sc_ok = sem("sc_ok")
    marks = sem("marks")
    nt_ok = sem("nt_ok")
    es_ok = sem("es_ok")
    gate_steps = sem("gate_steps")
    z_ps = sem("z_ps")
    zg_ok = sem("zg_ok")
    zT_ps = sem("zT_ps")
    zT_ok = sem("zT_ok")
    f_ps = sem("f_ps")
    fin_ok = sem("fin_ok")

    stored = [sem("stored0"), sem("stored1")]
    wo_in = [sem("wo_in0"), sem("wo_in1")]

    wo_v = Wo.rearrange("(c h p) n -> c p h n", p=P, h=HC)

    def spread(ap, n):
        return ap.unsqueeze(2).broadcast_to([ap.shape[0], ap.shape[1], n])

    block = ctx.enter_context(nc.Block())

    @block.sync
    def _(sp):
        def weights(c, u):
            if some(c - 2):
                sp.wait_ge(wo_ok, HC * (c - 2))
            sp.dma_start(wo_raw[u][:, :, :], wo_v[c]).then_inc(wo_in[u], 16)

        weights(1, 1)
        sp.dma_start(xs[:, :, :], x.rearrange("b t d -> t b d")).then_inc(x2_in, 16)
        weights(2, 0)
        sp.dma_start(cs[:, :], small).then_inc(small_in, 16)
        sp.dma_start(proj_sb[:, :, :], proj.rearrange("(c p) k -> p c k", p=P)).then_inc(ctx_in, 16)
        for c in range(NT):
            sp.dma_start(ctx_sb[:, c, :, :], ctxT[:, c * P:(c + 1) * P, :].rearrange("b p d -> p b d")).then_inc(ctx_in, 16)
        weights(3, 1)
        sp.dma_start(aT[:, :, :], AT.rearrange("(c p) n -> p c n", p=P)).then_inc(ffn_in, 16)
        sp.dma_start(bT[:, :, :], BT.rearrange("(c p) n -> p c n", p=P)).then_inc(ffn_in, 16)
        sp.dma_start(wr[:, :, :], wrT.rearrange("(c p) n -> p c n", p=P)).then_inc(ffn_in, 16)
        sp.dma_start(keys[:, :], keysT).then_inc(ffn_in, 16)
        with sp.Fori(2, NCH // 2) as p:
            weights(2 * p, 0)
            weights(2 * p + 1, 1)
        for b in range(B):
            sp.wait_ge(fin_ok, b + 1)
            sp.dma_start(out[b], fin[:, b % 2, :]).then_inc(stored[b % 2], 16)
        for done in stored:
            sp.wait_ge(done, 16 * B // 2)

    @block.tensor
    def _(pe):
        def chunk_product(c, u, b, first=False):
            pe.wait_ge(of_ok, 8 * c + b + 1)
            for h in range(HC):
                pe.matmul(bank[b][:, :], oF[:, b % 2, h, :], wo_hi[u][:, h, :], start=first and h == 0, stop=False,
                          skip_group_check=True)
                mm = pe.matmul(bank[b][:, :], oF[:, b % 2, h, :], wo_lo[u][:, h, :], start=False,
                               stop=(h == HC - 1), skip_group_check=True)
            mm.then_inc(w_ps, 1)

        def project_context():
            pe.wait_ge(ctx_in, 16 * (NT + 1))
            pe.wait_ge(x1_ok, 1)
            for b in range(B):
                for c in range(NT):
                    mm = pe.matmul(bank[0][:, b * 2 * XK:(b + 1) * 2 * XK], ctx_sb[:, c, b, :], proj_sb[:, c, :],
                                   start=(c == 0), stop=(c == NT - 1))
            mm.then_inc(cp_ps, 1)
            pe.wait_ge(ones_ok, 1)
            pe.wait_ge(x1_ok, 2)
            for c in range(NT):
                mm = pe.matmul(bank[1][:, 0:2 * XK], ones[:, :], proj_sb[:, c, :], start=(c == 0), stop=(c == NT - 1))
            mm.then_inc(sum_ps, 1)

        def keys_values():
            pe.wait_ge(small_in, 16)
            pe.wait_ge(cp_ok, 1)
            pe.wait_ge(x1_ok, 3)
            pe.matmul(bank[2][:, 0:B * XK], wkT, cp[:, 0, :, :].rearrange("p b k -> p (b k)"), start=True, stop=True)
            pe.matmul(bank[2][:, B * XK:2 * B * XK], wvT, cp[:, 1, :, :].rearrange("p b k -> p (b k)"),
                      start=True, stop=True).then_inc(kvx_ps, 1)

        for b in range(B):
            chunk_product(0, 0, b, first=True)
        with pe.Fori(0, NCH // 2 - 1) as p:
            pe.wait_ge(wo_ok, HC * (2 * p + 1))
            for b in range(B):
                chunk_product(2 * p + 1, 1, b)
            pe.wait_ge(wo_ok, HC * (2 * p + 2))
            for b in range(B):
                chunk_product(2 * p + 2, 0, b)
        pe.wait_ge(wo_ok, HC * (NCH - 1))
        for b in range(B):
            chunk_product(NCH - 1, 1, b)
            if b == 4:
                project_context()
            if b == 5:
                keys_values()

        def query(b):
            pe.wait_ge(h2_ok, b + 1)
            if b >= 2:
                pe.wait_ge(vbT_ok, b - 1)
            else:
                if b == 1:
                    pe.wait_ge(qx_ok, 1)
            pe.matmul(b_query[:, :], wqT, h2[:, b % 2, :], start=True, stop=True).then_inc(qx_ps, 1)

        def xscores(b, i):
            t = NT * b + i
            pe.wait_ge(qx_ok, b + 1)
            pe.wait_ge(kbd_ok, b + 1)
            if t < 2:
                pe.wait_ge(kvx_ok, 2)
            if some(t - 1):
                pe.wait_ge(xsub_ok, t - 1)
            pe.matmul(b_scores[t % 2][:, :], qx[:, b % 2, i * P:(i + 1) * P],
                      kbd[:, b % 2, :, :].rearrange("p h k -> p (h k)"), start=True, stop=True).then_inc(xs_ps, 1)

        def xtranspose(t):
            pe.wait_ge(xn_ok, t + 1)
            if t == 0:
                pe.wait_ge(x1_ok, B)
            if some(t - 1):
                pe.wait_ge(xt_ok, t - 1)
            for j in range(XJ):
                mm = pe.transpose(b_turned[t % 2][:, j * P:(j + 1) * P],
                                  ex[:, t % 3, :, :].rearrange("p h k -> p (h k)")[:, j * P:(j + 1) * P], ident)
            mm.then_inc(xt_ps, 1)

        def vtranspose(b):
            pe.wait_ge(vbd_ok, b + 1)
            pe.wait_ge(qx_ok, min(b + 2, B))
            for j in range(XJ):
                mm = pe.transpose(b_query[:, j * P:(j + 1) * P],
                                  vbd[:, :, :].rearrange("p h k -> p (h k)")[:, j * P:(j + 1) * P], ident)
            mm.then_inc(vbT_ps, 1)

        def xmix(b):
            pe.wait_ge(xt_ok, NT * b + NT)
            pe.wait_ge(vbT_ok, b + 1)
            if some(b):
                pe.wait_ge(x2_ok, b)
            for j in range(XJ):
                mm = pe.matmul(b_mix[:, :], vbT[:, b % 2, j, :], pxT[:, b % 2, j, :], start=(j == 0), stop=(j == XJ - 1))
            mm.then_inc(xv_ps, 1)

        def xout(b):
            pe.wait_ge(xo_ok, b + 1)
            pe.matmul(b_mix[:, :], wmT, xo[:, :], start=True, stop=True).then_inc(wm_ps, 1)

        def tokens(b):
            pe.wait_ge(h3_ok, b + 1)
            if some(b):
                pe.wait_ge(sc_ok, b)
            for c in range(C):
                mm = pe.transpose(b_route[:, c * P:(c + 1) * P], h3[:, c * P:(c + 1) * P], ident)
            mm.then_inc(h3T_ps, 1)

        def router_query(b):
            if b == 0:
                pe.wait_ge(ffn_in, 64)
            pe.wait_ge(h3T_ok, b + 1)
            for c in range(C):
                mm = pe.matmul(b_route[0:RDIM, 0:P], wr[:, c, :], h3T[:, c, :], start=(c == 0), stop=(c == C - 1))
            mm.then_inc(rq_ps, 1)

        def router_scores(b):
            pe.wait_ge(rq_ok, b + 1)
            pe.matmul(b_route[:, P:P + E_NUM], q16[:, :], keys[:, :], start=True, stop=True).then_inc(rs_ps, 1)

        def down(b):
            if some(b):
                pe.wait_ge(fin_ok, b)
            for c in range(C):
                mm = pe.matmul(b_z[:, :], h3T[:, c, :], aT[:, c, :], start=(c == 0), stop=(c == C - 1))
            mm.then_inc(z_ps, 1)

        def turn(b):
            pe.wait_ge(zg_ok, b + 1)
            for c in range(C):
                mm = pe.transpose(b_z[:, c * P:(c + 1) * P], zg[:, c * P:(c + 1) * P], ident)
            mm.then_inc(zT_ps, 1)

        def up(b):
            pe.wait_ge(zT_ok, b + 1)
            for c in range(C):
                mm = pe.matmul(b_z[:, :], zgT[:, c, :], bT[:, c, :], start=(c == 0), stop=(c == C - 1))
            mm.then_inc(f_ps, 1)

        query(0)
        for s in range(B + 3):
            fa, fb = s - 2, s - 3
            attends, mixes, routes, leaves = s < B, 1 <= s <= B, 0 <= fa < B, 0 <= fb
            if attends:
                xscores(s, 0)
            if leaves:
                turn(fb)
            if s + 1 < B:
                query(s + 1)
            if leaves:
                up(fb)
            if mixes:
                xtranspose(NT * s - 2)
            if attends:
                xscores(s, 1)
            if routes:
                tokens(fa)
            if mixes:
                xtranspose(NT * s - 1)
            if attends:
                vtranspose(s)
                xscores(s, 2)
            if routes:
                router_query(fa)
            if mixes:
                xmix(s - 1)
            if routes:
                router_scores(fa)
            if attends:
                xtranspose(NT * s)
                xscores(s, 3)
            if routes:
                down(fa)
            if mixes:
                xout(s - 1)
            if attends:
                xtranspose(NT * s + 1)

    @block.scalar
    def _(act):
        act.preload_act_table_set("natural_log_exp_and_others")

        def split(c, u, count):
            act.wait_ge(wo_in[u], count)
            if some(8 * (c - 1)):
                act.wait_ge(w_ps, 8 * (c - 1))
            act.activation(wo_hi[u][:, :, :], wo_raw[u][:, :, :], ACT.Copy).then_inc(wo_hi_ok, 1)

        def rsqrt2(g):
            of = slice(g * HALF, (g + 1) * HALF)
            act.wait_ge(ve2_ok, g + 1)
            act.activation(ln2[:, of], ve2[:, of], ACT.Ln).then_inc(ln2_ok, 1)
            act.wait_ge(ln2_ok, g + 1)
            act.activation(y2[:, of], ln2[:, of], ACT.Exp, scale=-0.5).then_inc(y2_ok, 1)

        def rsqrt3(b):
            act.wait_ge(ve3_ok, b + 1)
            act.activation(ln3[:, :], ve3[:, :], ACT.Ln).then_inc(ln3_ok, 1)
            act.wait_ge(ln3_ok, b + 1)
            act.activation(y3[:, :], ln3[:, :], ACT.Exp, scale=-0.5).then_inc(y3_ok, 1)

        def copy_query(b):
            act.wait_ge(qx_ps, b + 1)
            if some(NT * (b - 1)):
                act.wait_ge(xs_ps, NT * (b - 1))
            act.activation(qx[:, b % 2, :], b_query[:, :], ACT.Identity, bias=bq).then_inc(qx_ok, 1)

        def xexp(t):
            act.wait_ge(xsub_ok, t + 1)
            act.activation(ex[:, t % 3, :, :], ex[:, t % 3, :, :], ACT.Exp).then_inc(xexp_ok, 1)

        def copy_xt(b, i):
            t = NT * b + i
            act.wait_ge(xt_ps, t + 1)
            if some(b - 1):
                act.wait_ge(xv_ps, b - 1)
            act.activation(pxT[:, b % 2, :, i * P:(i + 1) * P], b_turned[t % 2][:, :].rearrange("p (j n) -> p j n", j=XJ),
                           ACT.Copy).then_inc(xt_ok, 1)

        def copy_vT(b):
            act.wait_ge(vbT_ps, b + 1)
            if some(b - 1):
                act.wait_ge(xv_ps, b - 1)
            act.activation(vbT[:, b % 2, :, :], b_query[:, :].rearrange("p (j c) -> p j c", j=XJ),
                           ACT.Copy).then_inc(vbT_ok, 1)

        def copy_mix(b):
            act.wait_ge(xv_ps, b + 1)
            if some(b):
                act.wait_ge(wm_ps, b)
            act.activation(xo[:, :], b_mix[:, :], ACT.Copy).then_inc(xo_ok, 1)

        def copy_h3T(b):
            act.wait_ge(h3T_ps, b + 1)
            if some(b):
                act.wait_ge(z_ps, b)
            act.activation(h3T[:, :, :], b_route[:, :].rearrange("p (c t) -> p c t", c=C), ACT.Copy).then_inc(h3T_ok, 1)

        def copy_router_query(b):
            act.wait_ge(rq_ps, b + 1)
            act.activation(q16[:, :], b_route[0:RDIM, 0:P], ACT.Copy).then_inc(rq_ok, 1)

        def copy_router_scores(b):
            act.wait_ge(rs_ps, b + 1)
            if some(b):
                act.wait_ge(marks, 5 * b - 3)
            act.activation(sc[:, :], b_route[:, P:P + E_NUM], ACT.Copy).then_inc(sc_ok, 1)

        def exp_router(b):
            act.wait_ge(nt_ok, b + 1)
            if some(b):
                act.wait_ge(gate_steps, 4 * b - 3)
            act.activation(esc[:, :], sc[:, :], ACT.Exp, bias=ntop[:, 0:1]).then_inc(es_ok, 1)

        def copy_zT(b):
            act.wait_ge(zT_ps, b + 1)
            if some(b):
                act.wait_ge(f_ps, b)
            act.activation(zgT[:, :, :], b_z[:, :].rearrange("p (c t) -> p c t", c=C), ACT.Copy).then_inc(zT_ok, 1)

        split(1, 1, 16)
        split(2, 0, 16)
        with act.Fori(1, NCH // 2 - 1) as p:
            split(2 * p + 1, 1, 16 * p + 16)
            split(2 * p + 2, 0, 16 * p + 16)
        split(NCH - 1, 1, 16 * (NCH // 2))
        act.wait_ge(cp_ps, 1)
        act.activation(cp[:, :, :, :], bank[0][:, :].rearrange("p (b a k) -> p a b k", b=B, a=2), ACT.Copy).then_inc(cp_ok, 1)
        rsqrt2(0)
        copy_query(0)
        for s in range(B + 3):
            fa, fb = s - 2, s - 3
            attends, mixes, routes, leaves = s < B, 1 <= s <= B, 0 <= fa < B, 0 <= fb
            if leaves:
                copy_zT(fb)
            if routes:
                rsqrt3(fa)
            if attends:
                xexp(NT * s)
            if s + 1 < B:
                copy_query(s + 1)
            if mixes:
                copy_xt(s - 1, 2)
            if s == 0:
                rsqrt2(1)
            if routes:
                copy_h3T(fa)
            if attends:
                xexp(NT * s + 1)
            if mixes:
                copy_xt(s - 1, 3)
            if attends:
                copy_vT(s)
                xexp(NT * s + 2)
            if routes:
                copy_router_query(fa)
            if mixes:
                copy_mix(s - 1)
            if routes:
                copy_router_scores(fa)
            if attends:
                copy_xt(s, 0)
                xexp(NT * s + 3)
            if routes:
                exp_router(fa)
            if attends:
                copy_xt(s, 1)

    @block.vector
    def _(dve):
        def split(c, u, h):
            dve.wait_ge(wo_hi_ok, c)
            dve.tensor_tensor(wo_lo[u][:, h, :], wo_raw[u][:, h, :], wo_hi[u][:, h, :].bitcast(F32),
                              ALU.subtract).then_inc(wo_ok, 1)

        def widen(c, b):
            n = 8 * c + b
            if some(n - 1):
                dve.wait_ge(w_ps, n - 1)
            dve.tensor_scalar(oF[:, b % 2, :, :], oT[:, bass.ds(HC * c, HC), b * P:(b + 1) * P], 1.0, None,
                              ALU.mult).then_inc(of_ok, 1)

        def first_residual(b):
            dve.wait_ge(w_ps, 8 * (NCH - 1) + b + 1)
            dve.tensor_tensor(xs[:, b, :], bank[b][:, :], xs[:, b, :], ALU.add).then_inc(x1_ok, 1)
            dve.wait_ge(x1_ok, b + 1)
            dve.bn_stats(st2[:, b, :], xs[:, b, :]).then_inc(st2_ok, 1)
            dve.wait_ge(st2_ok, b + 1)
            dve.bn_aggr(mv2[:, b, :], st2[:, b, :]).then_inc(mv2_ok, 1)

        def variance(g):
            of = slice(g * HALF, (g + 1) * HALF)
            dve.wait_ge(mv2_ok, HALF * g + HALF)
            dve.tensor_scalar(ve2[:, of], mv2[:, of, 1], EPS, None, ALU.add).then_inc(ve2_ok, 1)

        def newton(g):
            of = slice(g * HALF, (g + 1) * HALF)
            dve.wait_ge(y2_ok, g + 1)
            dve.tensor_tensor(nt2[:, of], y2[:, of], y2[:, of], ALU.mult).then_inc(newton2, 1)
            dve.wait_ge(newton2, 3 * g + 1)
            dve.tensor_tensor(nt2[:, of], nt2[:, of], ve2[:, of], ALU.mult).then_inc(newton2, 1)
            dve.wait_ge(newton2, 3 * g + 2)
            dve.tensor_scalar(nt2[:, of], nt2[:, of], -0.5, 1.5, ALU.mult, ALU.add).then_inc(newton2, 1)
            dve.wait_ge(newton2, 3 * g + 3)
            dve.tensor_tensor(rs2[:, of], y2[:, of], nt2[:, of], ALU.mult).then_inc(rs2_ok, 1)

        def normalise2(b):
            dve.wait_ge(rs2_ok, b // HALF + 1)
            if some(b - 1):
                dve.wait_ge(qx_ps, b - 1)
            dve.tensor_scalar(h2[:, b % 2, :], xs[:, b, :], mv2[:, b, 0:1], rs2[:, b:b + 1], ALU.subtract,
                              ALU.mult).then_inc(h2_ok, 1)

        def context_bias():
            dve.wait_ge(sum_ps, 1)
            dve.tensor_scalar(kvb[:, 0, :], bank[1][:, 0:XK], bk, None, ALU.mult).then_inc(kvb_ok, 1)
            dve.tensor_scalar(kvb[:, 1, :], bank[1][:, XK:2 * XK], bv, None, ALU.mult).then_inc(kvb_ok, 1)

        def context_keys():
            dve.wait_ge(kvb_ok, 2)
            dve.wait_ge(kvx_ps, 1)
            for a in range(2):
                dve.tensor_tensor(kvx[:, a, :, :],
                                  bank[2][:, a * B * XK:(a + 1) * B * XK].rearrange("p (b k) -> p b k", b=B),
                                  kvb[:, a, :].unsqueeze(1).broadcast_to([P, B, XK]), ALU.add).then_inc(kvx_ok, 1)

        dve.memset(ones[:, :], 1.0).then_inc(ones_ok, 1)
        for b in range(B):
            widen(0, b)
            if b >= HC:
                split(1, 1, b - HC)
        with dve.Fori(0, NCH // 2 - 1) as p:
            for b in range(B):
                widen(2 * p + 1, b)
                if b >= HC:
                    split(2 * p + 2, 0, b - HC)
            for b in range(B):
                widen(2 * p + 2, b)
                if b >= HC:
                    split(2 * p + 3, 1, b - HC)
        dve.wait_ge(small_in, 16)
        dve.tensor_scalar(hms[:, :], hmask, float(XD) ** -0.5, None, ALU.mult).then_inc(hms_ok, 1)
        dve.wait_ge(x2_in, 16)
        for b in range(B + 2):
            if b < B:
                widen(NCH - 1, b)
            if b >= 2:
                first_residual(b - 2)
            if b == HALF + 1:
                variance(0)
            if b == B - 1:
                context_bias()
                newton(0)
                normalise2(0)
            if b == B:
                context_keys()
        normalise2(1)
        variance(1)

        def xmax(t):
            dve.wait_ge(xs_ps, t + 1)
            dve.tensor_reduce(xmx[:, t % 2, :], b_scores[t % 2][:, :].rearrange("p (h k) -> p h k", h=XH), AX.X,
                              ALU.max).then_inc(xmax_ok, 1)
            dve.wait_ge(xmax_ok, t + 1)
            if some(t - 2):
                dve.wait_ge(xt_ps, t - 2)
            dve.tensor_tensor(ex[:, t % 3, :, :], b_scores[t % 2][:, :].rearrange("p (h k) -> p h k", h=XH),
                              spread(xmx[:, t % 2, :], XK), ALU.subtract).then_inc(xsub_ok, 1)

        def xsum(t):
            dve.wait_ge(xexp_ok, t + 1)
            dve.tensor_reduce(xsm[:, t % 2, :], ex[:, t % 3, :, :], AX.X, ALU.add).then_inc(xsum_ok, 1)
            dve.wait_ge(xsum_ok, t + 1)
            if some(t - 1):
                dve.wait_ge(xn_ok, t - 1)
            dve.reciprocal(xrz[:, t % 2, :], xsm[:, t % 2, :]).then_inc(xrz_ok, 1)

        def second_residual(b):
            dve.wait_ge(wm_ps, b + 1)
            dve.scalar_tensor_tensor(out=xs[:, b, :], in0=b_mix[:, :], scalar=bm, in1=xs[:, b, :], op0=ALU.add,
                                     op1=ALU.add).then_inc(x2_ok, 1)

        def stats3(b):
            dve.wait_ge(x2_ok, b + 1)
            dve.bn_stats(st3[:, :], xs[:, b, :]).then_inc(moments3, 1)
            dve.wait_ge(moments3, 2 * b + 1)
            dve.bn_aggr(mv3[:, :], st3[:, :]).then_inc(moments3, 1)
            dve.wait_ge(moments3, 2 * b + 2)
            dve.tensor_scalar(ve3[:, :], mv3[:, 1:2], EPS, None, ALU.add).then_inc(ve3_ok, 1)

        def normalise3(b):
            dve.wait_ge(y3_ok, b + 1)
            dve.scalar_tensor_tensor(out=nta3[:, :], in0=y3[:, :], scalar=ve3[:, 0:1], in1=y3[:, :], op0=ALU.mult,
                                     op1=ALU.mult).then_inc(newton3, 1)
            dve.wait_ge(newton3, 3 * b + 1)
            dve.tensor_scalar(ntb3[:, :], nta3[:, :], -0.5, 1.5, ALU.mult, ALU.add).then_inc(newton3, 1)
            dve.wait_ge(newton3, 3 * b + 2)
            dve.tensor_tensor(rs3[:, :], y3[:, :], ntb3[:, :], ALU.mult).then_inc(newton3, 1)
            dve.wait_ge(newton3, 3 * b + 3)
            if some(b):
                dve.wait_ge(h3T_ps, b)
            dve.tensor_scalar(h3[:, :], xs[:, b, :], mv3[:, 0:1], rs3[:, 0:1], ALU.subtract, ALU.mult).then_inc(h3_ok, 1)

        def choose_mark(b):
            dve.wait_ge(sc_ok, b + 1)
            dve.max(top[:, :], sc[:, :]).then_inc(marks, 1)
            dve.wait_ge(marks, 5 * b + 1)
            dve.match_replace(out=sc1[:, :], in_to_replace=top[:, :], in_values=sc[:, :], imm_value=-3e38).then_inc(marks, 1)
            dve.tensor_scalar(ntop[:, :], top[:, 0:1], -1.0, None, ALU.mult).then_inc(nt_ok, 1)
            dve.wait_ge(marks, 5 * b + 2)
            dve.max(top2[:, :], sc1[:, :]).then_inc(marks, 1)
            dve.wait_ge(marks, 5 * b + 3)
            dve.match_replace(out=sc2[:, :], in_to_replace=top2[:, :], in_values=sc1[:, :],
                              imm_value=-3e38).then_inc(marks, 1)
            dve.wait_ge(marks, 5 * b + 4)
            dve.tensor_scalar(sc2[:, :], sc2[:, :], -2e38, None, ALU.is_lt).then_inc(marks, 1)

        def choose_gate(b):
            dve.wait_ge(marks, 5 * b + 5)
            dve.wait_ge(es_ok, b + 1)
            dve.tensor_tensor(gt[:, :], esc[:, :], sc2[:, :], ALU.mult).then_inc(gate_steps, 1)
            dve.wait_ge(gate_steps, 4 * b + 1)
            dve.tensor_reduce(gsum[:, :], gt[:, :], AX.X, ALU.add).then_inc(gate_steps, 1)
            dve.wait_ge(gate_steps, 4 * b + 2)
            dve.reciprocal(grz[:, :], gsum[:, :]).then_inc(gate_steps, 1)
            dve.wait_ge(gate_steps, 4 * b + 3)
            dve.tensor_scalar(gt[:, :], gt[:, :], grz[:, 0:1], SCALING, ALU.mult, ALU.mult).then_inc(gate_steps, 1)

        def gated(b):
            dve.wait_ge(z_ps, b + 1)
            dve.wait_ge(gate_steps, 4 * b + 4)
            if some(b):
                dve.wait_ge(zT_ps, b)
            dve.tensor_tensor(zg[:, :].rearrange("p (e r) -> p e r", r=RANK),
                              b_z[:, :].rearrange("p (e r) -> p e r", r=RANK),
                              spread(gt[:, :], RANK), ALU.mult).then_inc(zg_ok, 1)

        def finish(b):
            dve.wait_ge(f_ps, b + 1)
            if some(16 * (b // 2)):
                dve.wait_ge(stored[b % 2], 16 * (b // 2))
            dve.tensor_tensor(fin[:, b % 2, :], b_z[:, :], xs[:, b, :], ALU.add).then_inc(fin_ok, 1)

        for s in range(B + 3):
            fa, fb = s - 2, s - 3
            attends, mixes, routes, leaves = s < B, 1 <= s <= B, 0 <= fa < B, 0 <= fb
            if attends:
                xmax(NT * s)
            if routes:
                normalise3(fa)
            if attends:
                xsum(NT * s)
                xmax(NT * s + 1)
            if leaves:
                finish(fb)
            if s == 0:
                newton(1)
            if attends:
                xsum(NT * s + 1)
                xmax(NT * s + 2)
                xsum(NT * s + 2)
            if routes:
                choose_mark(fa)
            if attends:
                xmax(NT * s + 3)
            if s + 2 < B:
                normalise2(s + 2)
            if attends:
                xsum(NT * s + 3)
            if routes:
                choose_gate(fa)
                gated(fa)
            if mixes:
                second_residual(s - 1)
                stats3(s - 1)

    @block.gpsimd
    def _(pool):
        def own_keys(b):
            if some(NT * (b - 1)):
                pool.wait_ge(xs_ps, NT * (b - 1))
            pool.tensor_tensor(kbd[:, b % 2, :, :], kvx[:, 0, b, :].unsqueeze(1).broadcast_to([P, XH, XK]),
                               spread(hms[:, :], XK), ALU.mult).then_inc(kbd_ok, 1)

        def own_values(b):
            if some(b):
                pool.wait_ge(vbT_ps, b)
            pool.tensor_tensor(vbd[:, :, :], kvx[:, 1, b, :].unsqueeze(1).broadcast_to([P, XH, XK]),
                               spread(hmask, XK), ALU.mult).then_inc(vbd_ok, 1)

        pool.wait_ge(hms_ok, 1)
        pool.wait_ge(kvx_ok, 2)
        own_keys(0)
        for s in range(B):
            for i in range(NT):
                t = NT * s + i
                if i == 0:
                    own_values(s)
                pool.wait_ge(xrz_ok, t + 1)
                pool.tensor_tensor(ex[:, t % 3, :, :], ex[:, t % 3, :, :], spread(xrz[:, t % 2, :], XK),
                                   ALU.mult).then_inc(xn_ok, 1)
                if i == 0 and s + 1 < B:
                    own_keys(s + 1)


def build(nc, x, consts, small, ctxT, proj, keysT, wrT, Wq, Wk, Wv, Wo, AT, BT, out):
    with ExitStack() as outer:
        oT = outer.enter_context(nc.sbuf_tensor("oT", [P, H, B * P], BF16))
        xall = oT[:, 0:B, :].rearrange("p h t -> p (h t)").bitcast(F32).rearrange("p (b n) -> p b n", b=B)
        w_raw = outer.enter_context(nc.sbuf_tensor("w_raw", [P, C, GRP * D], F32))
        w_hi = outer.enter_context(nc.sbuf_tensor("w_hi", [P, C, GRP * D], F32R))
        w_lo = outer.enter_context(nc.sbuf_tensor("w_lo", [P, C, GRP * D], F32R))
        with ExitStack() as ctx:
            attention(nc, x, consts, Wq, Wk, Wv, Wo, oT, xall, w_raw, w_hi, w_lo, outer, ctx)
        with ExitStack() as ctx:
            rest(nc, x, small, ctxT, proj, keysT, wrT, Wo, AT, BT, out, oT, w_raw, w_hi, w_lo, outer, ctx)


def kernel(**inputs):
    import numpy as _np
    import concourse.bacc as _bacc
    from concourse import mybir as _mybir
    from concourse.bass_utils import run_bass_kernel_spmd as _run

    nc = _bacc.Bacc("TRN2", target_bir_lowering=False, num_devices=1)
    g = {n: _np.asarray(a) for n, a in inputs.items()}
    X = "L0_xattn_"
    column = lambda n: g[X + n].reshape(P, 1)
    ins = {
        "x": g["x"],
        "consts": constants(),
        "small": _np.concatenate([_np.eye(P, dtype=_np.float32), head_mask(), g[X + "Wq"].T, g[X + "Wk"].T, g[X + "Wv"].T,
                                  g[X + "Wm"].T, column("bq"), column("bk"), column("bv"), column("bm")], axis=1),
        "ctxT": g["ctx_4096"].transpose(0, 2, 1),
        "proj": _np.concatenate([g[X + "proj_k"], g[X + "proj_v"]], axis=1),
        "keysT": g["L0_ffn_keys"].T,
        "wrT": g["L0_ffn_Wq_w"].T,
        "Wq": g["L0_attn_Wq"], "Wk": g["L0_attn_Wk"], "Wv": g["L0_attn_Wv"], "Wo": g["L0_attn_Wo"],
        "AT": g["L0_ffn_A_w"].T, "BT": g["L0_ffn_B_w"].T,
    }
    arrays, args = {}, []
    for name, a in ins.items():
        a = _np.ascontiguousarray(a)
        arrays[f"in_{name}"] = a
        args.append(nc.dram_tensor(f"in_{name}", a.shape, _mybir.dt.from_np(a.dtype), kind="ExternalInput").ap())
    args.append(nc.dram_tensor("out_x", (B, P, HID), _mybir.dt.float32, kind="ExternalOutput").ap())
    build(nc, *args)
    r = _run(nc, [arrays], core_ids=[0])
    return r.results[0]["out_x"]
```

```python
import concourse.bass as bass
import numpy as np
from concourse import mybir
from contextlib import ExitStack

F32 = mybir.dt.float32
F32R = mybir.dt.float32r
BF16 = mybir.dt.bfloat16
ALU = mybir.AluOpType
ACT = mybir.ActivationFunctionType
AX = mybir.AxisListType

P = 128
B = 8
HID = 512
C = HID // P
KVH = 8
GRP = 4
H = KVH * GRP
D = 128
WIN = 64
BLK = 32
NB = P // BLK
SPAN = WIN + BLK
LW = [BLK * (i + 1) for i in range(NB)]
LO = [sum(LW[:i]) for i in range(NB)]
LT = sum(LW)
HALF = B // 2
HC = 4
NCH = H // HC
THETA = 10000.0
GATE_NORM = 16.0
EPS = 1e-5
BIG = 1e30

K_ID, K_COS, K_SIN, K_MS, K_ML = 0, P, 2 * P, 3 * P, 3 * P + NB * SPAN
K_AB = K_ML + LT
K_ALL = K_AB + P + LT


def constants():
    c = np.zeros((P, K_ALL), np.float32)
    t = np.arange(P)
    c[:, K_ID:K_ID + P] = np.eye(P)
    half = np.arange(D // 2, dtype=np.float32)
    inv = (np.float32(1.0) / np.float32(THETA) ** (np.float32(2.0) * half / np.float32(D))).astype(np.float32)
    angle = t[:, None].astype(np.float32) * inv[None, :]
    cos, sin = np.cos(angle.astype(np.float64)), np.sin(angle.astype(np.float64))
    c[:, K_COS:K_COS + D] = np.concatenate([cos, cos], 1)
    c[:, K_SIN:K_SIN + D] = np.concatenate([-sin, sin], 1)
    upto = (t[:, None] <= t[None, :]).astype(np.float32)
    mid = BLK * (t // BLK) + BLK // 2 - 1
    ab = c[:, K_AB:K_AB + P + LT]
    ab[:, 0:P] = (upto - upto[:, mid]) / GATE_NORM
    for i in range(NB):
        m = BLK * i + BLK // 2 - 1
        ab[:, P + LO[i]:P + LO[i] + LW[i]] = (upto[:, m:m + 1] - upto[:, 0:LW[i]]) / GATE_NORM
    row = t % BLK
    ms = c[:, K_MS:K_MS + NB * SPAN].reshape(P, NB, SPAN)
    for i in range(NB):
        s = BLK * i - WIN + np.arange(SPAN)[None, :]
        back = BLK * i + row[:, None] - s
        ms[:, i] = np.where((s >= 0) & (back >= 0) & (back <= WIN), 0.0, -BIG)
        c[:, K_ML + LO[i]:K_ML + LO[i] + LW[i]] = 0.5 * (np.arange(LW[i])[None, :] <= BLK * i + row[:, None])
    return c


def some(count):
    return not isinstance(count, int) or count > 0


def attention(nc, x, consts, Wq, Wk, Wv, Wo, oT, xall, wq_raw, wq_hi, wq_lo, semctx, ctx):
    sb = lambda n, s, d=F32: ctx.enter_context(nc.sbuf_tensor(n, s, d))
    ps = lambda n, s, d=F32: ctx.enter_context(nc.psum_tensor(n, s, d))
    sem = lambda n: semctx.enter_context(nc.semaphore(n))

    cst = sb("cst", [P, K_AB])
    ident = cst[:, K_ID:K_ID + P]
    mask_w = cst[:, K_MS:K_MS + NB * SPAN].rearrange("p (i s) -> p i s", i=NB)
    mask_l = cst[:, K_ML:K_ML + LT]
    ab = sb("ab", [P, P + LT], F32R)
    stats = sb("stats", [P, B, 6])
    veps = sb("veps", [P, B])
    mv = sb("mv", [P, B, 2])
    std = sb("std", [P, B])
    rstd = sb("rstd", [P, B])
    newt = sb("newt", [P, B])
    hT_hi = sb("hT_hi", [P, C, B * P], F32R)
    hT_lo = sb("hT_lo", [P, C, B * P], F32R)
    wkv_raw = sb("wkv_raw", [P, C, 2 * D])
    wkv_hi = sb("wkv_hi", [P, C, 2 * D], F32R)
    wkv_lo = sb("wkv_lo", [P, C, 2 * D], F32R)
    kall = sb("kall", [P, HALF, D])
    ek = sb("ek", [P, HALF, D])
    gate = sb("gate", [P, HALF, D])
    g_hi = sb("g_hi", [P, HALF, D], F32R)
    g_lo = sb("g_lo", [P, HALF, D], F32R)
    kr = sb("kr", [P, HALF, D])
    kmx = sb("kmx", [P, HALF])
    ksm = sb("ksm", [P, HALF])
    krz = sb("krz", [P, HALF])
    ksT = sb("ksT", [P, HALF, P])
    krT = sb("krT", [P, B, WIN + P])
    dec = sb("dec", [P, B, P + LT])
    v_hi = sb("v_hi", [P, B, D], F32R)
    v_lo = sb("v_lo", [P, B, D], F32R)
    qs = sb("qs", [P, 2, GRP, D])
    eq = sb("eq", [P, 2, GRP, D])
    qr = sb("qr", [P, 2, GRP, D])
    swapped = sb("swapped", [P, GRP, D])
    qmx = sb("qmx", [P, 2, GRP])
    qsm = sb("qsm", [P, 2, GRP])
    qrz = sb("qrz", [P, 2, GRP])
    qrT = sb("qrT", [P, NB, GRP, BLK])
    qdT = sb("qdT", [P, NB, GRP, BLK])
    ss = sb("ss", [P, NB, SPAN])
    smx = sb("smx", [P, NB])
    ssm = sb("ssm", [P, NB])
    srz = sb("srz", [P, NB])
    srh = sb("srh", [P, NB])
    pm = sb("pm", [P, 2, LT])
    pT_hi = sb("pT_hi", [P, NB * P], F32R)
    pT_lo = sb("pT_lo", [P, NB * P], F32R)

    Qp = ps("Qp", [P, GRP, D])
    TQ = ps("TQ", [P, GRP, NB, BLK])
    TE = ps("TE", [P, GRP, NB, BLK])
    Sp = ps("Sp", [P, 512])
    Lp = ps("Lp", [P, 512])
    PTp = ps("PTp", [P, NB * P])
    OTp = ps("OTp", [P, NB, GRP, BLK])
    Kp = ps("Kp", [P, 512])

    h_banks = [Sp, Lp, TQ[:, :, :, :].rearrange("p h i t -> p (h i t)"), TE[:, :, :, :].rearrange("p h i t -> p (h i t)")]

    x_in = [sem(f"x_in{b}") for b in range(B)]
    ident_in = sem("ident_in")
    consts_in = sem("consts_in")
    sums_in = sem("sums_in")
    var_ok = sem("var_ok")
    kall_ok = sem("kall_ok")
    wq_in = sem("wq_in")
    wo_first = sem("wo_first")
    wo_first_hi = sem("wo_first_hi")
    wkv_in = sem("wkv_in")
    stats_ok = sem("stats_ok")
    mv_ok = sem("mv_ok")
    lnv_ok = sem("lnv_ok1")
    std_ok = sem("std_ok")
    newton_ok = sem("newton_ok")
    h_ok = sem("h_ok")
    hT_ps = sem("hT_ps")
    hT_ok = sem("hT_ok")
    hT_lo_ok = sem("hT_lo_ok")
    ab_ok = sem("ab_ok")
    pads_ok = sem("pads_ok")
    wq_hi_ok = sem("wq_hi_ok")
    wq_ok = sem("wq_ok")
    wq_last_ok = sem("wq_last_ok")
    wkv_hi_ok = sem("wkv_hi_ok")
    wkv_ok = sem("wkv_ok")
    kv_ps = sem("kv_ps")
    kv_ok = sem("kv_ok")
    kmax_ok = sem("kmax_ok")
    ksub_ok = sem("ksub_ok")
    kexp_ok = sem("kexp_ok")
    ksum_ok = sem("ksum_ok")
    krz_ok = sem("krz_ok")
    knorm_ok = sem("knorm_ok")
    gabs_ok = sem("gabs_ok")
    gexp_ok = sem("gexp_ok")
    gln_ok = sem("gln_ok")
    gate_ok = sem("gate_ok")
    ghi_ok = sem("ghi_ok")
    glo_ok = sem("glo_ok")
    krope_a = sem("krope_a")
    krope_b = sem("krope_b")
    krope_ok = sem("krope_ok")
    krT_ps = sem("krT_ps")
    krT_ok = sem("krT_ok")
    ksT_ps = sem("ksT_ps")
    ksT_ok = sem("ksT_ok")
    dec_ps = sem("dec_ps")
    dec_ok = sem("dec_ok")
    kd_ok = sem("kd_ok")
    q_ps = sem("q_ps")
    q_ok = sem("q_ok")
    qmax_ok = sem("qmax_ok")
    qexp_ok = sem("qexp_ok")
    qrz_ok = sem("qrz_ok")
    qnorm_ok = sem("qnorm_ok")
    qrope_a = sem("qrope_a")
    qrope_b = sem("qrope_b")
    qrope_ok = sem("qrope_ok")
    qrT_ps = sem("qrT_ps")
    qrT_ok = sem("qrT_ok")
    qeT_ps = sem("qeT_ps")
    qdT_ok = sem("qdT_ok")
    s_ps = sem("s_ps")
    l_ps = sem("l_ps")
    smask_ok = sem("smask_ok")
    smax_ok = sem("smax_ok")
    ssub_ok = sem("ssub_ok")
    sexp_ok = sem("sexp_ok")
    ssum_ok = sem("ssum_ok")
    srz_ok = sem("srz_ok")
    srh_ok = sem("srh_ok")
    lin_ok = sem("lin_ok")
    p_ok = sem("p_ok")
    pT_ps = sem("pT_ps")
    pT_ok = sem("pT_ok")
    pT_lo_ok = sem("pT_lo_ok")
    v_lo_ok = sem("v_lo_ok")
    o_ps = sem("o_ps")
    o_ok = sem("o_ok")

    def spread(ap, n):
        return ap.unsqueeze(2).broadcast_to([ap.shape[0], ap.shape[1], n])

    def table(lo, n):
        return cst[:, lo:lo + D].unsqueeze(1).broadcast_to([P, n, D])

    wq_v = Wq.rearrange("(c p) (k n) -> k p c n", p=P, k=KVH)
    wk_v = Wk.rearrange("(c p) (k n) -> k p c n", p=P, k=KVH)
    wv_v = Wv.rearrange("(c p) (k n) -> k p c n", p=P, k=KVH)
    x_v = x.rearrange("b t d -> t b d")
    x8 = xall

    block = ctx.enter_context(nc.Block())

    @block.sync
    def _(sp):
        for b in range(B):
            sp.dma_start(x8[:, b, :], x_v[:, b, :]).then_inc(x_in[b], 16)
            if b == 1:
                sp.dma_start(ident, consts[:, K_ID:K_ID + P]).then_inc(ident_in, 16)
            if b == HALF - 1:
                sp.dma_start(wkv_raw[:, :, 0:D], wk_v[0]).then_inc(wkv_in, 16)
                sp.dma_start(wkv_raw[:, :, D:2 * D], wv_v[0]).then_inc(wkv_in, 16)
        sp.dma_start(cst[:, K_COS:K_AB], consts[:, K_COS:K_AB]).then_inc(consts_in, 16)
        sp.dma_start(dec[:, B - 1, :], consts[:, K_AB:K_ALL]).then_inc(sums_in, 16)
        sp.dma_start(wq_raw[:, :, :], wq_v[0]).then_inc(wq_in, 16)

        def weights(k):
            sp.wait_ge(wkv_ok, k)
            sp.dma_start(wkv_raw[:, :, 0:D], wk_v[k]).then_inc(wkv_in, 16)
            sp.dma_start(wkv_raw[:, :, D:2 * D], wv_v[k]).then_inc(wkv_in, 16)
            sp.wait_ge(wq_ok, (C - 1) * k)
            sp.wait_ge(wq_last_ok, k)
            sp.dma_start(wq_raw[:, :, :], wq_v[k]).then_inc(wq_in, 16)

        for k in range(1, KVH):
            weights(k)
        sp.wait_ge(wq_ok, (C - 1) * KVH)
        sp.wait_ge(wq_last_ok, KVH)
        sp.dma_start(wq_raw[:, :, :], Wo[0:HC * P, :].rearrange("(h p) n -> p h n", p=P)).then_inc(wo_first, 16)

    @block.tensor
    def _(pe):
        def product(out, hi, lo, whi, wlo, split_of=None, chunks=range(C)):
            for c in chunks:
                if split_of is not None and c < C - 1:
                    pe.wait_ge(wq_ok, (C - 1) * split_of + c + 1)
                if split_of is not None and c == C - 1:
                    pe.wait_ge(wq_last_ok, split_of + 1)
                pe.matmul(out, hi[c], whi[c], start=(c == 0), stop=False)
                pe.matmul(out, hi[c], wlo[c], start=False, stop=False)
                mm = pe.matmul(out, lo[c], whi[c], start=False, stop=(c == C - 1))
            return mm

        def h_of(b):
            return [[t[:, c, b * P:(b + 1) * P] for c in range(C)] for t in (hT_hi, hT_lo)]

        def project_q(k, b, chunks=range(C)):
            if some(8 * k + b) and 0 in chunks:
                pe.wait_ge(q_ok, 8 * k + b)
            mm = product(Qp[:, :, :].rearrange("p h d -> p (h d)"), *h_of(b), [wq_hi[:, c, :] for c in range(C)],
                         [wq_lo[:, c, :] for c in range(C)], split_of=k if b == 0 else None, chunks=chunks)
            if C - 1 in chunks:
                mm.then_inc(q_ps, 1)

        def transpose_q(k, b):
            n = 8 * k + b
            pe.wait_ge(qrope_ok, n + 1)
            if some(n):
                pe.wait_ge(qrT_ok, n)
            for h in range(GRP):
                mm = pe.transpose(TQ[:, h, :, :].rearrange("p i t -> p (i t)"), qr[:, b % 2, h, :], ident)
            mm.then_inc(qrT_ps, 1)

        def transpose_qe(k, b):
            n = 8 * k + b
            pe.wait_ge(qnorm_ok, n + 1)
            if some(n):
                pe.wait_ge(qdT_ok, n)
            for h in range(GRP):
                mm = pe.transpose(TE[:, h, :, :].rearrange("p i t -> p (i t)"), eq[:, b % 2, h, :], ident)
            mm.then_inc(qeT_ps, 1)

        def scores(k, b):
            n = 8 * k + b
            m = 2 * k + b // HALF
            if b % HALF == 0:
                pe.wait_ge(krT_ok, m + 1)
            pe.wait_ge(qrT_ok, n + 1)
            if some(n):
                pe.wait_ge(smask_ok, n)
            for i in range(NB):
                mm = pe.matmul(Sp[:, i * SPAN:(i + 1) * SPAN], qrT[:, i, :, :].rearrange("p h t -> p (h t)"),
                               krT[:, b, BLK * i:BLK * i + SPAN], start=True, stop=True)
            mm.then_inc(s_ps, 1)

        def linear_scores(k, b):
            n = 8 * k + b
            if b % HALF == 0:
                pe.wait_ge(kd_ok, 2 * k + b // HALF + 1)
            pe.wait_ge(qdT_ok, n + 1)
            if some(n):
                pe.wait_ge(lin_ok, n)
            for i in range(NB):
                mm = pe.matmul(Lp[:, LO[i]:LO[i] + LW[i]], qdT[:, i, :, :].rearrange("p h t -> p (h t)"),
                               dec[:, b, P + LO[i]:P + LO[i] + LW[i]], start=True, stop=True)
            mm.then_inc(l_ps, 1)

        def transpose_p(k, b):
            n = 8 * k + b
            pe.wait_ge(p_ok, n + 1)
            if some(n):
                pe.wait_ge(pT_lo_ok, n)
            if isinstance(n, int) and n == 0:
                pe.wait_ge(pads_ok, 2)
            for i in range(NB):
                mm = pe.transpose(PTp[0:LW[i], i * P:(i + 1) * P], pm[:, b % 2, LO[i]:LO[i] + LW[i]], ident)
            mm.then_inc(pT_ps, 1)

        def mix(k, b):
            n = 8 * k + b
            pe.wait_ge(pT_lo_ok, n + 1)
            if some(n):
                pe.wait_ge(o_ok, n)
            out = OTp[:, :, :, :].rearrange("p i h t -> p (i h t)")
            pe.matmul(out, v_hi[:, b, :], pT_hi[:, :], start=True, stop=False)
            pe.matmul(out, v_lo[:, b, :], pT_hi[:, :], start=False, stop=False)
            pe.matmul(out, v_hi[:, b, :], pT_lo[:, :], start=False, stop=True).then_inc(o_ps, 1)

        def project_kv(k, hf, pair):
            m = 2 * k + hf
            if pair == 0:
                pe.wait_ge(wkv_ok, k + 1)
                if some(4 * m):
                    pe.wait_ge(dec_ok, 4 * m)
            else:
                pe.wait_ge(v_lo_ok, 2 * m + 1)
            for y in range(2):
                b = HALF * hf + 2 * pair + y
                mm = product(Kp[:, y * 2 * D:(y + 1) * 2 * D], *h_of(b), [wkv_hi[:, c, :] for c in range(C)],
                             [wkv_lo[:, c, :] for c in range(C)])
            mm.then_inc(kv_ps, 1)

        def transpose_kr(m):
            pe.wait_ge(krope_ok, m + 1)
            pe.wait_ge(v_lo_ok, 2 * m + 2)
            for y in range(HALF):
                mm = pe.transpose(Kp[:, y * P:(y + 1) * P], kr[:, y, :], ident)
            mm.then_inc(krT_ps, 1)

        def transpose_ks(m):
            pe.wait_ge(knorm_ok, m + 1)
            pe.wait_ge(krT_ok, m + 1)
            for y in range(HALF):
                mm = pe.transpose(Kp[:, y * P:(y + 1) * P], ek[:, y, :], ident)
            mm.then_inc(ksT_ps, 1)

        def decays(m, y):
            if y == 0:
                pe.wait_ge(glo_ok, m + 1)
                pe.wait_ge(ksT_ok, m + 1)
            else:
                if some(4 * m + y):
                    pe.wait_ge(dec_ok, 4 * m + y)
            pe.matmul(Kp[:, 0:P + LT], g_hi[:, y, :], ab[:, :], start=True, stop=False)
            pe.matmul(Kp[:, 0:P + LT], g_lo[:, y, :], ab[:, :], start=False, stop=True).then_inc(dec_ps, 1)

        def transpose_h(b):
            pe.wait_ge(h_ok, b + 1)
            if some(b - 3):
                pe.wait_ge(hT_lo_ok, b - 3)
            for c in range(C):
                mm = pe.transpose(h_banks[b % 4][:, c * P:(c + 1) * P], x8[:, b, c * P:(c + 1) * P], ident)
            mm.then_inc(hT_ps, 1)

        pe.wait_ge(ident_in, 16)
        for b in range(HALF):
            transpose_h(b)
        pe.wait_ge(hT_lo_ok, HALF)
        project_kv(0, 0, 0)
        for b in range(HALF, B):
            transpose_h(b)
        project_kv(0, 0, 1)
        pe.wait_ge(hT_lo_ok, B)
        project_q(0, 0)
        transpose_kr(0)
        transpose_ks(0)
        pe.wait_ge(ab_ok, 1)

        def head(k, first=False, last=False):
            for j in range(B):
                w = j % HALF
                kk, hf = (k, 1) if j < HALF else (k + 1, 0)
                m = 2 * kk + hf
                work = not (last and j >= HALF)
                k1, b1 = (k, j - 1) if j >= 1 else (k - 1, B - 1)
                k2, b2 = (k, j - 2) if j >= 2 else (k - 1, B + j - 2)
                live1, live2 = not (first and j < 1), not (first and j < 2)
                early = j == 0 and not first
                if early:
                    project_q(k, j, chunks=(0, 1))
                if j > 0:
                    project_q(k, j)
                if w == 0 and not early:
                    decays(m - 1, 0)
                if w == 3 and work:
                    transpose_kr(m)
                if live1:
                    transpose_q(k1, b1)
                if live1:
                    transpose_qe(k1, b1)
                if early:
                    decays(m - 1, 0)
                if early:
                    project_q(k, j, chunks=(2, 3))
                if w == 0:
                    decays(m - 1, 1)
                if live2:
                    transpose_p(k2, b2)
                if live1:
                    scores(k1, b1)
                if w == 0:
                    decays(m - 1, 2)
                if live1:
                    linear_scores(k1, b1)
                if w == 0:
                    decays(m - 1, 3)
                if w == 3 and work:
                    transpose_ks(m)
                if live2:
                    mix(k2, b2)
                if w < 2 and work:
                    project_kv(kk, hf, w)

        head(0, first=True)
        with pe.Fori(1, KVH - 1) as k:
            head(k)
        head(KVH - 1, last=True)
        transpose_q(KVH - 1, B - 1)
        transpose_qe(KVH - 1, B - 1)
        transpose_p(KVH - 1, B - 2)
        scores(KVH - 1, B - 1)
        linear_scores(KVH - 1, B - 1)
        mix(KVH - 1, B - 2)
        transpose_p(KVH - 1, B - 1)
        mix(KVH - 1, B - 1)

    @block.scalar
    def _(act):
        def split_wkv(k):
            act.wait_ge(wkv_in, 32 * k + 32)
            if some(4 * k):
                act.wait_ge(kv_ps, 4 * k)
            act.activation(wkv_hi[:, :, :], wkv_raw[:, :, :], ACT.Copy).then_inc(wkv_hi_ok, 1)

        def split_wq(k, c):
            act.wait_ge(wq_in, 16 * k + 16)
            if some(8 * k):
                act.wait_ge(q_ps, 8 * k)
            act.activation(wq_hi[:, c, :], wq_raw[:, c, :], ACT.Copy).then_inc(wq_hi_ok, 1)

        def copy_q(k, b):
            n = 8 * k + b
            act.wait_ge(q_ps, n + 1)
            if some(n - 1):
                act.wait_ge(qrope_b, n - 1)
            act.activation(qs[:, b % 2, :, :], Qp[:, :, :], ACT.Copy).then_inc(q_ok, 1)

        def exp_q(k, b):
            n = 8 * k + b
            act.wait_ge(qmax_ok, n + 1)
            if some(n - 1):
                act.wait_ge(qeT_ps, n - 1)
                act.wait_ge(qrz_ok, n - 1)
            for h in range(GRP):
                op = act.activation(eq[:, b % 2, h, :], qs[:, b % 2, h, :], ACT.Exp, bias=qmx[:, b % 2, h:h + 1],
                                    accum_out=qsm[:, b % 2, h:h + 1])
            op.then_inc(qexp_ok, 1)

        def copy_qrT(k, b):
            n = 8 * k + b
            act.wait_ge(qrT_ps, n + 1)
            if some(n):
                act.wait_ge(s_ps, n)
            act.activation(qrT[:, :, :, :], TQ[:, :, :, :].rearrange("p h i t -> p i h t"),
                           ACT.Copy).then_inc(qrT_ok, 1)

        def exp_s(k, b):
            act.wait_ge(ssub_ok, 8 * k + b + 1)
            act.activation(ss[:, :, :], ss[:, :, :], ACT.Exp).then_inc(sexp_ok, 1)

        def copy_pT(k, b):
            n = 8 * k + b
            act.wait_ge(pT_ps, n + 1)
            if some(n):
                act.wait_ge(o_ps, n)
            act.activation(pT_hi[:, :], PTp[:, :], ACT.Copy).then_inc(pT_ok, 1)

        def copy_o(k, b):
            act.wait_ge(o_ps, 8 * k + b + 1)
            act.wait_ge(ab_ok, 1)
            act.activation(oT[:, bass.ds(GRP * k, GRP), b * P:(b + 1) * P].rearrange("p h (i t) -> p i h t", i=NB),
                           OTp[:, :, :, :], ACT.Copy).then_inc(o_ok, 1)

        def copy_kv(k, hf, pair):
            m = 2 * k + hf
            kv = Kp[:, :].rearrange("p (y a d) -> p y a d", y=2, a=2)
            act.wait_ge(kv_ps, 2 * m + pair + 1)
            if pair == 0:
                if some(m):
                    act.wait_ge(ksub_ok, m)
                if some(m):
                    act.wait_ge(gate_ok, m)
                if some(m):
                    act.wait_ge(gabs_ok, m)
                if some(m):
                    act.wait_ge(krope_b, m)
            act.activation(kall[:, 2 * pair:2 * pair + 2, :], kv[:, :, 0, :], ACT.Copy).then_inc(kall_ok, 1)
            b = HALF * hf + 2 * pair
            if some(8 * k + b + 2 - B):
                act.wait_ge(o_ps, 8 * k + b + 2 - B)
            act.activation(v_hi[:, b:b + 2, :], kv[:, :, 1, :], ACT.Copy).then_inc(kv_ok, 1)

        def gate_abs(m):
            act.wait_ge(kall_ok, 2 * m + 2)
            if some(m):
                act.wait_ge(glo_ok, m)
            act.activation(gate[:, :, :], kall[:, :, :], ACT.Abs).then_inc(gabs_ok, 1)

        def gate_exp(m):
            act.wait_ge(gabs_ok, m + 1)
            act.activation(gate[:, :, :], gate[:, :, :], ACT.Exp, scale=-1.0).then_inc(gexp_ok, 1)

        def gate_ln(m):
            act.wait_ge(gexp_ok, m + 1)
            act.activation(gate[:, :, :], gate[:, :, :], ACT.Ln, bias=1.0).then_inc(gln_ok, 1)

        def exp_k(m):
            act.wait_ge(ksub_ok, m + 1)
            act.activation(ek[:, :, :], ek[:, :, :], ACT.Exp).then_inc(kexp_ok, 1)

        def gate_hi(m):
            act.wait_ge(gate_ok, m + 1)
            if some(4 * m):
                act.wait_ge(dec_ps, 4 * m)
            act.activation(g_hi[:, :, :], gate[:, :, :], ACT.Copy).then_inc(ghi_ok, 1)

        def copy_krT(k, hf):
            m = 2 * k + hf
            act.wait_ge(krT_ps, m + 1)
            if some(8 * k + HALF * hf - HALF):
                act.wait_ge(s_ps, 8 * k + HALF * hf - HALF)
            act.activation(krT[:, HALF * hf:HALF * hf + HALF, WIN:WIN + P],
                           Kp[:, :].rearrange("p (y s) -> p y s", y=HALF), ACT.Copy).then_inc(krT_ok, 1)

        def copy_ksT(m):
            act.wait_ge(ksT_ps, m + 1)
            if some(m):
                act.wait_ge(kd_ok, m)
            act.activation(ksT[:, :, :], Kp[:, :].rearrange("p (y s) -> p y s", y=HALF), ACT.Copy).then_inc(ksT_ok, 1)

        def exp_dec(k, hf, y):
            m = 2 * k + hf
            act.wait_ge(dec_ps, 4 * m + y + 1)
            if some(8 * k + HALF * hf - HALF):
                act.wait_ge(l_ps, 8 * k + HALF * hf - HALF)
            act.activation(dec[:, HALF * hf + y, :], Kp[:, 0:P + LT], ACT.Exp).then_inc(dec_ok, 1)

        act.preload_act_table_set("natural_log_exp_and_others")

        def rsqrt(g):
            of = slice(g * HALF, (g + 1) * HALF)
            act.wait_ge(var_ok, g + 1)
            act.activation(std[:, of], veps[:, of], ACT.Ln).then_inc(lnv_ok, 1)
            act.wait_ge(lnv_ok, g + 1)
            act.activation(rstd[:, of], std[:, of], ACT.Exp, scale=-0.5).then_inc(std_ok, 1)

        def hi_h(b):
            act.wait_ge(hT_ps, b + 1)
            act.activation(hT_hi[:, :, b * P:(b + 1) * P], h_banks[b % 4][:, :].rearrange("p (c t) -> p c t", c=C),
                           ACT.Copy).then_inc(hT_ok, 1)

        rsqrt(0)
        for b in range(HALF):
            hi_h(b)
        split_wkv(0)
        rsqrt(1)
        copy_kv(0, 0, 0)
        for b in range(HALF, B):
            hi_h(b)
        split_wq(0, 0)
        copy_kv(0, 0, 1)
        gate_abs(0)
        split_wq(0, 1)
        gate_exp(0)
        exp_k(0)
        split_wq(0, 2)
        gate_ln(0)
        split_wq(0, 3)
        act.wait_ge(sums_in, 16)
        act.activation(ab[:, :], dec[:, B - 1, :], ACT.Copy).then_inc(ab_ok, 1)
        gate_hi(0)
        copy_krT(0, 0)
        copy_ksT(0)

        def head(k, first=False, last=False):
            for j in range(B):
                w = j % HALF
                kk, hf = (k, 1) if j < HALF else (k + 1, 0)
                kp, hp = (k, 0) if j < HALF else (k, 1)
                m = 2 * kk + hf
                work = not (last and j >= HALF)
                k1, b1 = (k, j - 1) if j >= 1 else (k - 1, B - 1)
                k2, b2 = (k, j - 2) if j >= 2 else (k - 1, B + j - 2)
                live1, live2 = not (first and j < 1), not (first and j < 2)
                splits = j == B - 1 and not last
                if w == 2 and work:
                    gate_abs(m)
                    gate_exp(m)
                early = j == 0 and not first
                if not early:
                    copy_q(k, j)
                if w == 0 and not early:
                    exp_dec(kp, hp, 0)
                if w == 3 and work:
                    copy_krT(kk, hf)
                if live1:
                    copy_qrT(k1, b1)
                if early:
                    exp_dec(kp, hp, 0)
                    copy_q(k, j)
                if w == 0:
                    exp_dec(kp, hp, 1)
                if live2:
                    copy_pT(k2, b2)
                if w == 2 and work:
                    exp_k(m)
                    gate_ln(m)
                if w == 0:
                    exp_dec(kp, hp, 2)
                    exp_dec(kp, hp, 3)
                if splits:
                    split_wq(k + 1, 0)
                    split_wq(k + 1, 1)
                if w == 3 and work:
                    gate_hi(m)
                exp_q(k, j)
                if w == 3 and work:
                    copy_ksT(m)
                if splits:
                    split_wq(k + 1, 2)
                    split_wq(k + 1, 3)
                if live1:
                    exp_s(k1, b1)
                if live2:
                    copy_o(k2, b2)
                if w < 2 and work:
                    copy_kv(kk, hf, w)
                if j == 3 and not last:
                    split_wkv(k + 1)

        head(0, first=True)
        with act.Fori(1, KVH - 1) as k:
            head(k)
        head(KVH - 1, last=True)
        copy_qrT(KVH - 1, B - 1)
        copy_pT(KVH - 1, B - 2)
        act.wait_ge(wo_first, 16)
        act.wait_ge(q_ps, B * KVH)
        act.activation(wq_hi[:, :, :], wq_raw[:, :, :], ACT.Copy).then_inc(wo_first_hi, 1)
        exp_s(KVH - 1, B - 1)
        copy_o(KVH - 1, B - 2)
        copy_pT(KVH - 1, B - 1)
        copy_o(KVH - 1, B - 1)

    @block.vector
    def _(dve):
        def split_wkv(k):
            dve.wait_ge(wkv_hi_ok, k + 1)
            dve.tensor_tensor(wkv_lo[:, :, :], wkv_raw[:, :, :], wkv_hi[:, :, :].bitcast(F32),
                              ALU.subtract).then_inc(wkv_ok, 1)

        def split_wq(k, c):
            dve.wait_ge(wq_hi_ok, C * k + c + 1)
            dve.tensor_tensor(wq_lo[:, c, :], wq_raw[:, c, :], wq_hi[:, c, :].bitcast(F32),
                              ALU.subtract).then_inc(wq_ok, 1)

        def max_q(k, b):
            n = 8 * k + b
            dve.wait_ge(q_ok, n + 1)
            if some(n - 1):
                dve.wait_ge(qexp_ok, n - 1)
            dve.tensor_reduce(qmx[:, b % 2, :], qs[:, b % 2, :, :], AX.X, ALU.max, negate=True).then_inc(qmax_ok, 1)

        def recip_q(k, b):
            n = 8 * k + b
            dve.wait_ge(qexp_ok, n + 1)
            if some(n - 1):
                dve.wait_ge(qnorm_ok, n - 1)
            dve.reciprocal(qrz[:, b % 2, :], qsm[:, b % 2, :]).then_inc(qrz_ok, 1)

        def decay_q(k, b):
            n = 8 * k + b
            dve.wait_ge(qeT_ps, n + 1)
            if some(n):
                dve.wait_ge(l_ps, n)
            if isinstance(n, int) and n == 0:
                dve.wait_ge(dec_ok, HALF)
            dve.tensor_tensor(qdT[:, :, :, :], TE[:, :, :, :].rearrange("p h i t -> p i h t"),
                              dec[:, b, 0:P].rearrange("p (i t) -> p i t", i=NB).unsqueeze(2)
                              .broadcast_to([P, NB, GRP, BLK]), ALU.mult).then_inc(qdT_ok, 1)

        def mask_s(k, b):
            n = 8 * k + b
            dve.wait_ge(s_ps, n + 1)
            if some(n):
                dve.wait_ge(p_ok, n)
            dve.scalar_tensor_tensor(out=ss[:, :, :], in0=Sp[:, 0:NB * SPAN].rearrange("p (i s) -> p i s", i=NB),
                                     scalar=float(D) ** -0.5, in1=mask_w, op0=ALU.mult,
                                     op1=ALU.add).then_inc(smask_ok, 1)
            dve.wait_ge(smask_ok, n + 1)
            dve.tensor_reduce(smx[:, :], ss[:, :, :], AX.X, ALU.max).then_inc(smax_ok, 1)
            dve.wait_ge(smax_ok, n + 1)
            dve.tensor_tensor(ss[:, :, :], ss[:, :, :], spread(smx[:, :], SPAN), ALU.subtract).then_inc(ssub_ok, 1)

        def linear(k, b):
            n = 8 * k + b
            dve.wait_ge(l_ps, n + 1)
            if some(n - 1):
                dve.wait_ge(pT_ps, n - 1)
            dve.scalar_tensor_tensor(out=pm[:, b % 2, :], in0=Lp[:, 0:LT], scalar=BIG, in1=mask_l, op0=ALU.min,
                                     op1=ALU.mult).then_inc(lin_ok, 1)

        def combine(k, b):
            n = 8 * k + b
            dve.wait_ge(sexp_ok, n + 1)
            dve.tensor_reduce(ssm[:, :], ss[:, :, :], AX.X, ALU.add).then_inc(ssum_ok, 1)
            dve.wait_ge(ssum_ok, n + 1)
            dve.reciprocal(srz[:, :], ssm[:, :]).then_inc(srz_ok, 1)
            dve.wait_ge(srz_ok, n + 1)
            dve.tensor_scalar(srh[:, :], srz[:, :], 0.5, None, ALU.mult).then_inc(srh_ok, 1)
            dve.wait_ge(srh_ok, n + 1)
            dve.wait_ge(lin_ok, n + 1)
            for i in range(NB):
                w = min(LW[i], SPAN)
                seen = pm[:, b % 2, LO[i] + LW[i] - w:LO[i] + LW[i]]
                op = dve.scalar_tensor_tensor(out=seen, in0=ss[:, i, SPAN - w:SPAN], scalar=srh[:, i:i + 1], in1=seen,
                                              op0=ALU.mult, op1=ALU.add)
            op.then_inc(p_ok, 1)

        def lo_v(k, hf, pair):
            b = HALF * hf + 2 * pair
            kv = Kp[:, :].rearrange("p (y a d) -> p y a d", y=2, a=2)
            dve.wait_ge(kv_ok, 4 * k + 2 * hf + pair + 1)
            dve.tensor_tensor(v_lo[:, b:b + 2, :], kv[:, :, 1, :], v_hi[:, b:b + 2, :].bitcast(F32),
                              ALU.subtract).then_inc(v_lo_ok, 1)

        def lo_p(k, b):
            n = 8 * k + b
            dve.wait_ge(pT_ok, n + 1)
            if some(n):
                dve.wait_ge(o_ps, n)
            dve.tensor_tensor(pT_lo[:, :], PTp[:, :], pT_hi[:, :].bitcast(F32), ALU.subtract).then_inc(pT_lo_ok, 1)

        def softmax_k(m):
            dve.wait_ge(kv_ok, 2 * m + 2)
            dve.tensor_reduce(kmx[:, :], kall[:, :, :], AX.X, ALU.max).then_inc(kmax_ok, 1)
            dve.wait_ge(kmax_ok, m + 1)
            if some(m):
                dve.wait_ge(ksT_ps, m)
            dve.tensor_tensor(ek[:, :, :], kall[:, :, :], spread(kmx[:, :], D), ALU.subtract).then_inc(ksub_ok, 1)

        def sum_k(m):
            dve.wait_ge(kexp_ok, m + 1)
            dve.tensor_reduce(ksm[:, :], ek[:, :, :], AX.X, ALU.add).then_inc(ksum_ok, 1)
            dve.wait_ge(ksum_ok, m + 1)
            if some(m):
                dve.wait_ge(knorm_ok, m)
            dve.reciprocal(krz[:, :], ksm[:, :]).then_inc(krz_ok, 1)

        def gate_k(m):
            dve.wait_ge(gln_ok, m + 1)
            dve.scalar_tensor_tensor(out=gate[:, :, :], in0=kall[:, :, :], scalar=0.0, in1=gate[:, :, :], op0=ALU.min,
                                     op1=ALU.subtract).then_inc(gate_ok, 1)

        def decay_k(m, hf):
            dve.wait_ge(dec_ok, 4 * m + HALF)
            dve.wait_ge(ksT_ok, m + 1)
            for i in range(NB):
                to = dec[:, HALF * hf:HALF * hf + HALF, P + LO[i]:P + LO[i] + LW[i]]
                op = dve.tensor_tensor(to, ksT[:, :, 0:LW[i]], to, ALU.mult)
            op.then_inc(kd_ok, 1)

        dve.memset(krT[:, :, 0:WIN], 0.0).then_inc(pads_ok, 1)
        dve.memset(PTp[:, :], 0.0).then_inc(pads_ok, 1)

        def variances(g):
            for b in range(g * HALF, (g + 1) * HALF):
                dve.wait_ge(x_in[b], 16)
                dve.bn_stats(stats[:, b, :], x8[:, b, :]).then_inc(stats_ok, 1)
                dve.wait_ge(stats_ok, b + 1)
                dve.bn_aggr(mv[:, b, :], stats[:, b, :]).then_inc(mv_ok, 1)
            of = slice(g * HALF, (g + 1) * HALF)
            dve.wait_ge(mv_ok, HALF * g + HALF)
            dve.tensor_scalar(veps[:, of], mv[:, of, 1], EPS, None, ALU.add).then_inc(var_ok, 1)

        def normalise(g):
            of = slice(g * HALF, (g + 1) * HALF)
            dve.wait_ge(std_ok, g + 1)
            dve.tensor_tensor(newt[:, of], rstd[:, of], rstd[:, of], ALU.mult).then_inc(newton_ok, 1)
            dve.wait_ge(newton_ok, 4 * g + 1)
            dve.tensor_tensor(newt[:, of], newt[:, of], veps[:, of], ALU.mult).then_inc(newton_ok, 1)
            dve.wait_ge(newton_ok, 4 * g + 2)
            dve.tensor_scalar(newt[:, of], newt[:, of], -0.5, 1.5, ALU.mult, ALU.add).then_inc(newton_ok, 1)
            dve.wait_ge(newton_ok, 4 * g + 3)
            dve.tensor_tensor(rstd[:, of], rstd[:, of], newt[:, of], ALU.mult).then_inc(newton_ok, 1)
            dve.wait_ge(newton_ok, 4 * g + 4)
            for b in range(g * HALF, (g + 1) * HALF):
                dve.tensor_scalar(x8[:, b, :], x8[:, b, :], mv[:, b, 0:1], rstd[:, b:b + 1], ALU.subtract,
                                  ALU.mult).then_inc(h_ok, 1)

        def lo_h(b):
            cols = slice(b * P, (b + 1) * P)
            dve.wait_ge(hT_ok, b + 1)
            dve.tensor_tensor(hT_lo[:, :, cols], h_banks[b % 4][:, :].rearrange("p (c t) -> p c t", c=C),
                              hT_hi[:, :, cols].bitcast(F32), ALU.subtract).then_inc(hT_lo_ok, 1)

        variances(0)
        normalise(0)
        for b in range(HALF):
            lo_h(b)
        split_wkv(0)
        variances(1)
        normalise(1)
        lo_v(0, 0, 0)
        for b in range(HALF, B):
            lo_h(b)
        lo_v(0, 0, 1)
        split_wq(0, 0)
        softmax_k(0)
        split_wq(0, 1)
        sum_k(0)
        split_wq(0, 2)
        gate_k(0)

        def head(k, first=False, last=False):
            for j in range(B):
                w = j % HALF
                kk, hf = (k, 1) if j < HALF else (k + 1, 0)
                m = 2 * kk + hf
                work = not (last and j >= HALF)
                k1, b1 = (k, j - 1) if j >= 1 else (k - 1, B - 1)
                k2, b2 = (k, j - 2) if j >= 2 else (k - 1, B + j - 2)
                live1, live2 = not (first and j < 1), not (first and j < 2)
                splits = j == B - 1 and not last
                if w == 2 and work:
                    softmax_k(m)
                if live1:
                    decay_q(k1, b1)
                max_q(k, j)
                if live2:
                    lo_p(k2, b2)
                if splits:
                    split_wq(k + 1, 0)
                    split_wq(k + 1, 1)
                if live1:
                    mask_s(k1, b1)
                if w == 2 and work:
                    sum_k(m)
                recip_q(k, j)
                if splits:
                    split_wq(k + 1, 2)
                if live1:
                    linear(k1, b1)
                if live1:
                    combine(k1, b1)
                if w == 2 and work:
                    gate_k(m)
                if w == 0:
                    decay_k(m - 1, 1 - hf)
                if w < 2 and work:
                    lo_v(kk, hf, w)
                if j == 3 and not last:
                    split_wkv(k + 1)

        head(0, first=True)
        with dve.Fori(1, KVH - 1) as k:
            head(k)
        head(KVH - 1, last=True)
        decay_q(KVH - 1, B - 1)
        lo_p(KVH - 1, B - 2)
        mask_s(KVH - 1, B - 1)
        linear(KVH - 1, B - 1)
        combine(KVH - 1, B - 1)
        lo_p(KVH - 1, B - 1)

    @block.gpsimd
    def _(pool):
        def swapped_sin(src, to, n):
            for a in range(2):
                half, other = slice(a * (D // 2), (a + 1) * (D // 2)), slice((1 - a) * (D // 2), (2 - a) * (D // 2))
                sin = cst[:, K_SIN + a * (D // 2):K_SIN + (a + 1) * (D // 2)].unsqueeze(1).broadcast_to([P, n, D // 2])
                op = pool.tensor_tensor(to[:, :, half], src[:, :, other], sin, ALU.mult)
            return op

        def rotate_q(k, b, keys=None):
            n = 8 * k + b
            pool.wait_ge(q_ok, n + 1)
            if some(n - 1):
                pool.wait_ge(qrT_ps, n - 1)
            pool.tensor_tensor(qr[:, b % 2, :, :], qs[:, b % 2, :, :], table(K_COS, GRP), ALU.mult).then_inc(qrope_a, 1)
            if some(n):
                pool.wait_ge(qrope_ok, n)
            if keys is not None:
                pool.wait_ge(krope_ok, keys)
            swapped_sin(qs[:, b % 2, :, :], swapped, GRP).then_inc(qrope_b, 1)
            pool.wait_ge(qrope_a, n + 1)
            pool.wait_ge(qrope_b, n + 1)
            pool.tensor_tensor(qr[:, b % 2, :, :], qr[:, b % 2, :, :], swapped[:, :, :], ALU.add).then_inc(qrope_ok, 1)

        def normalise_q(k, b):
            pool.wait_ge(qrz_ok, 8 * k + b + 1)
            pool.tensor_tensor(eq[:, b % 2, :, :], eq[:, b % 2, :, :], spread(qrz[:, b % 2, :], D),
                               ALU.mult).then_inc(qnorm_ok, 1)

        def rotate_k(m, queries=0):
            pool.wait_ge(kall_ok, 2 * m + 2)
            if some(m):
                pool.wait_ge(krT_ps, m)
            pool.tensor_tensor(kr[:, :, :], kall[:, :, :], table(K_COS, HALF), ALU.mult).then_inc(krope_a, 1)
            if some(queries):
                pool.wait_ge(qrope_ok, queries)
            swapped_sin(kall, swapped, HALF).then_inc(krope_b, 1)
            pool.wait_ge(krope_a, m + 1)
            pool.wait_ge(krope_b, m + 1)
            pool.tensor_tensor(kr[:, :, :], kr[:, :, :], swapped[:, :, :], ALU.add).then_inc(krope_ok, 1)

        def gate_lo(m):
            pool.wait_ge(ghi_ok, m + 1)
            if some(4 * m):
                pool.wait_ge(dec_ps, 4 * m)
            pool.tensor_tensor(g_lo[:, :, :], gate[:, :, :], g_hi[:, :, :].bitcast(F32), ALU.subtract).then_inc(glo_ok, 1)

        def normalise_k(m):
            pool.wait_ge(krz_ok, m + 1)
            pool.tensor_tensor(ek[:, :, :], ek[:, :, :], spread(krz[:, :], D), ALU.mult).then_inc(knorm_ok, 1)

        def split_wq(k):
            pool.wait_ge(wq_hi_ok, C * k + C)
            pool.tensor_tensor(wq_lo[:, C - 1, :], wq_raw[:, C - 1, :], wq_hi[:, C - 1, :].bitcast(F32),
                               ALU.subtract).then_inc(wq_last_ok, 1)

        pool.wait_ge(consts_in, 16)
        rotate_k(0)
        split_wq(0)
        normalise_k(0)
        gate_lo(0)

        def head(k, last=False):
            for j in range(B):
                m = 2 * k + (1 if j < HALF else 2)
                w = j % HALF
                work = not (last and j >= HALF)
                if w == 2 and work:
                    rotate_k(m, queries=8 * k + j)
                    rotate_q(k, j, keys=m + 1)
                else:
                    rotate_q(k, j, keys=1 if j == 0 and isinstance(k, int) and k == 0 else None)
                if w == 3 and work:
                    gate_lo(m)
                normalise_q(k, j)
                if j == B - 1 and not last:
                    split_wq(k + 1)
                if w == 2 and work:
                    normalise_k(m)

        head(0)
        with pool.Fori(1, KVH - 1) as k:
            head(k)
        head(KVH - 1, last=True)
        pool.wait_ge(wo_first_hi, 1)
        pool.tensor_tensor(wq_lo[:, :, :], wq_raw[:, :, :], wq_hi[:, :, :].bitcast(F32), ALU.subtract)

XH, XK = 16, 32
XD = P // XH
XJ = XH * XK // P
NT = HID // P
E_NUM, RANK, TOP_K, RDIM = 64, 8, 16, 16
SCALING = 2.0

R_ID, R_HM, R_WQ, R_WK, R_WV, R_WM, R_B = 0, P, P + XH, 2 * P + XH, 3 * P + XH, 4 * P + XH, 5 * P + XH
R_ALL = R_B + 4


def head_mask():
    return (np.arange(P)[:, None] % XH == np.arange(XH)[None, :]).astype(np.float32)


def rest(nc, x, small, ctxT, proj, keysT, Wr, Wo, AT, BT, out, oT, w_raw, w_hi, w_lo, semctx, ctx):
    sb = lambda n, s, d=F32: ctx.enter_context(nc.sbuf_tensor(n, s, d))
    ps = lambda n, s, d=F32: ctx.enter_context(nc.psum_tensor(n, s, d))
    sem = lambda n: semctx.enter_context(nc.semaphore(n))

    cs = sb("cs", [P, R_ALL])
    ident = cs[:, R_ID:R_ID + P]
    wqT, wkT, wvT, wmT = (cs[:, o:o + P] for o in (R_WQ, R_WK, R_WV, R_WM))
    bq, bk, bv, bm = (cs[:, R_B + i:R_B + i + 1] for i in range(4))
    hmask = cs[:, R_HM:R_HM + XH]
    xs = sb("xs", [P, B, HID])
    wo_raw = [w_raw, sb("wo_raw1", [P, HC, HID])]
    wo_hi = [w_hi, sb("wo_hi1", [P, HC, HID], F32R)]
    wo_lo = [w_lo, sb("wo_lo1", [P, HC, HID], F32R)]
    oF = sb("oF", [P, 2, HC, P], F32R)
    ctx_sb = sb("ctx_sb", [P, NT, B, P])
    proj_sb = sb("proj_sb", [P, NT, 2 * XK])
    ones = sb("ones", [P, P])
    cp = sb("cp", [P, 2, B, XK])
    kvb = sb("kvb", [P, 2, XK])
    kvx = sb("kvx", [P, 2, B, XK])
    hms = sb("hms", [P, XH])
    kbd = sb("kbd", [P, 2, XH, XK])
    vbd = sb("vbd", [P, XH, XK])
    vbT = sb("vbT", [P, 2, XJ, P])
    h3T_hi, h3T_lo, zgT_hi, zgT_lo = (sb(n, [P, C, P], F32R) for n in ("h3T_hi", "h3T_lo", "zgT_hi", "zgT_lo"))
    wr = sb("wr", [RDIM, HID])
    keys = sb("keys", [RDIM, E_NUM])
    router = sb("router", [P, C, E_NUM])
    st2 = sb("st2", [P, B, 6])
    mv2 = sb("mv2", [P, B, 2])
    ve2 = sb("ve2", [P, B])
    ln2 = sb("ln2", [P, B])
    y2 = sb("y2", [P, B])
    nt2 = sb("nt2", [P, B])
    rs2 = sb("rs2", [P, B])
    st3 = sb("st3", [P, 6])
    mv3 = sb("mv3", [P, 2])
    ve3 = sb("ve3", [P, 1])
    ln3 = sb("ln3", [P, 1])
    y3 = sb("y3", [P, 1])
    nta3 = sb("nta3", [P, 1])
    ntb3 = sb("ntb3", [P, 1])
    rs3 = sb("rs3", [P, 1])
    xmx = sb("xmx", [P, 2, XH])
    xsm = sb("xsm", [P, 2, XH])
    xrz = sb("xrz", [P, 2, XH])
    top = sb("top", [P, 8])
    top2 = sb("top2", [P, 8])
    ntop = sb("ntop", [P, 1])
    gsum = sb("gsum", [P, 1])
    grz = sb("grz", [P, 1])
    sc = sb("sc", [P, E_NUM])
    sc1 = sb("sc1", [P, E_NUM])
    sc2 = sb("sc2", [P, E_NUM])
    esc = sb("esc", [P, E_NUM])
    gt = sb("gt", [P, E_NUM])

    late = oT[:, 0:H - HC, :].rearrange("p h t -> p (h t)").bitcast(F32)
    taken = [0]

    def view(shape):
        n = int(np.prod(shape))
        at = taken[0]
        taken[0] += n
        assert taken[0] <= (H - HC) * B * P // 2
        letters = "abcd"[:len(shape)]
        return late[:, at:at + n].rearrange(f"p ({' '.join(letters)}) -> p {' '.join(letters)}",
                                            **{l: m for l, m in zip(letters[1:], shape[1:])})

    h2 = view([2, HID])
    qx = view([2, HID])
    ex = view([3, XH, XK])
    pxT = view([2, XJ, HID])
    xo = view([HID])
    h3 = view([HID])
    h3T = view([C, P])
    zg = view([HID])
    fin = view([2, HID])

    bank = [ps(f"bank{i}", [P, HID]) for i in range(8)]
    b_query, b_mix, b_route, b_z = bank[0], bank[5], bank[6], bank[7]
    b_scores, b_turned = (bank[1], bank[2]), (bank[3], bank[4])

    small_in = sem("small_in")
    ctx_in = sem("ctx_in")
    x2_in = sem("x2_in")
    ffn_in = sem("ffn_in")
    ones_ok = sem("ones_ok")
    prepared_ps = sem("prepared_ps")
    cp_ok = sem("cp_ok")
    kvb_ok = sem("kvb_ok")
    kvx_ok = sem("kvx_ok")
    hms_ok = sem("hms_ok")
    kbd_ok = sem("kbd_ok")
    vbd_ok = sem("vbd_ok")
    vbT_ps = sem("vbT_ps")
    vbT_ok = sem("vbT_ok")
    wo_hi_ok = sem("wo_hi_ok")
    wo_ok = sem("wo_ok")
    of_ok = sem("of_ok")
    w_ps = sem("w_ps")
    x1_ok = sem("x1_ok")
    moments2 = sem("moments2")
    ve2_ok = sem("ve2_ok")
    ln2_ok = sem("ln2_ok")
    y2_ok = sem("y2_ok")
    newton2 = sem("newton2")
    rs2_ok = sem("rs2_ok")
    h2_ok = sem("h2_ok")
    qx_ps = sem("qx_ps")
    qx_ok = sem("qx_ok")
    xs_ps = sem("xs_ps")
    xmax_ok = sem("xmax_ok")
    xsub_ok = sem("xsub_ok")
    xexp_ok = sem("xexp_ok")
    xsum_ok = sem("xsum_ok")
    xrz_ok = sem("xrz_ok")
    xn_ok = sem("xn_ok")
    xt_ps = sem("xt_ps")
    xt_ok = sem("xt_ok")
    xv_ps = sem("xv_ps")
    xo_ok = sem("xo_ok")
    wm_ps = sem("wm_ps")
    x2_ok = sem("x2_ok")
    moments3 = sem("moments3")
    ve3_ok = sem("ve3_ok")
    ln3_ok = sem("ln3_ok")
    y3_ok = sem("y3_ok")
    newton3 = sem("newton3")
    h3_ok = sem("h3_ok")
    h3T_ps = sem("h3T_ps")
    h3T_ok = sem("h3T_ok")
    h3T_lo_ok = sem("h3T_lo_ok")
    ab_hi_ok = sem("ab_hi_ok")
    ab_lo_ok = sem("ab_lo_ok")
    router_ok = sem("router_ok")
    rs_ps = sem("rs_ps")
    sc_ok = sem("sc_ok")
    marks = sem("marks")
    nt_ok = sem("nt_ok")
    es_ok = sem("es_ok")
    gate_steps = sem("gate_steps")
    z_ps = sem("z_ps")
    zg_ok = sem("zg_ok")
    zT_ps = sem("zT_ps")
    zT_ok = sem("zT_ok")
    zT_lo_ok = sem("zT_lo_ok")
    f_ps = sem("f_ps")
    fin_ok = sem("fin_ok")

    stored = [sem("stored0"), sem("stored1")]
    wo_in = [sem("wo_in0"), sem("wo_in1")]

    wo_v = Wo.rearrange("(c h p) n -> c p h n", p=P, h=HC)

    def spread(ap, n):
        return ap.unsqueeze(2).broadcast_to([ap.shape[0], ap.shape[1], n])

    block = ctx.enter_context(nc.Block())

    @block.sync
    def _(sp):
        def weights(c, u):
            if some(c - 2):
                sp.wait_ge(wo_ok, HC * (c - 2))
            sp.dma_start(wo_raw[u][:, :, :], wo_v[c]).then_inc(wo_in[u], 16)

        weights(1, 1)
        sp.dma_start(xs[:, :, :], x.rearrange("b t d -> t b d")).then_inc(x2_in, 16)
        weights(2, 0)
        sp.dma_start(cs[:, :], small).then_inc(small_in, 16)
        sp.dma_start(proj_sb[:, :, :], proj.rearrange("(c p) k -> p c k", p=P)).then_inc(ctx_in, 16)
        for c in range(NT):
            sp.dma_start(ctx_sb[:, c, :, :], ctxT[:, c * P:(c + 1) * P, :].rearrange("b p d -> p b d")).then_inc(ctx_in, 16)
        weights(3, 1)
        sp.dma_start(wr[:, :], Wr).then_inc(ffn_in, 16)
        sp.dma_start(keys[:, :], keysT).then_inc(ffn_in, 16)
        with sp.Fori(2, NCH // 2) as p:
            weights(2 * p, 0)
            weights(2 * p + 1, 1)
        for u, low_rank in enumerate((AT, BT)):
            sp.wait_ge(wo_ok, HC * (NCH - 2 + u))
            sp.dma_start(wo_raw[u][:, :, :], low_rank.rearrange("(c p) n -> p c n", p=P)).then_inc(wo_in[u], 16)
        for b in range(B):
            sp.wait_ge(fin_ok, b + 1)
            sp.dma_start(out[b], fin[:, b % 2, :]).then_inc(stored[b % 2], 16)
        for done in stored:
            sp.wait_ge(done, 16 * B // 2)

    @block.tensor
    def _(pe):
        def chunk_product(c, u, b, first=False):
            pe.wait_ge(of_ok, 8 * c + b + 1)
            for h in range(HC):
                pe.matmul(bank[b][:, :], oF[:, b % 2, h, :], wo_hi[u][:, h, :], start=first and h == 0, stop=False,
                          skip_group_check=True)
                mm = pe.matmul(bank[b][:, :], oF[:, b % 2, h, :], wo_lo[u][:, h, :], start=False,
                               stop=(h == HC - 1), skip_group_check=True)
            mm.then_inc(w_ps, 1)

        def project_context():
            pe.wait_ge(ctx_in, 16 * (NT + 1))
            pe.wait_ge(x1_ok, 1)
            for b in range(B):
                for c in range(NT):
                    mm = pe.matmul(bank[0][:, b * 2 * XK:(b + 1) * 2 * XK], ctx_sb[:, c, b, :], proj_sb[:, c, :],
                                   start=(c == 0), stop=(c == NT - 1))
            mm.then_inc(prepared_ps, 1)
            pe.wait_ge(ones_ok, 1)
            pe.wait_ge(x1_ok, 2)
            for c in range(NT):
                mm = pe.matmul(bank[1][:, 0:2 * XK], ones[:, :], proj_sb[:, c, :], start=(c == 0), stop=(c == NT - 1))
            mm.then_inc(prepared_ps, 1)

        def keys_values():
            pe.wait_ge(small_in, 16)
            pe.wait_ge(cp_ok, 1)
            pe.wait_ge(x1_ok, 3)
            pe.matmul(bank[2][:, 0:B * XK], wkT, cp[:, 0, :, :].rearrange("p b k -> p (b k)"), start=True, stop=True)
            pe.matmul(bank[2][:, B * XK:2 * B * XK], wvT, cp[:, 1, :, :].rearrange("p b k -> p (b k)"),
                      start=True, stop=True).then_inc(prepared_ps, 1)

        def router_matrix():
            pe.wait_ge(ffn_in, 32)
            pe.wait_ge(x1_ok, 4)
            for c in range(C):
                mm = pe.matmul(bank[3][:, c * E_NUM:(c + 1) * E_NUM], wr[:, c * P:(c + 1) * P], keys[:, :],
                               start=True, stop=True)
            mm.then_inc(prepared_ps, 1)

        for b in range(B):
            chunk_product(0, 0, b, first=True)
        with pe.Fori(0, NCH // 2 - 1) as p:
            pe.wait_ge(wo_ok, HC * (2 * p + 1))
            for b in range(B):
                chunk_product(2 * p + 1, 1, b)
            pe.wait_ge(wo_ok, HC * (2 * p + 2))
            for b in range(B):
                chunk_product(2 * p + 2, 0, b)
        pe.wait_ge(wo_ok, HC * (NCH - 1))
        for b in range(B - 1):
            chunk_product(NCH - 1, 1, b)
            if b == 4:
                project_context()
            if b == 5:
                keys_values()
        router_matrix()

        def query(b):
            pe.wait_ge(h2_ok, b + 1)
            if b >= 2:
                pe.wait_ge(vbT_ok, b - 1)
            else:
                if b == 1:
                    pe.wait_ge(qx_ok, 1)
            pe.matmul(b_query[:, :], wqT, h2[:, b % 2, :], start=True, stop=True).then_inc(qx_ps, 1)

        def xscores(b, i):
            t = NT * b + i
            pe.wait_ge(qx_ok, b + 1)
            pe.wait_ge(kbd_ok, b + 1)
            if t < 2:
                pe.wait_ge(kvx_ok, 2)
            if some(t - 1):
                pe.wait_ge(xsub_ok, t - 1)
            pe.matmul(b_scores[t % 2][:, :], qx[:, b % 2, i * P:(i + 1) * P],
                      kbd[:, b % 2, :, :].rearrange("p h k -> p (h k)"), start=True, stop=True).then_inc(xs_ps, 1)

        def xtranspose(t):
            pe.wait_ge(xn_ok, t + 1)
            if t == 0:
                pe.wait_ge(x1_ok, B)
            if some(t - 1):
                pe.wait_ge(xt_ok, t - 1)
            for j in range(XJ):
                mm = pe.transpose(b_turned[t % 2][:, j * P:(j + 1) * P],
                                  ex[:, t % 3, :, :].rearrange("p h k -> p (h k)")[:, j * P:(j + 1) * P], ident)
            mm.then_inc(xt_ps, 1)

        def vtranspose(b):
            pe.wait_ge(vbd_ok, b + 1)
            pe.wait_ge(qx_ok, min(b + 2, B))
            for j in range(XJ):
                mm = pe.transpose(b_query[:, j * P:(j + 1) * P],
                                  vbd[:, :, :].rearrange("p h k -> p (h k)")[:, j * P:(j + 1) * P], ident)
            mm.then_inc(vbT_ps, 1)

        def xmix(b):
            pe.wait_ge(xt_ok, NT * b + NT)
            pe.wait_ge(vbT_ok, b + 1)
            if some(b):
                pe.wait_ge(x2_ok, b)
            for j in range(XJ):
                mm = pe.matmul(b_mix[:, :], vbT[:, b % 2, j, :], pxT[:, b % 2, j, :], start=(j == 0), stop=(j == XJ - 1))
            mm.then_inc(xv_ps, 1)

        def xout(b):
            pe.wait_ge(xo_ok, b + 1)
            pe.matmul(b_mix[:, :], wmT, xo[:, :], start=True, stop=True).then_inc(wm_ps, 1)

        def tokens(b):
            pe.wait_ge(h3_ok, b + 1)
            if some(b):
                pe.wait_ge(sc_ok, b)
            for c in range(C):
                mm = pe.transpose(b_route[:, c * P:(c + 1) * P], h3[:, c * P:(c + 1) * P], ident)
            mm.then_inc(h3T_ps, 1)

        def router_scores(b):
            if b == 0:
                pe.wait_ge(router_ok, 1)
            pe.wait_ge(h3T_ok, b + 1)
            for c in range(C):
                mm = pe.matmul(b_route[:, 0:E_NUM], h3T[:, c, :], router[:, c, :], start=(c == 0), stop=(c == C - 1))
            mm.then_inc(rs_ps, 1)

        def product(hi, lo, a):
            for c in range(C):
                pe.matmul(b_z[:, :], hi[:, c, :], wo_hi[a][:, c, :], start=(c == 0), stop=False)
                pe.matmul(b_z[:, :], hi[:, c, :], wo_lo[a][:, c, :], start=False, stop=False)
                mm = pe.matmul(b_z[:, :], lo[:, c, :], wo_hi[a][:, c, :], start=False, stop=(c == C - 1))
            return mm

        def down(b):
            if b == 0:
                pe.wait_ge(ab_lo_ok, C)
            if some(b):
                pe.wait_ge(fin_ok, b)
            pe.wait_ge(h3T_lo_ok, b + 1)
            product(h3T_hi, h3T_lo, 0).then_inc(z_ps, 1)

        def turn(b):
            pe.wait_ge(zg_ok, b + 1)
            for c in range(C):
                mm = pe.transpose(b_z[:, c * P:(c + 1) * P], zg[:, c * P:(c + 1) * P], ident)
            mm.then_inc(zT_ps, 1)

        def up(b):
            if b == 0:
                pe.wait_ge(ab_lo_ok, 2 * C)
            pe.wait_ge(zT_lo_ok, b + 1)
            product(zgT_hi, zgT_lo, 1).then_inc(f_ps, 1)

        query(0)
        chunk_product(NCH - 1, 1, B - 1)

        for s in range(B + 3):
            fa, fb = s - 2, s - 3
            attends, mixes, routes, leaves = s < B, 1 <= s <= B, 0 <= fa < B, 0 <= fb
            if attends:
                xscores(s, 0)
            if mixes:
                xtranspose(NT * s - 2)
            if s + 1 < B:
                query(s + 1)
            if leaves:
                turn(fb)
            if attends:
                xscores(s, 1)
            if mixes:
                xtranspose(NT * s - 1)
            if attends:
                vtranspose(s)
            if leaves:
                up(fb)
            if routes:
                tokens(fa)
            if attends:
                xscores(s, 2)
            if mixes:
                xmix(s - 1)
            if routes:
                router_scores(fa)
            if attends:
                xtranspose(NT * s)
                xscores(s, 3)
            if routes:
                down(fa)
            if mixes:
                xout(s - 1)
            if attends:
                xtranspose(NT * s + 1)

    @block.scalar
    def _(act):
        act.preload_act_table_set("natural_log_exp_and_others")

        def split(c, u, count):
            act.wait_ge(wo_in[u], count)
            if some(8 * (c - 1)):
                act.wait_ge(w_ps, 8 * (c - 1))
            act.activation(wo_hi[u][:, :, :], wo_raw[u][:, :, :], ACT.Copy).then_inc(wo_hi_ok, 1)

        def split_low_rank(u):
            act.wait_ge(wo_in[u], 16 * (NCH // 2 + u))
            act.wait_ge(w_ps, 8 * (NCH - 1 + u))
            act.activation(wo_hi[u][:, :, :], wo_raw[u][:, :, :], ACT.Copy).then_inc(ab_hi_ok, 1)

        def rsqrt2(g):
            of = slice(g * HALF, (g + 1) * HALF)
            act.wait_ge(ve2_ok, g + 1)
            act.activation(ln2[:, of], ve2[:, of], ACT.Ln).then_inc(ln2_ok, 1)
            act.wait_ge(ln2_ok, g + 1)
            act.activation(y2[:, of], ln2[:, of], ACT.Exp, scale=-0.5).then_inc(y2_ok, 1)

        def rsqrt3(b):
            act.wait_ge(ve3_ok, b + 1)
            act.activation(ln3[:, :], ve3[:, :], ACT.Ln).then_inc(ln3_ok, 1)
            act.wait_ge(ln3_ok, b + 1)
            act.activation(y3[:, :], ln3[:, :], ACT.Exp, scale=-0.5).then_inc(y3_ok, 1)

        def copy_query(b):
            act.wait_ge(qx_ps, b + 1)
            if some(NT * (b - 1)):
                act.wait_ge(xs_ps, NT * (b - 1))
            act.activation(qx[:, b % 2, :], b_query[:, :], ACT.Identity, bias=bq).then_inc(qx_ok, 1)

        def xexp(t):
            act.wait_ge(xsub_ok, t + 1)
            act.activation(ex[:, t % 3, :, :], ex[:, t % 3, :, :], ACT.Exp).then_inc(xexp_ok, 1)

        def copy_xt(b, i):
            t = NT * b + i
            act.wait_ge(xt_ps, t + 1)
            if some(b - 1):
                act.wait_ge(xv_ps, b - 1)
            act.activation(pxT[:, b % 2, :, i * P:(i + 1) * P], b_turned[t % 2][:, :].rearrange("p (j n) -> p j n", j=XJ),
                           ACT.Copy).then_inc(xt_ok, 1)

        def copy_vT(b):
            act.wait_ge(vbT_ps, b + 1)
            if some(b - 1):
                act.wait_ge(xv_ps, b - 1)
            act.activation(vbT[:, b % 2, :, :], b_query[:, :].rearrange("p (j c) -> p j c", j=XJ),
                           ACT.Copy).then_inc(vbT_ok, 1)

        def copy_mix(b):
            act.wait_ge(xv_ps, b + 1)
            if some(b):
                act.wait_ge(wm_ps, b)
            act.activation(xo[:, :], b_mix[:, :], ACT.Copy).then_inc(xo_ok, 1)

        def copy_h3T(b):
            act.wait_ge(h3T_ps, b + 1)
            if some(b):
                act.wait_ge(z_ps, b)
                act.wait_ge(h3T_lo_ok, b)
            turned = b_route[:, :].rearrange("p (c t) -> p c t", c=C)
            act.activation(h3T_hi[:, :, :], turned, ACT.Copy)
            act.activation(h3T[:, :, :], turned, ACT.Copy).then_inc(h3T_ok, 1)

        def copy_router_scores(b):
            act.wait_ge(rs_ps, b + 1)
            if some(b):
                act.wait_ge(marks, 5 * b - 3)
            act.activation(sc[:, :], b_route[:, 0:E_NUM], ACT.Copy).then_inc(sc_ok, 1)

        def exp_router(b):
            act.wait_ge(nt_ok, b + 1)
            if some(b):
                act.wait_ge(gate_steps, 4 * b - 3)
            act.activation(esc[:, :], sc[:, :], ACT.Exp, bias=ntop[:, 0:1]).then_inc(es_ok, 1)

        def copy_zT(b):
            act.wait_ge(zT_ps, b + 1)
            if some(b):
                act.wait_ge(f_ps, b)
            act.activation(zgT_hi[:, :, :], b_z[:, :].rearrange("p (c t) -> p c t", c=C), ACT.Copy).then_inc(zT_ok, 1)

        split(1, 1, 16)
        split(2, 0, 16)
        with act.Fori(1, NCH // 2 - 1) as p:
            split(2 * p + 1, 1, 16 * p + 16)
            split(2 * p + 2, 0, 16 * p + 16)
        split(NCH - 1, 1, 16 * (NCH // 2))
        split_low_rank(0)
        act.wait_ge(prepared_ps, 1)
        act.activation(cp[:, :, :, :], bank[0][:, :].rearrange("p (b a k) -> p a b k", b=B, a=2), ACT.Copy).then_inc(cp_ok, 1)
        rsqrt2(0)
        act.wait_ge(prepared_ps, 4)
        act.activation(router[:, :, :], bank[3][:, 0:C * E_NUM].rearrange("p (c e) -> p c e", c=C),
                       ACT.Copy).then_inc(router_ok, 1)
        copy_query(0)
        for s in range(B + 3):
            fa, fb = s - 2, s - 3
            attends, mixes, routes, leaves = s < B, 1 <= s <= B, 0 <= fa < B, 0 <= fb
            if s + 1 < B:
                copy_query(s + 1)
            if leaves:
                copy_zT(fb)
            if routes:
                rsqrt3(fa)
            if mixes:
                copy_xt(s - 1, 2)
            if attends:
                xexp(NT * s)
            if mixes:
                copy_xt(s - 1, 3)
            if s == 0:
                rsqrt2(1)
            if attends:
                copy_vT(s)
                xexp(NT * s + 1)
            if routes:
                copy_h3T(fa)
            if attends:
                xexp(NT * s + 2)
            if mixes:
                copy_mix(s - 1)
            if routes:
                copy_router_scores(fa)
            if attends:
                copy_xt(s, 0)
            if routes:
                exp_router(fa)
            if attends:
                xexp(NT * s + 3)
            if attends:
                copy_xt(s, 1)
            if s == 0:
                split_low_rank(1)

    @block.vector
    def _(dve):
        def split(c, u, h):
            dve.wait_ge(wo_hi_ok, c)
            dve.tensor_tensor(wo_lo[u][:, h, :], wo_raw[u][:, h, :], wo_hi[u][:, h, :].bitcast(F32),
                              ALU.subtract).then_inc(wo_ok, 1)

        def widen(c, b):
            n = 8 * c + b
            if some(n - 1):
                dve.wait_ge(w_ps, n - 1)
            dve.tensor_scalar(oF[:, b % 2, :, :], oT[:, bass.ds(HC * c, HC), b * P:(b + 1) * P], 1.0, None,
                              ALU.mult).then_inc(of_ok, 1)

        def first_residual(b):
            dve.wait_ge(w_ps, 8 * (NCH - 1) + b + 1)
            dve.tensor_tensor(xs[:, b, :], bank[b][:, :], xs[:, b, :], ALU.add).then_inc(x1_ok, 1)
            dve.wait_ge(x1_ok, b + 1)
            dve.bn_stats(st2[:, b, :], xs[:, b, :]).then_inc(moments2, 1)
            dve.wait_ge(moments2, 2 * b + 1)
            dve.bn_aggr(mv2[:, b, :], st2[:, b, :]).then_inc(moments2, 1)

        def variance(g):
            of = slice(g * HALF, (g + 1) * HALF)
            dve.wait_ge(moments2, 2 * (HALF * g + HALF))
            dve.tensor_scalar(ve2[:, of], mv2[:, of, 1], EPS, None, ALU.add).then_inc(ve2_ok, 1)

        def newton(g):
            of = slice(g * HALF, (g + 1) * HALF)
            dve.wait_ge(y2_ok, g + 1)
            dve.tensor_tensor(nt2[:, of], y2[:, of], y2[:, of], ALU.mult).then_inc(newton2, 1)
            dve.wait_ge(newton2, 3 * g + 1)
            dve.tensor_tensor(nt2[:, of], nt2[:, of], ve2[:, of], ALU.mult).then_inc(newton2, 1)
            dve.wait_ge(newton2, 3 * g + 2)
            dve.tensor_scalar(nt2[:, of], nt2[:, of], -0.5, 1.5, ALU.mult, ALU.add).then_inc(newton2, 1)
            dve.wait_ge(newton2, 3 * g + 3)
            dve.tensor_tensor(rs2[:, of], y2[:, of], nt2[:, of], ALU.mult).then_inc(rs2_ok, 1)

        def normalise2(b):
            dve.wait_ge(rs2_ok, b // HALF + 1)
            if some(b - 1):
                dve.wait_ge(qx_ps, b - 1)
            dve.tensor_scalar(h2[:, b % 2, :], xs[:, b, :], mv2[:, b, 0:1], rs2[:, b:b + 1], ALU.subtract,
                              ALU.mult).then_inc(h2_ok, 1)

        def context_bias():
            dve.wait_ge(prepared_ps, 2)
            dve.tensor_scalar(kvb[:, 0, :], bank[1][:, 0:XK], bk, None, ALU.mult).then_inc(kvb_ok, 1)
            dve.tensor_scalar(kvb[:, 1, :], bank[1][:, XK:2 * XK], bv, None, ALU.mult).then_inc(kvb_ok, 1)

        def context_keys():
            dve.wait_ge(kvb_ok, 2)
            dve.wait_ge(prepared_ps, 3)
            for a in range(2):
                dve.tensor_tensor(kvx[:, a, :, :],
                                  bank[2][:, a * B * XK:(a + 1) * B * XK].rearrange("p (b k) -> p b k", b=B),
                                  kvb[:, a, :].unsqueeze(1).broadcast_to([P, B, XK]), ALU.add).then_inc(kvx_ok, 1)

        for b in range(B):
            widen(0, b)
            if b == 1:
                dve.memset(ones[:, :], 1.0).then_inc(ones_ok, 1)
            if b >= HC:
                split(1, 1, b - HC)
        with dve.Fori(0, NCH // 2 - 1) as p:
            for b in range(B):
                widen(2 * p + 1, b)
                if b >= HC:
                    split(2 * p + 2, 0, b - HC)
            for b in range(B):
                widen(2 * p + 2, b)
                if b >= HC:
                    split(2 * p + 3, 1, b - HC)
        dve.wait_ge(small_in, 16)
        dve.tensor_scalar(hms[:, :], hmask, float(XD) ** -0.5, None, ALU.mult).then_inc(hms_ok, 1)
        dve.wait_ge(x2_in, 16)
        for b in range(B + 2):
            if b < B:
                widen(NCH - 1, b)
            if b >= 2:
                first_residual(b - 2)
            if b == HALF + 1:
                variance(0)
            if b == HALF + 2:
                newton(0)
                normalise2(0)
                context_bias()
            if b == B - 1:
                context_keys()
            if b == B:
                normalise2(1)
        variance(1)

        def xmax(t):
            dve.wait_ge(xs_ps, t + 1)
            dve.tensor_reduce(xmx[:, t % 2, :], b_scores[t % 2][:, :].rearrange("p (h k) -> p h k", h=XH), AX.X,
                              ALU.max).then_inc(xmax_ok, 1)
            dve.wait_ge(xmax_ok, t + 1)
            if some(t - 2):
                dve.wait_ge(xt_ps, t - 2)
            dve.tensor_tensor(ex[:, t % 3, :, :], b_scores[t % 2][:, :].rearrange("p (h k) -> p h k", h=XH),
                              spread(xmx[:, t % 2, :], XK), ALU.subtract).then_inc(xsub_ok, 1)

        def xsum(t):
            dve.wait_ge(xexp_ok, t + 1)
            dve.tensor_reduce(xsm[:, t % 2, :], ex[:, t % 3, :, :], AX.X, ALU.add).then_inc(xsum_ok, 1)
            dve.wait_ge(xsum_ok, t + 1)
            if some(t - 1):
                dve.wait_ge(xn_ok, t - 1)
            dve.reciprocal(xrz[:, t % 2, :], xsm[:, t % 2, :]).then_inc(xrz_ok, 1)

        def second_residual(b):
            dve.wait_ge(wm_ps, b + 1)
            dve.scalar_tensor_tensor(out=xs[:, b, :], in0=b_mix[:, :], scalar=bm, in1=xs[:, b, :], op0=ALU.add,
                                     op1=ALU.add).then_inc(x2_ok, 1)

        def stats3(b):
            dve.wait_ge(x2_ok, b + 1)
            dve.bn_stats(st3[:, :], xs[:, b, :]).then_inc(moments3, 1)
            dve.wait_ge(moments3, 2 * b + 1)
            dve.bn_aggr(mv3[:, :], st3[:, :]).then_inc(moments3, 1)
            dve.wait_ge(moments3, 2 * b + 2)
            dve.tensor_scalar(ve3[:, :], mv3[:, 1:2], EPS, None, ALU.add).then_inc(ve3_ok, 1)

        def normalise3(b):
            dve.wait_ge(y3_ok, b + 1)
            dve.scalar_tensor_tensor(out=nta3[:, :], in0=y3[:, :], scalar=ve3[:, 0:1], in1=y3[:, :], op0=ALU.mult,
                                     op1=ALU.mult).then_inc(newton3, 1)
            dve.wait_ge(newton3, 3 * b + 1)
            dve.tensor_scalar(ntb3[:, :], nta3[:, :], -0.5, 1.5, ALU.mult, ALU.add).then_inc(newton3, 1)
            dve.wait_ge(newton3, 3 * b + 2)
            dve.tensor_tensor(rs3[:, :], y3[:, :], ntb3[:, :], ALU.mult).then_inc(newton3, 1)
            dve.wait_ge(newton3, 3 * b + 3)
            if some(b):
                dve.wait_ge(h3T_ps, b)
            dve.tensor_scalar(h3[:, :], xs[:, b, :], mv3[:, 0:1], rs3[:, 0:1], ALU.subtract, ALU.mult).then_inc(h3_ok, 1)

        def choose_mark(b):
            dve.wait_ge(sc_ok, b + 1)
            dve.max(top[:, :], sc[:, :]).then_inc(marks, 1)
            dve.wait_ge(marks, 5 * b + 1)
            dve.match_replace(out=sc1[:, :], in_to_replace=top[:, :], in_values=sc[:, :], imm_value=-3e38).then_inc(marks, 1)
            dve.tensor_scalar(ntop[:, :], top[:, 0:1], -1.0, None, ALU.mult).then_inc(nt_ok, 1)
            dve.wait_ge(marks, 5 * b + 2)
            dve.max(top2[:, :], sc1[:, :]).then_inc(marks, 1)
            dve.wait_ge(marks, 5 * b + 3)
            dve.match_replace(out=sc2[:, :], in_to_replace=top2[:, :], in_values=sc1[:, :],
                              imm_value=-3e38).then_inc(marks, 1)
            dve.wait_ge(marks, 5 * b + 4)
            dve.tensor_scalar(sc2[:, :], sc2[:, :], -2e38, None, ALU.is_lt).then_inc(marks, 1)

        def choose_gate(b):
            dve.wait_ge(marks, 5 * b + 5)
            dve.wait_ge(es_ok, b + 1)
            dve.tensor_tensor(gt[:, :], esc[:, :], sc2[:, :], ALU.mult).then_inc(gate_steps, 1)
            dve.wait_ge(gate_steps, 4 * b + 1)
            dve.tensor_reduce(gsum[:, :], gt[:, :], AX.X, ALU.add).then_inc(gate_steps, 1)
            dve.wait_ge(gate_steps, 4 * b + 2)
            dve.reciprocal(grz[:, :], gsum[:, :]).then_inc(gate_steps, 1)
            dve.wait_ge(gate_steps, 4 * b + 3)
            dve.tensor_scalar(gt[:, :], gt[:, :], grz[:, 0:1], SCALING, ALU.mult, ALU.mult).then_inc(gate_steps, 1)

        def gated(b):
            dve.wait_ge(z_ps, b + 1)
            dve.wait_ge(gate_steps, 4 * b + 4)
            if some(b):
                dve.wait_ge(zT_ps, b)
            dve.tensor_tensor(zg[:, :].rearrange("p (e r) -> p e r", r=RANK),
                              b_z[:, :].rearrange("p (e r) -> p e r", r=RANK),
                              spread(gt[:, :], RANK), ALU.mult).then_inc(zg_ok, 1)

        def lo_h3T(b):
            dve.wait_ge(h3T_ok, b + 1)
            if some(b):
                dve.wait_ge(z_ps, b)
            dve.tensor_tensor(h3T_lo[:, :, :], h3T[:, :, :], h3T_hi[:, :, :].bitcast(F32),
                              ALU.subtract).then_inc(h3T_lo_ok, 1)

        def lo_zT(b):
            dve.wait_ge(zT_ok, b + 1)
            if some(b):
                dve.wait_ge(f_ps, b)
            dve.tensor_tensor(zgT_lo[:, :, :], b_z[:, :].rearrange("p (c t) -> p c t", c=C),
                              zgT_hi[:, :, :].bitcast(F32), ALU.subtract).then_inc(zT_lo_ok, 1)

        def finish(b):
            dve.wait_ge(f_ps, b + 1)
            if some(16 * (b // 2)):
                dve.wait_ge(stored[b % 2], 16 * (b // 2))
            dve.tensor_tensor(fin[:, b % 2, :], b_z[:, :], xs[:, b, :], ALU.add).then_inc(fin_ok, 1)

        for s in range(B + 3):
            fa, fb = s - 2, s - 3
            attends, mixes, routes, leaves = s < B, 1 <= s <= B, 0 <= fa < B, 0 <= fb
            if leaves:
                lo_zT(fb)
            if attends:
                xmax(NT * s)
            if routes:
                normalise3(fa)
            if attends:
                xmax(NT * s + 1)
                xsum(NT * s)
            if s == 0:
                newton(1)
            if attends and not leaves:
                xmax(NT * s + 2)
            if attends:
                xsum(NT * s + 1)
            if leaves:
                finish(fb)
            if routes:
                lo_h3T(fa)
            if attends and leaves:
                xmax(NT * s + 2)
            if attends and not leaves:
                xmax(NT * s + 3)
            if attends:
                xsum(NT * s + 2)
            if routes:
                choose_mark(fa)
            if attends and leaves:
                xmax(NT * s + 3)
            if routes:
                choose_gate(fa)
            if attends:
                xsum(NT * s + 3)
            if s + 2 < B:
                normalise2(s + 2)
            if routes:
                gated(fa)
            if mixes:
                second_residual(s - 1)
                stats3(s - 1)

    @block.gpsimd
    def _(pool):
        def own_keys(b):
            if some(NT * (b - 1)):
                pool.wait_ge(xs_ps, NT * (b - 1))
            pool.tensor_tensor(kbd[:, b % 2, :, :], kvx[:, 0, b, :].unsqueeze(1).broadcast_to([P, XH, XK]),
                               spread(hms[:, :], XK), ALU.mult).then_inc(kbd_ok, 1)

        def own_values(b):
            if some(b):
                pool.wait_ge(vbT_ps, b)
            pool.tensor_tensor(vbd[:, :, :], kvx[:, 1, b, :].unsqueeze(1).broadcast_to([P, XH, XK]),
                               spread(hmask, XK), ALU.mult).then_inc(vbd_ok, 1)

        def split_low_rank(u, c):
            pool.wait_ge(ab_hi_ok, u + 1)
            pool.tensor_tensor(wo_lo[u][:, c, :], wo_raw[u][:, c, :], wo_hi[u][:, c, :].bitcast(F32),
                               ALU.subtract).then_inc(ab_lo_ok, 1)

        for c in range(C):
            split_low_rank(0, c)
        pool.wait_ge(hms_ok, 1)
        pool.wait_ge(kvx_ok, 2)
        own_keys(0)
        for s in range(B):
            for i in range(NT):
                t = NT * s + i
                if i == 0:
                    own_values(s)
                pool.wait_ge(xrz_ok, t + 1)
                pool.tensor_tensor(ex[:, t % 3, :, :], ex[:, t % 3, :, :], spread(xrz[:, t % 2, :], XK),
                                   ALU.mult).then_inc(xn_ok, 1)
                if i == 0 and s + 1 < B:
                    own_keys(s + 1)
                if s == 1:
                    split_low_rank(1, i)


def build(nc, x, consts, small, ctxT, proj, keysT, Wr, Wq, Wk, Wv, Wo, AT, BT, out):
    with ExitStack() as outer:
        oT = outer.enter_context(nc.sbuf_tensor("oT", [P, H, B * P], BF16))
        xall = oT[:, 0:B, :].rearrange("p h t -> p (h t)").bitcast(F32).rearrange("p (b n) -> p b n", b=B)
        w_raw = outer.enter_context(nc.sbuf_tensor("w_raw", [P, C, GRP * D], F32))
        w_hi = outer.enter_context(nc.sbuf_tensor("w_hi", [P, C, GRP * D], F32R))
        w_lo = outer.enter_context(nc.sbuf_tensor("w_lo", [P, C, GRP * D], F32R))
        with ExitStack() as ctx:
            attention(nc, x, consts, Wq, Wk, Wv, Wo, oT, xall, w_raw, w_hi, w_lo, outer, ctx)
        with ExitStack() as ctx:
            rest(nc, x, small, ctxT, proj, keysT, Wr, Wo, AT, BT, out, oT, w_raw, w_hi, w_lo, outer, ctx)


def kernel(**inputs):
    import numpy as _np
    import concourse.bacc as _bacc
    from concourse import mybir as _mybir
    from concourse.bass_utils import run_bass_kernel_spmd as _run

    nc = _bacc.Bacc("TRN2", target_bir_lowering=False, num_devices=1)
    g = {n: _np.asarray(a) for n, a in inputs.items()}
    X = "L0_xattn_"
    column = lambda n: g[X + n].reshape(P, 1)
    ins = {
        "x": g["x"],
        "consts": constants(),
        "small": _np.concatenate([_np.eye(P, dtype=_np.float32), head_mask(), g[X + "Wq"].T, g[X + "Wk"].T, g[X + "Wv"].T,
                                  g[X + "Wm"].T, column("bq"), column("bk"), column("bv"), column("bm")], axis=1),
        "ctxT": g["ctx_4096"].transpose(0, 2, 1),
        "proj": _np.concatenate([g[X + "proj_k"], g[X + "proj_v"]], axis=1),
        "keysT": g["L0_ffn_keys"].T,
        "Wr": g["L0_ffn_Wq_w"],
        "Wq": g["L0_attn_Wq"], "Wk": g["L0_attn_Wk"], "Wv": g["L0_attn_Wv"], "Wo": g["L0_attn_Wo"],
        "AT": g["L0_ffn_A_w"].T, "BT": g["L0_ffn_B_w"].T,
    }
    arrays, args = {}, []
    for name, a in ins.items():
        a = _np.ascontiguousarray(a)
        arrays[f"in_{name}"] = a
        args.append(nc.dram_tensor(f"in_{name}", a.shape, _mybir.dt.from_np(a.dtype), kind="ExternalInput").ap())
    args.append(nc.dram_tensor("out_x", (B, P, HID), _mybir.dt.float32, kind="ExternalOutput").ap())
    build(nc, *args)
    r = _run(nc, [arrays], core_ids=[0])
    return r.results[0]["out_x"]
```
